# Optimizing a Trainium2 kernel written in Bass

```python
import numpy as np
import jax
import jax.numpy as jnp

def _softmax(x, axis=-1):
    return jax.nn.softmax(x, axis=axis)

def _gelu(x):
    return jax.nn.gelu(x, approximate=True)

def _silu(x):
    return jax.nn.silu(x)

def _sigmoid(x):
    return jax.nn.sigmoid(x)

def _layernorm(x, axis=-1, eps=1e-05):
    m = jnp.mean(x, axis=axis, keepdims=True)
    v = jnp.var(x, axis=axis, keepdims=True)
    return (x - m) / jnp.sqrt(v + eps)

def _scatter_add(tgt, idx, src, axis=0):
    return tgt.at[idx].add(src)

def _segment_sum(src, seg, n):
    return jax.ops.segment_sum(src, seg, n)
kernel_name = 'mk_gnn_preln_d2_gnn_r8_dc8ca7'

def setup_inputs(seed: int=0):
    np.random.seed(seed)
    _w = jnp.asarray

    def _rec_inputs():
        import jax
        import jax.numpy as jnp
        _gk = jax.random.key(seed)
        x = -0.0001126 + 1 * jax.random.normal(jax.random.fold_in(_gk, 1), (1250, 768), jnp.float32)
        src = jax.random.randint(jax.random.fold_in(_gk, 2), (20000,), 0, 1250, jnp.int32)
        dst = jnp.minimum((1250 * jax.random.uniform(jax.random.fold_in(_gk, 3), (20000,)) ** 2.0).astype(jnp.int32), 9999)
        _o = jnp.argsort(dst, stable=True)
        src = src[_o]
        dst = dst[_o]
        edge_type_34 = jax.random.randint(jax.random.fold_in(_gk, 12), (20000,), 0, 34, jnp.int32)
        return (x, src, dst, edge_type_34)
    x, src, dst, edge_type_34 = _rec_inputs()

    def _L0_gnn_setup():
        import jax, jax.numpy as jnp
        import numpy as np
        N_NODES = 1250
        NEG_SLOPE = 0.2
        EPS = 1e-16

        def gat_layer(x, W, att_src, att_dst, bias, src, dst, heads, out_ch, concat):
            n = x.shape[0]
            h = (x @ W.T).reshape(n, heads, out_ch)
            a_src = jnp.einsum('nhc,hc->nh', h, att_src)
            a_dst = jnp.einsum('nhc,hc->nh', h, att_dst)
            e = a_src[src] + a_dst[dst]
            e = jax.nn.leaky_relu(e, NEG_SLOPE)
            m = jax.ops.segment_max(e, dst, num_segments=n)
            ex = jnp.exp(e - m[dst])
            denom = jax.ops.segment_sum(ex, dst, num_segments=n)
            alpha = ex / (denom[dst] + EPS)
            msg = alpha[:, :, None] * h[src]
            out = jax.ops.segment_sum(msg, dst, num_segments=n)
            if concat:
                out = out.reshape(n, heads * out_ch)
            else:
                out = out.mean(axis=1)
            return out + bias
        key = jax.random.key(seed)
        ks = jax.random.split(key, 12)
        x = jax.random.normal(ks[0], (N_NODES, 768), dtype=jnp.float32)
        edge_index = jax.random.randint(ks[1], (2, 20000), 0, N_NODES, dtype=jnp.int64)
        s1 = 1.0 / np.sqrt(768.0)
        W1 = jax.random.normal(ks[2], (8 * 128, 768), dtype=jnp.float32) * s1
        att_src1 = jax.random.normal(ks[3], (8, 128), dtype=jnp.float32) * (1.0 / np.sqrt(128.0))
        att_dst1 = jax.random.normal(ks[4], (8, 128), dtype=jnp.float32) * (1.0 / np.sqrt(128.0))
        b1 = jnp.zeros((8 * 128,), dtype=jnp.float32)
        s2 = 1.0 / np.sqrt(1024.0)
        W2 = jax.random.normal(ks[5], (1 * 768, 1024), dtype=jnp.float32) * s2
        att_src2 = jax.random.normal(ks[6], (1, 768), dtype=jnp.float32) * (1.0 / np.sqrt(768.0))
        att_dst2 = jax.random.normal(ks[7], (1, 768), dtype=jnp.float32) * (1.0 / np.sqrt(768.0))
        b2 = jnp.zeros((768,), dtype=jnp.float32)
        return {'x': x, 'edge_index': edge_index, 'W1': W1, 'att_src1': att_src1, 'att_dst1': att_dst1, 'b1': b1, 'W2': W2, 'att_src2': att_src2, 'att_dst2': att_dst2, 'b2': b2}
    _L0_gnn_all = _L0_gnn_setup()
    _L0_gnn_in = {k: v for k, v in _L0_gnn_all.items() if k in ('W1', 'att_src1', 'att_dst1', 'b1', 'W2', 'att_src2', 'att_dst2', 'b2')}
    del _L0_gnn_all

    def _L1_gnn_setup():
        import jax, jax.numpy as jnp
        import numpy as np
        N_NODES = 1250
        N_EDGES = 12500
        N_REL = 34
        DIM = 768

        def _graph_encoder(x, edge_index, edge_type, W_rel, W_root, b_rgcn, W_gcn, b_gcn):
            n = x.shape[0]
            src, dst = (edge_index[0], edge_index[1])
            ones = jnp.ones((src.shape[0],), dtype=x.dtype)
            seg = edge_type * n + dst
            agg = jax.ops.segment_sum(x[src], seg, num_segments=N_REL * n)
            cnt = jax.ops.segment_sum(ones, seg, num_segments=N_REL * n)
            mean = agg.reshape(N_REL, n, -1) / jnp.maximum(cnt, 1.0).reshape(N_REL, n, 1)
            h1 = jnp.einsum('rni,rio->no', mean, W_rel) + x @ W_root + b_rgcn
            xw = h1 @ W_gcn
            deg = jax.ops.segment_sum(ones, dst, num_segments=n) + 1.0
            dinv = jax.lax.rsqrt(deg)
            norm = dinv[src] * dinv[dst]
            out = jax.ops.segment_sum(xw[src] * norm[:, None], dst, num_segments=n)
            out = out + xw * (dinv * dinv)[:, None]
            return out + b_gcn
        key = jax.random.key(seed)
        ks = jax.random.split(key, 6)
        scale = 1.0 / np.sqrt(DIM)
        x = jax.random.normal(ks[0], (N_NODES, DIM), dtype=jnp.float32)
        edge_index = jax.random.randint(ks[1], (2, N_EDGES), 0, N_NODES, dtype=jnp.int32)
        edge_type = jax.random.randint(ks[2], (N_EDGES,), 0, N_REL, dtype=jnp.int32)
        W_rel = jax.random.normal(ks[3], (N_REL, DIM, DIM), dtype=jnp.float32) * scale
        W_root = jax.random.normal(ks[4], (DIM, DIM), dtype=jnp.float32) * scale
        b_rgcn = jnp.zeros((DIM,), dtype=jnp.float32)
        W_gcn = jax.random.normal(ks[5], (DIM, DIM), dtype=jnp.float32) * scale
        b_gcn = jnp.zeros((DIM,), dtype=jnp.float32)
        return {'x': x, 'edge_index': edge_index, 'edge_type': edge_type, 'W_rel': W_rel, 'W_root': W_root, 'b_rgcn': b_rgcn, 'W_gcn': W_gcn, 'b_gcn': b_gcn}
    _L1_gnn_all = _L1_gnn_setup()
    _L1_gnn_in = {k: v for k, v in _L1_gnn_all.items() if k in ('W_rel', 'W_root', 'b_rgcn', 'W_gcn', 'b_gcn')}
    del _L1_gnn_all
    return {'x': x, 'src': src, 'dst': dst, 'edge_type_34': edge_type_34, 'L0_gnn_W1': _L0_gnn_in['W1'], 'L0_gnn_att_src1': _L0_gnn_in['att_src1'], 'L0_gnn_att_dst1': _L0_gnn_in['att_dst1'], 'L0_gnn_b1': _L0_gnn_in['b1'], 'L0_gnn_W2': _L0_gnn_in['W2'], 'L0_gnn_att_src2': _L0_gnn_in['att_src2'], 'L0_gnn_att_dst2': _L0_gnn_in['att_dst2'], 'L0_gnn_b2': _L0_gnn_in['b2'], 'L1_gnn_W_rel': _L1_gnn_in['W_rel'], 'L1_gnn_W_root': _L1_gnn_in['W_root'], 'L1_gnn_b_rgcn': _L1_gnn_in['b_rgcn'], 'L1_gnn_W_gcn': _L1_gnn_in['W_gcn'], 'L1_gnn_b_gcn': _L1_gnn_in['b_gcn']}

def reference(x, src, dst, edge_type_34, L0_gnn_W1, L0_gnn_att_src1, L0_gnn_att_dst1, L0_gnn_b1, L0_gnn_W2, L0_gnn_att_src2, L0_gnn_att_dst2, L0_gnn_b2, L1_gnn_W_rel, L1_gnn_W_root, L1_gnn_b_rgcn, L1_gnn_W_gcn, L1_gnn_b_gcn):
    import jax
    import jax.numpy as jnp

    def _L0_gnn_ref(x, edge_index, W1, att_src1, att_dst1, b1, W2, att_src2, att_dst2, b2):
        import jax, jax.numpy as jnp
        import numpy as np
        N_NODES = 1250
        NEG_SLOPE = 0.2
        EPS = 1e-16

        def gat_layer(x, W, att_src, att_dst, bias, src, dst, heads, out_ch, concat):
            n = x.shape[0]
            h = (x @ W.T).reshape(n, heads, out_ch)
            a_src = jnp.einsum('nhc,hc->nh', h, att_src)
            a_dst = jnp.einsum('nhc,hc->nh', h, att_dst)
            e = a_src[src] + a_dst[dst]
            e = jax.nn.leaky_relu(e, NEG_SLOPE)
            m = jax.ops.segment_max(e, dst, num_segments=n)
            ex = jnp.exp(e - m[dst])
            denom = jax.ops.segment_sum(ex, dst, num_segments=n)
            alpha = ex / (denom[dst] + EPS)
            msg = alpha[:, :, None] * h[src]
            out = jax.ops.segment_sum(msg, dst, num_segments=n)
            if concat:
                out = out.reshape(n, heads * out_ch)
            else:
                out = out.mean(axis=1)
            return out + bias
        src, dst = (edge_index[0], edge_index[1])
        h = gat_layer(x, W1, att_src1, att_dst1, b1, src, dst, heads=8, out_ch=128, concat=True)
        h = jax.nn.relu(h)
        out = gat_layer(h, W2, att_src2, att_dst2, b2, src, dst, heads=1, out_ch=768, concat=True)
        return out

    def _L1_gnn_ref(x, edge_index, edge_type, W_rel, W_root, b_rgcn, W_gcn, b_gcn):
        import jax, jax.numpy as jnp
        import numpy as np
        N_NODES = 1250
        N_EDGES = 12500
        N_REL = 34
        DIM = 768

        def _graph_encoder(x, edge_index, edge_type, W_rel, W_root, b_rgcn, W_gcn, b_gcn):
            n = x.shape[0]
            src, dst = (edge_index[0], edge_index[1])
            ones = jnp.ones((src.shape[0],), dtype=x.dtype)
            seg = edge_type * n + dst
            agg = jax.ops.segment_sum(x[src], seg, num_segments=N_REL * n)
            cnt = jax.ops.segment_sum(ones, seg, num_segments=N_REL * n)
            mean = agg.reshape(N_REL, n, -1) / jnp.maximum(cnt, 1.0).reshape(N_REL, n, 1)
            h1 = jnp.einsum('rni,rio->no', mean, W_rel) + x @ W_root + b_rgcn
            xw = h1 @ W_gcn
            deg = jax.ops.segment_sum(ones, dst, num_segments=n) + 1.0
            dinv = jax.lax.rsqrt(deg)
            norm = dinv[src] * dinv[dst]
            out = jax.ops.segment_sum(xw[src] * norm[:, None], dst, num_segments=n)
            out = out + xw * (dinv * dinv)[:, None]
            return out + b_gcn
        return _graph_encoder(x, edge_index, edge_type, W_rel, W_root, b_rgcn, W_gcn, b_gcn)
    edge_index = jnp.stack([src, dst])
    h = jnp.maximum(_layernorm(x, axis=-1), 0.0)
    x = x + _L0_gnn_ref(h, edge_index, L0_gnn_W1, L0_gnn_att_src1, L0_gnn_att_dst1, L0_gnn_b1, L0_gnn_W2, L0_gnn_att_src2, L0_gnn_att_dst2, L0_gnn_b2)
    h = jnp.maximum(_layernorm(x, axis=-1), 0.0)
    x = x + _L1_gnn_ref(h, edge_index, edge_type_34, L1_gnn_W_rel, L1_gnn_W_root, L1_gnn_b_rgcn, L1_gnn_W_gcn, L1_gnn_b_gcn)
    return x

_drawn_inputs = setup_inputs


def setup_inputs(seed=0):
    import zlib

    import numpy as np

    out = dict(_drawn_inputs(seed))
    spreads = {'L0_gnn_b1': (0.0, 0.1),
     'L0_gnn_b2': (0.0, 0.1),
     'L1_gnn_b_rgcn': (0.0, 0.1),
     'L1_gnn_b_gcn': (0.0, 0.1)}
    factors = {'L0_gnn_att_src1': 3.465,
     'L0_gnn_att_dst1': 8.0,
     'L0_gnn_att_src2': 8.0,
     'L0_gnn_att_dst2': 8.0}
    for name, (base, spread) in spreads.items():
        noise = np.random.default_rng([zlib.crc32(name.encode()), seed]).standard_normal(out[name].shape)
        drawn = base * np.exp(spread * noise) if base else spread * noise
        out[name] = jnp.asarray(drawn.astype(out[name].dtype))
    for name, factor in factors.items():
        out[name] = (out[name] * factor).astype(out[name].dtype)
    return out
```

```python
import concourse.bass as bass
from concourse import mybir
from contextlib import ExitStack


P = 128
NODES = 1250
DIM = 768
EDGES = 20000
HEADS, HEAD_DIM = 8, 128
RELATIONS = 34
NEG_SLOPE = 0.2
SOFTMAX_EPS = 1e-16
LN_EPS = 1e-5
NEGATIVE = -1e30
BIG = 3e38

NT = -(-NODES // P)
LAST = NODES - (NT - 1) * P
NP = NT * P
KD = DIM // P
HID = HEADS * HEAD_DIM
KH = HID // P
HCOLS = HEAD_DIM + 1

EP, EC = 125, EDGES // 125
REL_TILES = (EDGES - RELATIONS) // P + 1 + RELATIONS
REL_TILES += REL_TILES % 2
GT = 4
GROUPS = (EDGES - NT) // (GT * P) + 1 + NT
GROUPS += GROUPS % 2
DST_TILES = GROUPS * GT
F_SRC, F_DLOC, F_REL, F_FLAT, F_SLOT, FIELDS = 0, 1, 2, 3, 4, 8
CC = NP + RELATIONS


def gnn_kernel(nc, x, src, dst, etype, W1, as1, ad1, b1, W2, as2, ad2, b2,
               Wrel, Wroot, brg, Wgcn, bgcn, out):
    f32, bf16, i32 = mybir.dt.float32, mybir.dt.bfloat16, mybir.dt.int32
    ALU, ACT, AX = mybir.AluOpType, mybir.ActivationFunctionType, mybir.AxisListType
    ds = bass.ds

    def dram(name, shape, dt=f32):
        return nc.dram_tensor(name, shape, dt, kind="Internal").ap()

    dst_table = dram("dst_table", (DST_TILES * P, FIELDS))
    rel_table = dram("rel_table", (REL_TILES * P, 1))
    uv_rows = dram("uv_rows", (2 * HEADS * NT, P))
    m_rows = dram("m_rows", (HEADS * NT, P))
    uv2_rows = dram("uv2_rows", (2 * NT, P))
    m2_rows = dram("m2_rows", (NT, P))
    inv_count = dram("inv_count", (NP * RELATIONS, 1))
    h1_dram = dram("h1_dram", (NP, HID))
    h_dram = dram("h_dram", (NP, DIM))
    msg_dram = dram("msg_dram", (REL_TILES * P, DIM))

    def row_of(rows, r):
        return rows[r * NT:(r + 1) * NT, :].rearrange("(o a) b -> o (a b)", o=1).to_broadcast([P, NP])

    def vector_row(v, n):
        return v.rearrange("(o n) -> o n", o=1).to_broadcast([P, n])

    top = ExitStack()
    with top:
        def holder(stack):
            def sb(name, shape, dt=f32):
                return stack.enter_context(nc.sbuf_tensor(name, shape, dt))
            return sb

        def sem(name):
            return top.enter_context(nc.semaphore(name))

        keep = holder(top)
        PS = top.enter_context(nc.psum_tensor("PS", [P, 8, 512], f32))
        PSf = PS[:, :, :].rearrange("p b n -> p (b n)")

        def banks(b, n):
            return PSf[:, b * 512:b * 512 + n]

        iota = keep("iota", [P, NP])
        pidx = keep("pidx", [P, 1])
        ident = keep("ident", [P, P])
        eps_ln = keep("eps_ln", [P, 1])
        region_x = keep("region_x", [P, NT * DIM])
        region_h = keep("region_h", [P, NT * HEADS * HCOLS])
        dinv = keep("dinv", [P, NT])
        etab = keep("etab", [P, DST_TILES, FIELDS])
        rtab = keep("rtab", [P, REL_TILES])
        tile_rel = keep("tile_rel", [1, REL_TILES], i32)
        rel_end = keep("rel_end", [1, RELATIONS], i32)
        group_tile = keep("group_tile", [1, GROUPS], i32)
        pos_rel = keep("pos_rel", [P, EC])
        pos_dst = keep("pos_dst", [P, EC])
        src_f = keep("src_f", [P, EC])
        weight = keep("weight", [P, DST_TILES + 4])
        uv = keep("uv", [P, 2 * HEADS, NT])
        uv2 = keep("uv2", [P, 2, NT])
        x_sb = region_x[:, :].rearrange("p (j i) -> p j i", i=DIM)
        x2 = x_sb
        mask = region_x[:, 0:NT * NP // 2].bitcast(bf16).rearrange("p (j s) -> p j s", s=NP)
        hA = region_h[:, :].rearrange("p (j h c) -> p j h c", h=HEADS, c=HCOLS)
        hB = region_h[:, 0:NT * (DIM + 1)].rearrange("p (j c) -> p j c", c=DIM + 1)
        acc = region_h[:, 0:NT * DIM].rearrange("p (j c) -> p j c", c=DIM)

        s_chain, links = sem("dve_chain"), [0]

        def chain(dve):
            def link(ins):
                links[0] += 1
                ins.then_inc(s_chain, 1)
                dve.wait_ge(s_chain, links[0])
            return link

        s_go = sem("gather_go")

        s_go_sp = sem("sync_go")

        class Projection:
            def __init__(self, tag, k, widths):
                self.k, self.widths = k, widths
                self.turned = sem(tag + "_tile_turned")
                self.moved = sem(tag + "_tile_moved")
                self.multiplied = sem(tag + "_tile_multiplied")
                self.taken = sem(tag + "_tile_taken")

        def project_pe(pe, pj, source, input_ready, xT, rhs):
            def turn(j):
                ready = input_ready[0]
                pe.wait_ge(ready[j % 2] if isinstance(ready, list) else ready, input_ready[1](j))
                if j:
                    pe.wait_ge(pj.moved, j)
                for k in range(pj.k):
                    last = nc.tensor.transpose(banks(0, 1024)[:, k * P:(k + 1) * P],
                                               source(j)[:, k * P:(k + 1) * P], ident[:, :])
                last.then_inc(pj.turned, 1)

            turn(0)
            for j in range(NT):
                if j + 1 < NT:
                    turn(j + 1)
                pe.wait_ge(pj.moved, j + 1)
                if j >= 2:
                    pe.wait_ge(pj.taken, j - 1)
                for k in range(pj.k):
                    at = 0
                    for w in pj.widths:
                        last = nc.tensor.matmul(banks(2 + 3 * (j % 2), 1536)[:, at:at + w],
                                                xT[:, j % 2, k, :], rhs[:, k, at:at + w],
                                                start=(k == 0), stop=(k == pj.k - 1))
                        at += w
                last.then_inc(pj.multiplied, 1)

        def project_act(act, pj, xT, move=None):
            for j in range(NT):
                act.wait_ge(pj.turned, j + 1)
                if j >= 2:
                    act.wait_ge(pj.multiplied, j - 1)
                if move is None:
                    nc.scalar.copy(xT[:, j % 2, 0:pj.k, :].rearrange("p k n -> p (k n)"),
                                   banks(0, pj.k * P)).then_inc(pj.moved, 1)
                else:
                    move(j).then_inc(pj.moved, 1)

        with ExitStack() as st:
            sb = holder(st)
            tri = sb("tri", [P, P])
            ones = sb("ones", [P, P])
            w1 = sb("w1", [P, HEADS, DIM])
            attc = sb("attc", [P, HEADS, 2])
            w1T = sb("w1T", [P, KD, HID + 2 * HEADS])
            h0T = sb("h0T", [P, 2, KD, P])
            stats = sb("stats", [P, NT, 2, 6])
            mv = sb("mv", [P, NT, 2])
            rstd = sb("rstd", [P, NT])
            nmr = sb("nmr", [P, NT])
            rows_sb = sb("rows_sb", [80, 2, P])

            s_const, s_ids, s_x, s_w1, s_att = (sem(n) for n in
                                                ("const", "ids", "x_in", "w1_in", "att_in"))
            s_w1t, s_w1e, s_wa, s_mv, s_sd, s_ln, s_h0 = (sem(n) for n in (
                "w1_turned", "w1_moved", "att_folded", "ln_stats", "ln_sd", "ln_scale", "h0"))
            s_tot, s_pref, s_tabs, s_ones, s_blank = (sem(n) for n in
                                             ("bucket_tot", "bucket_prefix", "tables_blank", "ones_col", "blank_rows"))
            s_pos, s_stage = (sem(n) for n in ("edge_pos", "edge_staged"))
            s_scat = [sem(f"dst_scattered{u}") for u in range(4)]
            s_uvT, s_uve, s_uvo, s_pad = (sem(n) for n in ("uv_turned", "uv_moved", "uv_out", "x_pad"))
            pj = Projection("w1", KD, [512, 512, 2 * HEADS])

            with ExitStack() as st2:
                sb2 = holder(st2)
                ids = sb2("ids", [P, 3, EC], i32)
                cut = sb2("cut", [P, 2, EC], i32)
                keyr = sb2("keyr", [P, EC])
                keyd = sb2("keyd", [P, EC])
                fields = sb2("fields", [P, EC, FIELDS])
                work = sb2("work", [P, 2 * RELATIONS * EC])
                hot = work[:, 0:RELATIONS * EC].rearrange("p (b c) -> p b c", c=EC)
                run = work[:, RELATIONS * EC:].rearrange("p (b c) -> p b c", c=EC)
                before = sb2("before", [P, RELATIONS])
                tot = sb2("tot", [P, RELATIONS])
                tiles = sb2("tiles", [P, RELATIONS])
                tilesi = sb2("tilesi", [P, RELATIONS], i32)
                base = sb2("base", [P, RELATIONS])
                off = sb2("off", [P, RELATIONS])
                cmpr = sb2("cmpr", [1, REL_TILES])
                blank = sb2("blank", [P, DST_TILES * FIELDS])
                stage_row = sb2("stage_row", [P, 4, FIELDS])
                stage_idx = sb2("stage_idx", [P, 4, 1], i32)

                with nc.Block() as block:
                    @block.sync
                    def _(sp):
                        for n, v in enumerate((src, dst, etype)):
                            sp.dma_start(ids[:EP, n, :], v.rearrange("(p c) -> p c", c=EC)).then_inc(s_ids, 16)
                        sp.dma_start(w1[:, :, :], W1.rearrange("(h c) i -> c h i", c=P)).then_inc(s_w1, 16)
                        with nc.allow_non_contiguous_dma(reason="attention vectors as columns"):
                            sp.dma_start(attc[:, :, 0], as1.rearrange("h c -> c h")).then_inc(s_att, 16)
                            sp.dma_start(attc[:, :, 1], ad1.rearrange("h c -> c h")).then_inc(s_att, 16)
                        sp.dma_start(x_sb[:, 0:NT - 1, :], x[0:(NT - 1) * P, :].rearrange("(j p) i -> p j i", p=P)).then_inc(s_x, 16)
                        sp.wait_ge(s_pad, 1)
                        sp.dma_start(x_sb[:LAST, NT - 1, :], x[(NT - 1) * P:NODES, :]).then_inc(s_x, 16)
                        sp.wait_ge(s_uve, 2)
                        for c in range(2):
                            sp.dma_start(uv_rows[80 * c:80 * c + 80, :], rows_sb[:, c, :]).then_inc(s_uvo, 16)
                        sp.wait_ge(s_uvo, 32)

                    @block.gpsimd
                    def _(pool):
                        pool.memset(x_sb[:, NT - 1, :], 0.0).then_inc(s_pad, 1)
                        pool.iota(iota[:, :], [[1, NP]], base=0, channel_multiplier=0,
                                  allow_small_or_imprecise_dtypes=True).then_inc(s_const, 1)
                        pool.iota(pidx[:, :], [[1, 1]], base=0, channel_multiplier=1,
                                  allow_small_or_imprecise_dtypes=True).then_inc(s_const, 1)
                        pool.memset(blank[:, :], 0.0).then_inc(s_blank, 1)
                        pool.wait_ge(s_blank, 1)
                        pool.dma_start(rel_table.rearrange("(p a) o -> p (a o)", p=P),
                                       blank[:, 0:REL_TILES]).then_inc(s_tabs, 16)
                        pool.wait_ge(s_tabs, 16)
                        pool.memset(blank[:, :].rearrange("p (a f) -> p a f", f=FIELDS)[:, :, F_DLOC:F_DLOC + 1], -1.0).then_inc(s_blank, 1)
                        pool.wait_ge(s_blank, 2)
                        pool.dma_start(dst_table.rearrange("(p a) f -> p (a f)", p=P),
                                       blank[:, :]).then_inc(s_tabs, 16)
                        pool.wait_ge(s_tabs, 32)
                        with pool.Fori(0, EC // 4) as i:
                            for u in range(4):
                                pool.wait_ge(s_stage, i * 4 + (u + 1))
                                pool.sem_inc(s_go, 1)
                                pool.indirect_dma_start(dst_table, bass.IndirectOffsetOnAxis(stage_idx[:EP, u, :], 0),
                                                        stage_row[:EP, u, :], None).then_inc(s_scat[u], 16)
                        for u in range(4):
                            pool.wait_ge(s_scat[u], 4 * EC)

                    @block.scalar
                    def _(act):
                        act.wait_ge(s_const, 2)
                        act.wait_ge(s_w1, 16)
                        for g in range(2 * KD):
                            act.wait_ge(s_w1t, g + 1)
                            nc.scalar.copy(w1T[:, g // 2, 512 * (g % 2):512 * (g % 2) + 512],
                                           banks(g % 2, 512)).then_inc(s_w1e, 1)
                        act.wait_ge(s_wa, 1)
                        nc.scalar.copy(w1T[:, :, HID:], banks(2, 16 * KD).rearrange("p (k c) -> p k c", k=KD)).then_inc(s_w1e, 1)
                        act.wait_ge(s_mv, 1)
                        nc.scalar.activation(rstd[:, :], mv[:, :, 1], ACT.Sqrt, bias=eps_ln[:, :]).then_inc(s_sd, 1)
                        act.wait_ge(s_ln, 1)
                        for j in range(NT):
                            nc.scalar.activation(x_sb[:, j, :], x_sb[:, j, :], ACT.Relu, bias=nmr[:, j:j + 1],
                                                 scale=rstd[:, j:j + 1]).then_inc(s_h0, 1)
                        project_act(act, pj, h0T)
                        for c in range(2):
                            act.wait_ge(s_uvT, c + 1)
                            nc.scalar.copy(rows_sb[:, c, :], banks(c, P)[:80, :]).then_inc(s_uve, 1)
                        act.wait_ge(s_pos, 1)

                        def stage(t, u):
                            nc.scalar.copy(stage_row[:EP, u, :], fields[:EP, ds(t, 1), :].rearrange("p o f -> p (o f)"))
                            nc.scalar.copy(stage_idx[:EP, u, :], pos_dst[:EP, ds(t, 1)]).then_inc(s_stage, 1)

                        for u in range(4):
                            stage(u, u)
                        with act.Fori(1, EC // 4) as i:
                            for u in range(4):
                                act.wait_ge(s_scat[u], i * 16)
                                stage(i * 4 + u, u)

                    @block.vector
                    def _(dve):
                        link = chain(dve)
                        v = nc.vector
                        v.memset(eps_ln[:, :], LN_EPS)
                        v.memset(hA[:, :, :, HEAD_DIM:], 1.0).then_inc(s_ones, 1)
                        link(v.memset(ones[:, :], 1.0))
                        dve.wait_ge(s_const, 2)
                        v.tensor_scalar(tri[:, :], iota[:, 0:P], pidx[:, :], None, ALU.is_gt)
                        v.tensor_scalar(ident[:, :], iota[:, 0:P], pidx[:, :], None, ALU.is_equal).then_inc(s_const, 1)
                        dve.wait_ge(s_x, 32)
                        for j in range(NT):
                            for c in range(2):
                                last = v.bn_stats(stats[:, j, c, :], x_sb[:, j, c * 384:(c + 1) * 384])
                        link(last)
                        for j in range(NT):
                            last = v.bn_aggr(mv[:, j, :], stats[:, j, :, :].rearrange("p a b -> p (a b)"))
                        last.then_inc(s_mv, 1)
                        dve.wait_ge(s_sd, 1)
                        link(v.reciprocal(rstd[:, :], rstd[:, :]))
                        v.scalar_tensor_tensor(nmr[:, :], mv[:, :, 0], -1.0, rstd[:, :], ALU.mult, ALU.mult).then_inc(s_ln, 1)

                        dve.wait_ge(s_ids, 48)
                        v.tensor_single_scalar(cut[:EP, 0, :], ids[:EP, 1, :], 7, ALU.arith_shift_right)
                        link(v.tensor_single_scalar(cut[:EP, 1, :], ids[:EP, 1, :], P - 1, ALU.bitwise_and))
                        v.memset(fields[:, :, :], 0.0)
                        v.tensor_copy(keyd[:EP, :], cut[:EP, 0, :])
                        link(v.tensor_copy(keyr[:EP, :], ids[:EP, 2, :]))
                        v.tensor_copy(fields[:EP, :, F_SRC], ids[:EP, 0, :])
                        v.tensor_copy(fields[:EP, :, F_DLOC], cut[:EP, 1, :])
                        v.tensor_copy(fields[:EP, :, F_REL], keyr[:EP, :])
                        link(v.tensor_copy(fields[:EP, :, F_FLAT], ids[:EP, 1, :]))
                        link(v.scalar_tensor_tensor(fields[:EP, :, F_FLAT], fields[:EP, :, F_FLAT], float(RELATIONS),
                                                    keyr[:EP, :], ALU.mult, ALU.add))

                        def places(n, key, nb, unit_shift, least, pos):
                            h, r = hot[:EP, 0:nb, :], run[:EP, 0:nb, :]
                            link(v.tensor_tensor(h, key[:EP, :].unsqueeze(1).to_broadcast([EP, nb, EC]),
                                                 iota[:EP, 0:nb].unsqueeze(2).to_broadcast([EP, nb, EC]), ALU.is_equal))
                            hf, rf = h.rearrange("p b c -> p (b c)"), r.rearrange("p b c -> p (b c)")
                            link(v.tensor_tensor_scan(rf, hf, hf, 0.0, ALU.add, ALU.max))
                            link(v.memset(before[:EP, 0:1], 0.0))
                            link(v.tensor_copy(before[:EP, 1:nb], r[:, 0:nb - 1, EC - 1]))
                            v.tensor_tensor(tot[:EP, 0:nb], r[:, :, EC - 1], before[:EP, 0:nb], ALU.subtract).then_inc(s_tot, 1)
                            dve.wait_ge(s_pref, n + 1)
                            b = 3 + n
                            link(v.tensor_scalar(tiles[:, 0:nb], banks(b, 128)[:, 64:64 + nb], float(2 ** unit_shift - 1), None, ALU.add))
                            link(v.tensor_copy(tilesi[:, 0:nb], tiles[:, 0:nb]))
                            link(v.tensor_single_scalar(tilesi[:, 0:nb], tilesi[:, 0:nb], unit_shift, ALU.arith_shift_right))
                            link(v.tensor_copy(tiles[:, 0:nb], tilesi[:, 0:nb]))
                            link(v.tensor_scalar(tiles[:, 0:nb], tiles[:, 0:nb], least, None, ALU.max))
                            link(v.tensor_tensor_scan(base[:, 0:nb], tiles[:, 0:nb], tiles[:, 0:nb], 0.0, ALU.add, ALU.max))
                            link(v.tensor_tensor(base[:, 0:nb], base[:, 0:nb], tiles[:, 0:nb], ALU.subtract))
                            link(v.scalar_tensor_tensor(off[:EP, 0:nb], base[:EP, 0:nb], float(2 ** unit_shift),
                                                        banks(b, 64)[:EP, 0:nb], ALU.mult, ALU.add))
                            link(v.scalar_tensor_tensor(off[:EP, 0:nb], off[:EP, 0:nb], -1.0, before[:EP, 0:nb],
                                                        ALU.add, ALU.subtract))
                            link(v.tensor_tensor(r, r, off[:EP, 0:nb].unsqueeze(2).to_broadcast([EP, nb, EC]), ALU.add))
                            link(v.tensor_tensor(h, h, r, ALU.mult))
                            link(v.tensor_reduce(pos, h.rearrange("p b c -> p c b"), AX.X, ALU.add))

                        def group_of(units, nb, result):
                            c = work[0:1, 0:units * nb].rearrange("p (t b) -> p t b", b=nb)
                            link(v.tensor_tensor(c, base[0:1, 0:nb].unsqueeze(1).to_broadcast([1, units, nb]),
                                                 iota[0:1, 0:units].unsqueeze(2).to_broadcast([1, units, nb]), ALU.is_le))
                            link(v.tensor_reduce(cmpr[0:1, 0:units], c, AX.X, ALU.add))
                            link(v.tensor_scalar(cmpr[0:1, 0:units], cmpr[0:1, 0:units], -1.0, None, ALU.add))
                            link(v.tensor_copy(result, cmpr[0:1, 0:units]))

                        places(0, keyr, RELATIONS, 7, 1.0, pos_rel[:EP, :])
                        group_of(REL_TILES, RELATIONS, tile_rel[:, :])
                        link(v.tensor_tensor(off[0:1, :], base[0:1, :], tiles[0:1, :], ALU.add))
                        link(v.tensor_copy(rel_end[:, :], off[0:1, :]))
                        link(v.tensor_copy(fields[:EP, :, F_SLOT], pos_rel[:EP, :]))
                        places(1, keyd, NT, 9, 0.0, pos_dst[:EP, :])
                        group_of(GROUPS, NT, group_tile[:, :])
                        v.tensor_copy(src_f[:EP, :], ids[:EP, 0, :]).then_inc(s_pos, 1)

                        for j in range(NT):
                            dve.wait_ge(pj.multiplied, j + 1)
                            v.tensor_copy(hA[:, j, :, 0:HEAD_DIM],
                                          banks(2 + 3 * (j % 2), HID).rearrange("p (h c) -> p h c", h=HEADS))
                            v.tensor_copy(uv[:, :, j], banks(2 + 3 * (j % 2), HID + 2 * HEADS)[:, HID:]).then_inc(pj.taken, 1)

                    @block.tensor
                    def _(pe):
                        pe.wait_ge(s_const, 3)
                        pe.wait_ge(s_w1, 16)
                        for g in range(2 * KD):
                            if g >= 2:
                                pe.wait_ge(s_w1e, g - 1)
                            for u in range(4):
                                h = 4 * (g % 2) + u
                                last = nc.tensor.transpose(banks(g % 2, 512)[:, u * P:(u + 1) * P],
                                                           w1[:, h, (g // 2) * P:(g // 2 + 1) * P], ident[:, :])
                            last.then_inc(s_w1t, 1)
                        pe.wait_ge(s_att, 32)
                        for k in range(KD):
                            for h in range(HEADS):
                                last = nc.tensor.matmul(banks(2, 96)[:, k * 16 + 2 * h:k * 16 + 2 * h + 2],
                                                        w1[:, h, k * P:(k + 1) * P], attc[:, h, :], start=True, stop=True)
                        last.then_inc(s_wa, 1)
                        for n, nb in enumerate((RELATIONS, NT)):
                            pe.wait_ge(s_tot, n + 1)
                            nc.tensor.matmul(banks(3 + n, 64)[:EP, 0:nb], tri[:EP, :EP], tot[:EP, 0:nb], start=True, stop=True)
                            nc.tensor.matmul(banks(3 + n, 128)[:, 64:64 + nb], ones[:EP, :], tot[:EP, 0:nb],
                                             start=True, stop=True).then_inc(s_pref, 1)
                        pe.wait_ge(s_w1e, 2 * KD + 1)
                        pe.wait_ge(s_pos, 1)
                        project_pe(pe, pj, lambda j: x_sb[:, j, :], (s_h0, lambda j: j + 1), h0T, w1T)
                        pe.wait_ge(pj.taken, NT)
                        for c in range(2):
                            nc.tensor.transpose(banks(c, P)[:80, :], uv[:, :, :].rearrange("p c j -> p (c j)")[:, 80 * c:80 * c + 80],
                                                ident[:, :]).then_inc(s_uvT, 1)

        CT = keep("CT", [P, NT, NP])
        with ExitStack() as st:
            sb = holder(st)
            C = sb("C", [P, NT, CC])
            with ExitStack() as st2:
                sb2 = holder(st2)
                hot_src = sb2("hot_src", [P, GT, CC], bf16)
                hot_dst = sb2("hot_dst", [P, GT, P], bf16)
                inv = sb2("inv", [P, NT, RELATIONS])
                deg = sb2("deg", [P, NT])
                stage_row2 = sb2("stage_row2", [P, 4, 1])
                stage_idx2 = sb2("stage_idx2", [P, 4, 1], i32)
                s_et, s_rt, s_c0, s_hot, s_used, s_add = (sem(n) for n in (
                    "etab_in", "rtab_in", "counts_blank", "hot_ready", "hot_used", "group_added"))
                s_st2, s_inv, s_invo, s_cT, s_cTe, s_deg, s_sd2 = (sem(n) for n in (
                    "rel_staged", "inv_ready", "inv_out", "ct_turned", "ct_moved", "deg_ready", "deg_sqrt"))

                s_sc2 = [sem(f"rel_scattered{u}") for u in range(4)]

                with nc.Block() as block:
                    @block.sync
                    def _(sp):
                        sp.dma_start(etab[:, :, :], dst_table.rearrange("(t p) f -> p t f", p=P)).then_inc(s_et, 16)
                        sp.wait_ge(s_inv, 1)
                        sp.dma_start(inv_count.rearrange("(j p r) o -> p j (r o)", p=P, r=RELATIONS), inv[:, :, :]).then_inc(s_invo, 16)
                        sp.wait_ge(s_invo, 16)
                        for u in range(4):
                            sp.wait_ge(s_sc2[u], 4 * EC)
                        with nc.allow_non_contiguous_dma(reason="a slot list by partitions"):
                            sp.dma_start(rtab[:, :], rel_table.rearrange("(t p) o -> p (t o)", p=P)).then_inc(s_rt, 16)
                        sp.wait_ge(s_rt, 16)

                    @block.gpsimd
                    def _(pool):
                        with pool.Fori(0, EC // 4) as i:
                            for u in range(4):
                                pool.wait_ge(s_st2, i * 4 + (u + 1))
                                pool.sem_inc(s_go, 1)
                                pool.indirect_dma_start(rel_table, bass.IndirectOffsetOnAxis(stage_idx2[:EP, u, :], 0),
                                                        stage_row2[:EP, u, :], None).then_inc(s_sc2[u], 16)

                    @block.scalar
                    def _(act):

                        def stage(t, u):
                            nc.scalar.copy(stage_row2[:EP, u, :], src_f[:EP, ds(t, 1)])
                            nc.scalar.copy(stage_idx2[:EP, u, :], pos_rel[:EP, ds(t, 1)]).then_inc(s_st2, 1)

                        for u in range(4):
                            stage(u, u)
                        with act.Fori(1, EC // 4) as i:
                            for u in range(4):
                                act.wait_ge(s_sc2[u], i * 16)
                                stage(i * 4 + u, u)
                        act.wait_ge(s_deg, 1)
                        nc.scalar.activation(deg[:, :], deg[:, :], ACT.Sqrt).then_inc(s_sd2, 1)
                        for k in range(NT):
                            act.wait_ge(s_cT, k + 1)
                            nc.scalar.copy(CT[:, k, :], banks(3 * (k % 2), NP)).then_inc(s_cTe, 1)

                    @block.vector
                    def _(dve):
                        v = nc.vector
                        link = chain(dve)
                        link(v.memset(C[:, :, :].rearrange("p j c -> p (j c)"), 0.0))
                        dve.wait_ge(s_et, 16)
                        with dve.Fori(0, GROUPS // 2) as i:
                            for u in range(2 * GT):
                                t = i * (2 * GT) + u
                                dve.wait_ge(s_used, t + 1)
                                e = etab[:, ds(t, 1), :].rearrange("p o f -> p (o f)")
                                v.tensor_scalar(hot_src[:, u % GT, 0:NP], iota[:, :], e[:, F_SRC:F_SRC + 1], None, ALU.is_equal)
                                v.tensor_scalar(hot_src[:, u % GT, NP:], iota[:, 0:RELATIONS], e[:, F_REL:F_REL + 1], None, ALU.is_equal)
                                v.tensor_scalar(hot_dst[:, u % GT, :], iota[:, 0:P], e[:, F_DLOC:F_DLOC + 1], None, ALU.is_equal).then_inc(s_hot, 1)
                            for g in range(2):
                                at = dve.value_load(group_tile[0:1, ds(i * 2 + g, 1)], min_val=0, max_val=NT - 1)
                                dve.wait_ge(s_used, i * (2 * GT) + (g + 1) * GT + GT)
                                c = C[:, ds(at, 1), :].rearrange("p o c -> p (o c)")
                                v.tensor_tensor(c, c, banks(3 * g, CC), ALU.add).then_inc(s_add, 1)
                                dve.wait_ge(s_add, i * 2 + (g + 3))
                        link(v.tensor_scalar(inv[:, :, :], C[:, :, NP:], 1.0, None, ALU.max))
                        v.reciprocal(inv[:, :, :], inv[:, :, :]).then_inc(s_inv, 1)
                        link(v.tensor_reduce(deg[:, :], C[:, :, 0:NP], AX.X, ALU.add))
                        v.tensor_scalar(deg[:, :], deg[:, :], 1.0, None, ALU.add).then_inc(s_deg, 1)
                        for j in range(NT):
                            v.tensor_scalar(mask[:, j, :], C[:, j, 0:NP], 0.0, NEGATIVE, ALU.is_equal, ALU.mult)
                        dve.wait_ge(s_sd2, 1)
                        v.reciprocal(dinv[:, :], deg[:, :])

                    @block.tensor
                    def _(pe):
                        pe.sem_inc(s_used, GT)
                        pe.sem_inc(s_add, 2)
                        with pe.Fori(0, GROUPS // 2) as i:
                            for g in range(2):
                                pe.wait_ge(s_add, i * 2 + (g + 1))
                                for q in range(GT):
                                    u = g * GT + q
                                    pe.wait_ge(s_hot, i * (2 * GT) + (u + 1))
                                    for a in range(0, CC, 512):
                                        w = min(512, CC - a)
                                        last = nc.tensor.matmul(banks(3 * g, 1536)[:, a:a + w], hot_dst[:, q, :], hot_src[:, q, a:a + w],
                                                                start=(q == 0), stop=(q == GT - 1))
                                    last.then_inc(s_used, 1)
                        pe.wait_ge(s_add, GROUPS + 2)
                        for k in range(NT):
                            if k >= 2:
                                pe.wait_ge(s_cTe, k - 1)
                            for j in range(NT):
                                last = nc.tensor.transpose(banks(3 * (k % 2), NP)[:, j * P:(j + 1) * P],
                                                           C[:, j, k * P:(k + 1) * P], ident[:, :])
                            last.then_inc(s_cT, 1)


        SLOTS = 5
        with ExitStack() as st:
            sb = holder(st)
            rows_v = sb("rows_v", [P, 2, NP])
            rows_m = sb("rows_m", [P, 2, NP])
            tt = sb("tt", [P, SLOTS, NP])
            M = sb("M", [P, HEADS, NT])
            Mz = sb("Mz", [P, HEADS, NT])
            u_pos = sb("u_pos", [P, HEADS, NT])
            u_neg = sb("u_neg", [P, HEADS, NT])
            m_sb = sb("m_sb", [80, P])
            rden = sb("rden", [P, NT])
            hn = sb("hn", [P, 2, NT, HEAD_DIM])
            widx = sb("widx", [P, 4, 1], i32)
            wst = sb("wst", [P, 4, 1])
            s_row = [sem("row_u0"), sem("row_u1")]
            s_rowf, s_M, s_MT, s_Me, s_Mo = (sem(n) for n in ("row_free", "m_ready", "m_turned", "m_moved", "m_out"))
            s_vm = [sem("vm_row0"), sem("vm_row1")]
            s_pre, s_sub, s_exp, s_mul, s_mm = (sem(n) for n in ("leaky", "shifted", "exped", "probs", "head_tile_done"))
            s_hn, s_den, s_hfree, s_wkeep, s_rm = (sem(n) for n in ("head_out", "head_sums", "head_free", "w_kept", "rows_mixed"))
            s_hd = [sem("head_stored0"), sem("head_stored1")]
            s_wst, s_wld = sem("w_staged"), [sem(f"w_gathered{u}") for u in range(4)]

            with nc.Block() as block:
                @block.sync
                def _(sp):
                    for h in range(HEADS):
                        if h >= 2:
                            sp.wait_ge(s_rowf, h - 1)
                        sp.dma_start(rows_v[:, h % 2, :], row_of(uv_rows, 2 * h)).then_inc(s_row[h % 2], 16)
                    sp.wait_ge(s_Me, 1)
                    sp.dma_start(m_rows, m_sb[:, :]).then_inc(s_Mo, 16)
                    sp.wait_ge(s_Mo, 16)
                    vr = uv_rows.rearrange("(h c j) p -> h c (j p)", c=2, j=NT)
                    mr = m_rows.rearrange("(h j) p -> h (j p)", j=NT)
                    h1v = h1_dram.rearrange("(j p) (h c) -> h p j c", p=P, h=HEADS)

                    def load(h, g):
                        sp.dma_start(rows_v[:, g, :], vr[ds(h, 1), 1, :].to_broadcast([P, NP])).then_inc(s_vm[g], 16)
                        sp.dma_start(rows_m[:, g, :], mr[ds(h, 1), :].to_broadcast([P, NP])).then_inc(s_vm[g], 16)

                    def store(h, g):
                        sp.wait_ge(s_hn, h + 3)
                        sp.sem_inc(s_go_sp, 1)
                        sp.dma_start(h1v[ds(h, 1), :, :, :].rearrange("o p j c -> (o p) j c"), hn[:, g, :, :]).then_inc(s_hd[g], 16)

                    for g in range(2):
                        load(g, g)
                    with sp.Fori(0, HEADS // 2 - 1) as i:
                        for g in range(2):
                            store(i * 2 + g, g)
                            load(i * 2 + (g + 2), g)
                            sp.wait_ge(s_hd[g], i * 16 + 16)
                            sp.sem_inc(s_hfree, 1)
                    for g in range(2):
                        store(HEADS - 2 + g, g)
                    for g in range(2):
                        sp.wait_ge(s_hd[g], 8 * HEADS)

                @block.gpsimd
                def _(pool):
                    def gather(t, u):
                        nc.gpsimd.tensor_copy(widx[:, u, :], etab[:, ds(t, 1), F_FLAT:F_FLAT + 1].rearrange("p o f -> p (o f)")).then_inc(s_wst, 1)
                        pool.wait_ge(s_wst, t + 1)
                        pool.sem_inc(s_go, 1)
                        pool.indirect_dma_start(wst[:, u, :], None, inv_count,
                                                bass.IndirectOffsetOnAxis(widx[:, u, :], 0)).then_inc(s_wld[u], 16)

                    for u in range(4):
                        gather(u, u)
                    with pool.Fori(1, DST_TILES // 4) as i:
                        for u in range(4):
                            pool.wait_ge(s_wld[u], i * 16)
                            nc.gpsimd.tensor_copy(weight[:, ds(i * 4 + u, 1)], wst[:, u, :]).then_inc(s_wkeep, 1)
                            pool.wait_ge(s_wkeep, i * 4 + (u - 3))
                            gather(i * 4 + u, u)
                    for u in range(4):
                        pool.wait_ge(s_wld[u], 4 * DST_TILES)
                        nc.gpsimd.tensor_copy(weight[:, DST_TILES + u:DST_TILES + u + 1], wst[:, u, :])

                @block.scalar
                def _(act):
                    act.wait_ge(s_MT, 1)
                    nc.scalar.copy(m_sb[:, :], banks(0, P)[:80, :]).then_inc(s_Me, 1)
                    with act.Fori(0, HEADS // 2) as i:
                        for g in range(2):
                            h = i * 2 + g
                            act.wait_ge(s_vm[g], i * 32 + 32)

                            def leaky(k):
                                act.wait_ge(s_mm, h * NT + (k + 1))
                                nc.scalar.activation(tt[:, k % SLOTS, :], rows_v[:, g, :], ACT.Relu,
                                                     bias=u_pos[:, ds(h, 1), k:k + 1].rearrange("p o k -> p (o k)"),
                                                     scale=1.0 - NEG_SLOPE).then_inc(s_pre, 1)
                            leaky(0)
                            for k in range(NT):
                                if k + 1 < NT:
                                    leaky(k + 1)
                                act.wait_ge(s_sub, h * NT + (k + 1))
                                nc.scalar.activation(tt[:, k % SLOTS, :], tt[:, k % SLOTS, :], ACT.Exp).then_inc(s_exp, 1)

                @block.vector
                def _(dve):
                    v = nc.vector
                    link = chain(dve)
                    for h in range(HEADS):
                        dve.wait_ge(s_row[h % 2], 16 * (h // 2 + 1))
                        for j in range(NT):
                            link(v.tensor_tensor_reduce(out=tt[:, 0, :], in0=mask[:, j, :], in1=rows_v[:, h % 2, :], scale=1.0,
                                                        scalar=NEGATIVE, op0=ALU.add, op1=ALU.max, accum_out=M[:, h, j:j + 1]))
                        dve.sem_inc(s_rowf, 1)
                    dve.wait_ge(s_rowf, HEADS)
                    uvc = uv[:, :, :].rearrange("p (h c) j -> p h c j", c=2)
                    v.tensor_scalar(u_pos[:, :, :], uvc[:, :, 0, :], 1.0 - NEG_SLOPE, None, ALU.mult)
                    v.tensor_scalar(u_neg[:, :, :], uvc[:, :, 0, :], NEG_SLOPE, None, ALU.mult)
                    link(v.scalar_tensor_tensor(M[:, :, :], M[:, :, :], NEGATIVE / 2, M[:, :, :], ALU.is_gt, ALU.mult))
                    link(v.tensor_tensor(M[:, :, :], M[:, :, :], uvc[:, :, 1, :], ALU.add))
                    link(v.tensor_scalar(Mz[:, :, :], M[:, :, :], NEG_SLOPE, None, ALU.mult))
                    v.tensor_tensor(Mz[:, :, :], Mz[:, :, :], M[:, :, :], ALU.max).then_inc(s_M, 1)
                    hd = HEAD_DIM
                    with dve.Fori(0, HEADS // 2) as i:
                        for g in range(2):
                            h = i * 2 + g
                            dve.wait_ge(s_vm[g], i * 32 + 32)
                            v.scalar_tensor_tensor(rows_m[:, g, :], rows_v[:, g, :], NEG_SLOPE, rows_m[:, g, :],
                                                   ALU.mult, ALU.subtract).then_inc(s_rm, 1)
                            dve.wait_ge(s_rm, h + 1)

                            def shift(k):
                                dve.wait_ge(s_pre, h * NT + (k + 1))
                                v.scalar_tensor_tensor(tt[:, k % SLOTS, :], tt[:, k % SLOTS, :],
                                                       u_neg[:, ds(h, 1), k:k + 1].rearrange("p o k -> p (o k)"),
                                                       rows_m[:, g, :], ALU.add, ALU.add).then_inc(s_sub, 1)
                            shift(0)
                            for k in range(NT):
                                if k + 1 < NT:
                                    shift(k + 1)
                                dve.wait_ge(s_exp, h * NT + (k + 1))
                                v.scalar_tensor_tensor(tt[:, k % SLOTS, :], tt[:, k % SLOTS, :], BIG, CT[:, k, :],
                                                       ALU.min, ALU.mult).then_inc(s_mul, 1)
                            dve.wait_ge(s_mm, h * NT + (NT + SLOTS))
                            dve.wait_ge(s_hfree, h + 1)
                            three = PS[:, 4 * g:4 * g + 3, 0:3 * HCOLS].rearrange("p q (t c) -> p q t c", c=HCOLS)
                            v.tensor_scalar(rden[:, 0:9].rearrange("p (q t) -> p q t", t=3), three[:, :, :, hd], SOFTMAX_EPS, None, ALU.add)
                            link_sem = v.tensor_scalar(rden[:, 9:10], banks(4 * g + 3, HCOLS)[:, hd:], SOFTMAX_EPS, None, ALU.add)
                            link_sem.then_inc(s_den, 1)
                            dve.wait_ge(s_den, h * 2 + 1)
                            v.reciprocal(rden[:, :], rden[:, :]).then_inc(s_den, 1)
                            dve.wait_ge(s_den, h * 2 + 2)
                            for q in range(3):
                                v.tensor_tensor(hn[:, g, 3 * q:3 * q + 3, :], three[:, q, :, 0:hd],
                                                rden[:, 3 * q:3 * q + 3].unsqueeze(2).to_broadcast([P, 3, hd]), ALU.mult)
                            v.tensor_scalar(hn[:, g, 9, :], banks(4 * g + 3, hd), rden[:, 9:10], None, ALU.mult).then_inc(s_hn, 1)

                @block.tensor
                def _(pe):
                    pe.sem_inc(s_mm, SLOTS)
                    pe.sem_inc(s_hn, 2)
                    pe.sem_inc(s_hfree, 2)
                    pe.wait_ge(s_M, 1)
                    nc.tensor.transpose(banks(0, P)[:80, :], Mz[:, :, :].rearrange("p h j -> p (h j)"), ident[:, :]).then_inc(s_MT, 1)
                    pe.wait_ge(s_Me, 1)
                    with pe.Fori(0, HEADS // 2) as i:
                        for g in range(2):
                            h = i * 2 + g
                            pe.wait_ge(s_hn, h + 1)
                            for k in range(NT):
                                pe.wait_ge(s_mul, h * NT + (k + 1))
                                for j in range(NT):
                                    last = nc.tensor.matmul(PS[:, 4 * g + j // 3, (j % 3) * HCOLS:(j % 3 + 1) * HCOLS],
                                                            tt[:, k % SLOTS, j * P:(j + 1) * P],
                                                            hA[:, k, ds(h, 1), :].rearrange("p o c -> p (o c)"),
                                                            start=(k == 0 and j % 3 == 0), stop=(k == NT - 1), skip_group_check=True)
                                last.then_inc(s_mm, 1)

        with ExitStack() as st:
            sb = holder(st)
            w2 = sb("w2", [P, KD, HID])
            att2 = sb("att2", [P, KD, 2])
            w2T = sb("w2T", [P, KH, DIM + 2])
            b1c = sb("b1c", [P, KH])
            h1 = sb("h1", [P, 2, HID])
            h1T = sb("h1T", [P, 2, KH, P])
            rows2 = sb("rows2", [2 * NT, P])
            s_w2, s_p2, s_w2t, s_w2e, s_wa2, s_h1, s_uT2, s_ue2, s_uo2, s_one2 = (sem(n) for n in (
                "w2_in", "att2_in", "w2_turned", "w2_moved", "att2_folded", "h1_in", "uv2_turned", "uv2_moved", "uv2_out", "ones2"))
            s_h1 = [sem("h1_in0"), sem("h1_in1")]
            pj2 = Projection("w2", KH, [512, DIM + 2 - 512])

            with nc.Block() as block:
                @block.sync
                def _(sp):
                    sp.dma_start(w2[:, :, :], W2.rearrange("(k p) c -> p k c", p=P)).then_inc(s_w2, 16)
                    with nc.allow_non_contiguous_dma(reason="vectors as columns"):
                        sp.dma_start(att2[:, :, 0], as2.rearrange("o (k p) -> p (o k)", p=P)).then_inc(s_p2, 16)
                        sp.dma_start(att2[:, :, 1], ad2.rearrange("o (k p) -> p (o k)", p=P)).then_inc(s_p2, 16)
                        sp.dma_start(b1c[:, :], b1.rearrange("(k p) -> p k", p=P)).then_inc(s_p2, 16)
                    for j in range(NT):
                        if j >= 2:
                            sp.wait_ge(pj2.turned, j - 1)
                        sp.dma_start(h1[:, j % 2, :], h1_dram[j * P:(j + 1) * P, :]).then_inc(s_h1[j % 2], 16)
                    sp.wait_ge(s_ue2, 1)
                    sp.dma_start(uv2_rows, rows2[:, :]).then_inc(s_uo2, 16)
                    sp.wait_ge(s_uo2, 16)

                @block.scalar
                def _(act):
                    for g in range(2 * KH):
                        act.wait_ge(s_w2t, g + 1)
                        nc.scalar.copy(w2T[:, g // 2, 384 * (g % 2):384 * (g % 2) + 384], banks(g % 2, 384)).then_inc(s_w2e, 1)
                    act.wait_ge(s_wa2, 1)
                    nc.scalar.copy(w2T[:, :, DIM:], banks(2, 2 * KH).rearrange("p (k c) -> p k c", k=KH)).then_inc(s_w2e, 1)
                    act.wait_ge(s_p2, 48)

                    def relu_bias(j):
                        for k in range(KH):
                            last = nc.scalar.activation(h1T[:, j % 2, k, :], banks(0, 1024)[:, k * P:(k + 1) * P],
                                                        ACT.Relu, bias=b1c[:, k:k + 1])
                        return last
                    project_act(act, pj2, h1T, relu_bias)
                    act.wait_ge(s_uT2, 1)
                    nc.scalar.copy(rows2[:, :], banks(0, P)[:2 * NT, :]).then_inc(s_ue2, 1)

                @block.vector
                def _(dve):
                    v = nc.vector
                    v.memset(hB[:, :, DIM:], 1.0)
                    for j in range(NT):
                        dve.wait_ge(pj2.multiplied, j + 1)
                        v.tensor_copy(hB[:, j, 0:DIM], banks(2 + 3 * (j % 2), DIM))
                        v.tensor_copy(uv2[:, :, j], banks(2 + 3 * (j % 2), DIM + 2)[:, DIM:]).then_inc(pj2.taken, 1)

                @block.tensor
                def _(pe):
                    pe.wait_ge(s_w2, 16)
                    for g in range(2 * KH):
                        if g >= 2:
                            pe.wait_ge(s_w2e, g - 1)
                        for u in range(3):
                            o = 3 * (g % 2) + u
                            last = nc.tensor.transpose(banks(g % 2, 384)[:, u * P:(u + 1) * P],
                                                       w2[:, o, (g // 2) * P:(g // 2 + 1) * P], ident[:, :])
                        last.then_inc(s_w2t, 1)
                    pe.wait_ge(s_p2, 48)
                    for k in range(KH):
                        for o in range(KD):
                            last = nc.tensor.matmul(banks(2, 16)[:, 2 * k:2 * k + 2], w2[:, o, k * P:(k + 1) * P], att2[:, o, :],
                                                    start=(o == 0), stop=(o == KD - 1))
                    last.then_inc(s_wa2, 1)
                    pe.wait_ge(s_w2e, 2 * KH + 1)

                    def h1_ready(j):
                        return 16 * (j // 2 + 1)
                    project_pe(pe, pj2, lambda j: h1[:, j % 2, :], (s_h1, h1_ready), h1T, w2T)
                    pe.wait_ge(pj2.taken, NT)
                    nc.tensor.transpose(banks(0, P)[:2 * NT, :], uv2[:, :, :].rearrange("p c j -> p (c j)"), ident[:, :]).then_inc(s_uT2, 1)

        with ExitStack() as st:
            sb = holder(st)
            row_a = sb("row_a", [P, NP])
            row_m = sb("row_m", [P, NP])
            pr = sb("pr", [P, NT, NP])
            M2 = sb("M2", [P, NT])
            Mz2 = sb("Mz2", [P, NT])
            u2p = sb("u2p", [P, NT])
            u2n = sb("u2n", [P, NT])
            m2_sb = sb("m2_sb", [NT, P])
            rden2 = sb("rden2", [P, NT])
            b2row = sb("b2row", [P, DIM])
            s_ra, s_rm, s_M2, s_M2T, s_M2e, s_M2o, s_b2, s_x2, s_xb = (sem(n) for n in (
                "row2_in", "rowm2_in", "m2_ready", "m2_turned", "m2_moved", "m2_out", "b2_in", "x_again", "x_pad2"))
            s_pre2, s_sub2, s_exp2, s_mul2, s_mm2, s_tk2 = (sem(n) for n in (
                "leaky2", "shifted2", "exped2", "probs2", "tile_done2", "tile_taken2"))

            with nc.Block() as block:
                @block.sync
                def _(sp):
                    sp.dma_start(row_a[:, :], row_of(uv2_rows, 0)).then_inc(s_ra, 16)
                    sp.dma_start(b2row[:, :], vector_row(b2, DIM)).then_inc(s_b2, 16)
                    sp.wait_ge(s_M2, 1)
                    sp.dma_start(row_a[:, :], row_of(uv2_rows, 1)).then_inc(s_ra, 16)
                    sp.wait_ge(s_M2e, 1)
                    sp.dma_start(m2_rows, m2_sb[:, :]).then_inc(s_M2o, 16)
                    sp.wait_ge(s_M2o, 16)
                    sp.dma_start(row_m[:, :], row_of(m2_rows, 0)).then_inc(s_rm, 16)
                    sp.dma_start(x2[:, 0:NT - 1, :], x[0:(NT - 1) * P, :].rearrange("(j p) i -> p j i", p=P)).then_inc(s_x2, 16)
                    sp.wait_ge(s_xb, 1)
                    sp.dma_start(x2[:LAST, NT - 1, :], x[(NT - 1) * P:NODES, :]).then_inc(s_x2, 16)

                @block.gpsimd
                def _(pool):
                    pool.wait_ge(s_M2, 1)
                    pool.memset(x2[:, NT - 1, :], 0.0).then_inc(s_xb, 1)

                @block.scalar
                def _(act):
                    act.wait_ge(s_M2T, 1)
                    nc.scalar.copy(m2_sb[:, :], banks(0, P)[:NT, :]).then_inc(s_M2e, 1)
                    act.wait_ge(s_ra, 32)
                    for k in range(NT):
                        nc.scalar.activation(pr[:, k, :], row_a[:, :], ACT.Relu, bias=u2p[:, k:k + 1],
                                             scale=1.0 - NEG_SLOPE).then_inc(s_pre2, 1)
                    for k in range(NT):
                        act.wait_ge(s_sub2, k + 1)
                        nc.scalar.activation(pr[:, k, :], pr[:, k, :], ACT.Exp).then_inc(s_exp2, 1)

                @block.vector
                def _(dve):
                    v = nc.vector
                    link = chain(dve)
                    dve.wait_ge(s_ra, 16)
                    for j in range(NT):
                        link(v.tensor_tensor_reduce(out=pr[:, 0, :], in0=mask[:, j, :], in1=row_a[:, :], scale=1.0,
                                                    scalar=NEGATIVE, op0=ALU.add, op1=ALU.max, accum_out=M2[:, j:j + 1]))
                    v.tensor_scalar(u2p[:, :], uv2[:, 0, :], 1.0 - NEG_SLOPE, None, ALU.mult)
                    v.tensor_scalar(u2n[:, :], uv2[:, 0, :], NEG_SLOPE, None, ALU.mult)
                    link(v.scalar_tensor_tensor(M2[:, :], M2[:, :], NEGATIVE / 2, M2[:, :], ALU.is_gt, ALU.mult))
                    link(v.tensor_tensor(M2[:, :], M2[:, :], uv2[:, 1, :], ALU.add))
                    link(v.tensor_scalar(Mz2[:, :], M2[:, :], NEG_SLOPE, None, ALU.mult))
                    v.tensor_tensor(Mz2[:, :], Mz2[:, :], M2[:, :], ALU.max).then_inc(s_M2, 1)
                    dve.wait_ge(s_rm, 16)
                    dve.wait_ge(s_ra, 32)
                    link(v.scalar_tensor_tensor(row_m[:, :], row_a[:, :], NEG_SLOPE, row_m[:, :], ALU.mult, ALU.subtract))

                    def shift(k):
                        dve.wait_ge(s_pre2, k + 1)
                        v.scalar_tensor_tensor(pr[:, k, :], pr[:, k, :], u2n[:, k:k + 1], row_m[:, :], ALU.add, ALU.add).then_inc(s_sub2, 1)
                    shift(0)
                    for k in range(NT):
                        if k + 1 < NT:
                            shift(k + 1)
                        dve.wait_ge(s_exp2, k + 1)
                        v.scalar_tensor_tensor(pr[:, k, :], pr[:, k, :], BIG, CT[:, k, :], ALU.min, ALU.mult).then_inc(s_mul2, 1)
                    dve.wait_ge(s_x2, 32)
                    dve.wait_ge(s_b2, 16)
                    for j in range(NT):
                        last = v.tensor_tensor(x2[:, j, :], x2[:, j, :], b2row[:, :], ALU.add)
                    link(last)
                    for j in range(NT):
                        o = banks(2 * (j % 4), DIM + 1)
                        dve.wait_ge(s_mm2, j + 1)
                        link(v.tensor_scalar(rden2[:, j:j + 1], o[:, DIM:], SOFTMAX_EPS, None, ALU.add))
                        link(v.reciprocal(rden2[:, j:j + 1], rden2[:, j:j + 1]))
                        v.scalar_tensor_tensor(x2[:, j, :], o[:, 0:DIM], rden2[:, j:j + 1], x2[:, j, :], ALU.mult, ALU.add).then_inc(s_tk2, 1)

                @block.tensor
                def _(pe):
                    pe.wait_ge(s_M2, 1)
                    nc.tensor.transpose(banks(0, P)[:NT, :], Mz2[:, :], ident[:, :]).then_inc(s_M2T, 1)
                    pe.wait_ge(s_M2e, 1)
                    for j in range(NT):
                        if j >= 4:
                            pe.wait_ge(s_tk2, j - 3)
                        for k in range(NT):
                            if j == 0:
                                pe.wait_ge(s_mul2, k + 1)
                            for a, w in ((0, 512), (512, DIM + 1 - 512)):
                                last = nc.tensor.matmul(banks(2 * (j % 4), 1024)[:, a:a + w], pr[:, k, j * P:(j + 1) * P],
                                                        hB[:, k, a:a + w], start=(k == 0), stop=(k == NT - 1))
                        last.then_inc(s_mm2, 1)

        with ExitStack() as st:
            sb = holder(st)
            hR = sb("hR", [P, NT, DIM])
            wr = sb("wr", [P, KD, DIM])
            hT = sb("hT", [P, 2, KD, P])
            brow = sb("brow", [P, DIM])
            stats2 = sb("stats2", [P, NT, 2, 6])
            mv2 = sb("mv2", [P, NT, 2])
            rstd2 = sb("rstd2", [P, NT])
            nmr2 = sb("nmr2", [P, NT])
            s_wr, s_br, s_mvb, s_sdb, s_lnb, s_hb, s_ho = (sem(n) for n in (
                "wroot_in", "brgcn_in", "ln2_stats", "ln2_sd", "ln2_scale", "h_ready", "h_out"))
            pj3 = Projection("wroot", KD, [512, 256])

            with nc.Block() as block:
                @block.sync
                def _(sp):
                    sp.dma_start(wr[:, :, :], Wroot.rearrange("(k p) o -> p k o", p=P)).then_inc(s_wr, 16)
                    sp.dma_start(brow[:, :], vector_row(brg, DIM)).then_inc(s_br, 16)
                    for j in range(NT):
                        sp.wait_ge(s_hb, j + 1)
                        sp.dma_start(h_dram[j * P:(j + 1) * P, :], hR[:, j, :]).then_inc(s_ho, 16)
                    sp.wait_ge(s_ho, 16 * NT)

                @block.scalar
                def _(act):
                    act.wait_ge(s_mvb, 1)
                    nc.scalar.activation(rstd2[:, :], mv2[:, :, 1], ACT.Sqrt, bias=eps_ln[:, :]).then_inc(s_sdb, 1)
                    act.wait_ge(s_lnb, 1)
                    for j in range(NT):
                        nc.scalar.activation(hR[:, j, :], x2[:, j, :], ACT.Relu, bias=nmr2[:, j:j + 1],
                                             scale=rstd2[:, j:j + 1]).then_inc(s_hb, 1)
                    project_act(act, pj3, hT)

                @block.vector
                def _(dve):
                    v = nc.vector
                    link = chain(dve)
                    for j in range(NT):
                        for c in range(2):
                            last = v.bn_stats(stats2[:, j, c, :], x2[:, j, c * 384:(c + 1) * 384])
                    link(last)
                    for j in range(NT):
                        last = v.bn_aggr(mv2[:, j, :], stats2[:, j, :, :].rearrange("p a b -> p (a b)"))
                    last.then_inc(s_mvb, 1)
                    dve.wait_ge(s_sdb, 1)
                    link(v.reciprocal(rstd2[:, :], rstd2[:, :]))
                    dve.wait_ge(s_mvb, 1)
                    v.scalar_tensor_tensor(nmr2[:, :], mv2[:, :, 0], -1.0, rstd2[:, :], ALU.mult, ALU.mult).then_inc(s_lnb, 1)
                    dve.wait_ge(s_br, 16)
                    for j in range(NT):
                        dve.wait_ge(pj3.multiplied, j + 1)
                        v.tensor_tensor(acc[:, j, :], banks(2 + 3 * (j % 2), DIM), brow[:, :], ALU.add).then_inc(pj3.taken, 1)

                @block.tensor
                def _(pe):
                    pe.wait_ge(s_wr, 16)
                    project_pe(pe, pj3, lambda j: hR[:, j, :], (s_hb, lambda j: j + 1), hT, wr)

        with ExitStack() as st:
            sb = holder(st)
            wrel = sb("wrel", [P, 2, KD, DIM])
            gx = sb("gx", [P, 2, DIM])
            gT = sb("gT", [P, 2, KD, P])
            mo = sb("mo", [P, 2, DIM])
            gidx = sb("gidx", [P, 2, 1], i32)
            s_w, s_idx, s_tn, s_tm, s_mt, s_mo = (sem(n) for n in (
                "wrel_in", "src_staged", "edges_turned", "edges_moved", "messages_done", "messages_moved"))
            s_gx = [sem(f"edges_in{u}") for u in range(2)]
            s_ms = [sem(f"messages_stored{u}") for u in range(2)]
            TL = REL_TILES

            with nc.Block() as block:
                @block.sync
                def _(sp):
                    wv = Wrel.rearrange("r (k p) o -> p r k o", p=P)
                    for r in range(2):
                        sp.dma_start(wrel[:, r, :, :], wv[:, r, :, :]).then_inc(s_w, 16)
                        if r == 0:
                            sp.wait_ge(s_w, 16)
                    with sp.Fori(0, RELATIONS // 2 - 1) as i:
                        for g in range(2):
                            end = sp.value_load(rel_end[0:1, ds(i * 2 + g, 1)], min_val=1, max_val=TL)
                            sp.wait_ge(s_w, i * 32 + (16 * g + 32))
                            sp.sem_inc(s_go_sp, 1)
                            sp.wait_ge(s_mt, end + 2)
                            sp.sem_inc(s_go_sp, 1)
                            sp.dma_start(wrel[:, g, :, :], wv[:, ds(i * 2 + (g + 2), 1), :, :].rearrange("p o k n -> p (o k) n")).then_inc(s_w, 16)
                    sp.wait_ge(s_w, 16 * RELATIONS)

                @block.gpsimd
                def _(pool):
                    with pool.Fori(0, TL // 2) as i:
                        for u in range(2):
                            t = i * 2 + u
                            pool.wait_ge(s_tn, t + 1)
                            nc.gpsimd.tensor_copy(gidx[:, u, :], rtab[:, ds(t, 1)]).then_inc(s_idx, 1)
                            pool.wait_ge(s_idx, t + 1)
                            pool.sem_inc(s_go, 1)
                            pool.indirect_dma_start(gx[:, u, :], None, h_dram,
                                                    bass.IndirectOffsetOnAxis(gidx[:, u, :], 0)).then_inc(s_gx[u], 16)

                @block.scalar
                def _(act):
                    mv_ = msg_dram.rearrange("(t p) o -> t p o", p=P)

                    def move(t, u):
                        act.wait_ge(s_tn, t + 3)
                        act.wait_ge(s_mt, t + 1)
                        nc.scalar.copy(gT[:, u, :, :].rearrange("p k n -> p (k n)"), banks(6 * u, DIM)).then_inc(s_tm, 1)

                    def store(t, u):
                        act.wait_ge(s_mo, t + 3)
                        act.dma_start(mv_[ds(t, 1), :, :].rearrange("o p n -> (o p) n"), mo[:, u, :]).then_inc(s_ms[u], 16)

                    move(0, 0)
                    with act.Fori(0, TL // 2 - 1) as i:
                        for u in range(2):
                            move(i * 2 + (u + 1), (u + 1) % 2)
                            store(i * 2 + u, u)
                    move(TL - 1, 1)
                    store(TL - 2, 0)
                    store(TL - 1, 1)
                    for u in range(2):
                        act.wait_ge(s_ms[u], 8 * TL)

                @block.vector
                def _(dve):
                    def take(t, u):
                        dve.wait_ge(s_mt, t + 3)
                        nc.vector.tensor_copy(mo[:, u, :], banks(2 + 2 * u, DIM)).then_inc(s_mo, 1)

                    for u in range(2):
                        take(u, u)
                    with dve.Fori(1, TL // 2) as i:
                        for u in range(2):
                            dve.wait_ge(s_ms[u], i * 16)
                            take(i * 2 + u, u)

                @block.tensor
                def _(pe):
                    for s in (s_tn, s_tm, s_mt, s_mo):
                        pe.sem_inc(s, 2)

                    def turn(t, n, u):
                        pe.wait_ge(s_gx[u], n)
                        pe.wait_ge(s_tm, t + 1)
                        for k in range(KD):
                            last = nc.tensor.transpose(banks(6 * u, DIM)[:, k * P:(k + 1) * P], gx[:, u, k * P:(k + 1) * P], ident[:, :])
                        last.then_inc(s_tn, 1)

                    def multiply(t, u):
                        r = pe.value_load(tile_rel[0:1, ds(t, 1)], min_val=0, max_val=RELATIONS - 1)
                        pe.wait_ge(s_w, r * 16 + 16)
                        slot = pe.snap(r % 2)
                        pe.wait_ge(s_tm, t + 3)
                        pe.wait_ge(s_mo, t + 1)
                        for k in range(KD):
                            for a, w in ((0, 512), (512, 256)):
                                last = nc.tensor.matmul(banks(2 + 2 * u, DIM)[:, a:a + w], gT[:, u, k, :],
                                                        wrel[:, ds(slot, 1), k, a:a + w].rearrange("p o n -> p (o n)"),
                                                        start=(k == 0), stop=(k == KD - 1))
                        last.then_inc(s_mt, 1)

                    turn(0, 16, 0)
                    with pe.Fori(0, TL // 2 - 1) as i:
                        turn(i * 2 + 1, i * 16 + 16, 1)
                        multiply(i * 2, 0)
                        turn(i * 2 + 2, i * 16 + 32, 0)
                        multiply(i * 2 + 1, 1)
                    turn(TL - 1, 8 * TL, 1)
                    multiply(TL - 2, 0)
                    multiply(TL - 1, 1)

        with ExitStack() as st:
            sb = holder(st)
            RING = 2 * GT
            mg = sb("mg", [P, RING, DIM])
            hotw = sb("hotw", [P, RING, P])
            midx = sb("midx", [P, RING, 1], i32)
            s_mg = [sem(f"messages_in{u}") for u in range(RING)]
            s_ix, s_hw, s_us, s_ad = (sem(n) for n in ("slots_staged", "hotw_ready", "messages_used", "sum_added"))

            with nc.Block() as block:
                @block.gpsimd
                def _(pool):
                    with pool.Fori(0, GROUPS // 2) as i:
                        for u in range(RING):
                            t = i * RING + u
                            pool.wait_ge(s_us, t + 1)
                            nc.gpsimd.tensor_copy(midx[:, u, :], etab[:, ds(t, 1), F_SLOT:F_SLOT + 1].rearrange("p o f -> p (o f)")).then_inc(s_ix, 1)
                            pool.wait_ge(s_ix, t + 1)
                            pool.sem_inc(s_go, 1)
                            pool.indirect_dma_start(mg[:, u, :], None, msg_dram,
                                                    bass.IndirectOffsetOnAxis(midx[:, u, :], 0)).then_inc(s_mg[u], 16)

                @block.vector
                def _(dve):
                    v = nc.vector
                    with dve.Fori(0, GROUPS // 2) as i:
                        for u in range(RING):
                            t = i * RING + u
                            dve.wait_ge(s_us, t + 1)
                            v.tensor_scalar(hotw[:, u, :], iota[:, 0:P], etab[:, ds(t, 1), F_DLOC:F_DLOC + 1].rearrange("p o f -> p (o f)"),
                                            weight[:, ds(t + 4, 1)], ALU.is_equal, ALU.mult).then_inc(s_hw, 1)
                        for g in range(2):
                            at = dve.value_load(group_tile[0:1, ds(i * 2 + g, 1)], min_val=0, max_val=NT - 1)
                            dve.wait_ge(s_us, i * RING + (GT * (g + 1) + RING))
                            a = acc[:, ds(at, 1), :].rearrange("p o c -> p (o c)")
                            v.tensor_tensor(a, a, banks(2 * g, DIM), ALU.add).then_inc(s_ad, 1)
                            dve.wait_ge(s_ad, i * 2 + (g + 3))

                @block.tensor
                def _(pe):
                    pe.sem_inc(s_us, RING)
                    pe.sem_inc(s_ad, 2)
                    with pe.Fori(0, GROUPS // 2) as i:
                        for g in range(2):
                            pe.wait_ge(s_ad, i * 2 + (g + 1))
                            for q in range(GT):
                                u = g * GT + q
                                pe.wait_ge(s_hw, i * RING + (u + 1))
                                pe.wait_ge(s_mg[u], i * 16 + 16)
                                for a, w in ((0, 512), (512, 256)):
                                    last = nc.tensor.matmul(banks(2 * g, DIM)[:, a:a + w], hotw[:, u, :], mg[:, u, a:a + w],
                                                            start=(q == 0), stop=(q == GT - 1))
                                last.then_inc(s_us, 1)

        with ExitStack() as st:
            sb = holder(st)
            wg = sb("wg", [P, KD, DIM])
            cT = sb("cT", [P, 2, KD, P])
            Y = sb("Y", [P, NT, DIM])
            bgrow = sb("bgrow", [P, DIM])
            s_wg, s_bg, s_acc, s_self, s_res, s_ys, s_fm, s_fo, s_st = (sem(n) for n in (
                "wgcn_in", "bgcn_in", "h1_ready", "self_edges", "residual", "scaled", "sums_done", "rows_ready", "out_stored"))
            pj4 = Projection("wgcn", KD, [512, 256])

            with nc.Block() as block:
                @block.sync
                def _(sp):
                    sp.dma_start(wg[:, :, :], Wgcn.rearrange("(k p) o -> p k o", p=P)).then_inc(s_wg, 16)
                    sp.dma_start(bgrow[:, :], vector_row(bgcn, DIM)).then_inc(s_bg, 16)
                    for j in range(NT):
                        n = P if j < NT - 1 else LAST
                        sp.wait_ge(s_fo, j + 1)
                        sp.dma_start(out[j * P:j * P + n, :], x2[:n, j, :]).then_inc(s_st, 16)
                    sp.wait_ge(s_st, 16 * NT)

                @block.scalar
                def _(act):
                    project_act(act, pj4, cT)

                @block.vector
                def _(dve):
                    v = nc.vector
                    for k in range(NT):
                        v.tensor_tensor(CT[:, k, k * P:(k + 1) * P], CT[:, k, k * P:(k + 1) * P], ident[:, :], ALU.add).then_inc(s_self, 1)
                    dve.wait_ge(s_bg, 16)
                    for j in range(NT):
                        v.tensor_tensor(x2[:, j, :], x2[:, j, :], bgrow[:, :], ALU.add).then_inc(s_res, 1)
                    for j in range(NT):
                        dve.wait_ge(pj4.multiplied, j + 1)
                        v.tensor_scalar(Y[:, j, :], banks(2 + 3 * (j % 2), DIM), dinv[:, j:j + 1], None, ALU.mult).then_inc(pj4.taken, 1)
                    dve.wait_ge(s_res, NT)
                    for j in range(NT):
                        dve.wait_ge(s_fm, j + 1)
                        v.scalar_tensor_tensor(x2[:, j, :], banks(2 * (j % 4), DIM), dinv[:, j:j + 1], x2[:, j, :], ALU.mult, ALU.add).then_inc(s_fo, 1)

                @block.tensor
                def _(pe):
                    pe.wait_ge(s_wg, 16)
                    pe.sem_inc(s_acc, 1)
                    project_pe(pe, pj4, lambda j: acc[:, j, :], (s_acc, lambda j: 1), cT, wg)
                    pe.wait_ge(s_self, NT)
                    pe.wait_ge(pj4.taken, NT)
                    for j in range(NT):
                        if j >= 4:
                            pe.wait_ge(s_fo, j - 3)
                        for k in range(NT):
                            for a, w in ((0, 512), (512, 256)):
                                last = nc.tensor.matmul(banks(2 * (j % 4), DIM)[:, a:a + w], CT[:, k, j * P:(j + 1) * P],
                                                        Y[:, k, a:a + w], start=(k == 0), stop=(k == NT - 1))
                        last.then_inc(s_fm, 1)


_INS = ['x', 'src', 'dst', 'edge_type_34', 'L0_gnn_W1', 'L0_gnn_att_src1', 'L0_gnn_att_dst1', 'L0_gnn_b1',
        'L0_gnn_W2', 'L0_gnn_att_src2', 'L0_gnn_att_dst2', 'L0_gnn_b2', 'L1_gnn_W_rel', 'L1_gnn_W_root',
        'L1_gnn_b_rgcn', 'L1_gnn_W_gcn', 'L1_gnn_b_gcn']


def kernel(**inputs):
    import numpy as _np
    import concourse.bacc as _bacc
    from concourse import mybir as _mybir
    from concourse.bass_utils import run_bass_kernel_spmd as _run

    nc = _bacc.Bacc("TRN2", target_bir_lowering=False, num_devices=1)
    arrays, args = {}, []
    for name in _INS:
        a = _np.ascontiguousarray(inputs[name])
        arrays[f"in_{name}_dram"] = a
        args.append(nc.dram_tensor(f"in_{name}_dram", a.shape, _mybir.dt.from_np(a.dtype), kind="ExternalInput").ap())
    args.append(nc.dram_tensor("out_0_dram", (NODES, DIM), _mybir.dt.float32, kind="ExternalOutput").ap())
    gnn_kernel(nc, *args)
    r = _run(nc, [arrays], core_ids=[0])
    return r.results[0]["out_0_dram"]
```

```python
import concourse.bass as bass
from concourse import mybir
from contextlib import ExitStack


P = 128
NODES = 1250
DIM = 768
EDGES = 20000
HEADS, HEAD_DIM = 8, 128
RELATIONS = 34
NEG_SLOPE = 0.2
SOFTMAX_EPS = 1e-16
LN_EPS = 1e-5
NEGATIVE = -1e30
BIG = 3e38

NT = -(-NODES // P)
LAST = NODES - (NT - 1) * P
NP = NT * P
KD = DIM // P
HID = HEADS * HEAD_DIM
KH = HID // P
HCOLS = HEAD_DIM + 1

EP, EC = 125, EDGES // 125
REL_TILES = (EDGES - RELATIONS) // P + 1 + RELATIONS
REL_TILES += REL_TILES % 2
REL_ROOM = REL_TILES + NT
SB = 8
GT = 4
GROUPS = (EDGES - NT) // (GT * P) + 1 + NT
GROUPS += -GROUPS % 4
DST_TILES = GROUPS * GT
F_SRC, F_DLOC, F_REL, F_DREL, FIELDS = 0, 1, 2, 3, 4
TABLE_COLS = -(-REL_TILES // P)
CC = NP + RELATIONS


def gnn_kernel(nc, x, src, dst, etype, W1, as1, ad1, b1, W2, as2, ad2, b2,
               Wrel, Wroot, brg, Wgcn, bgcn, out):
    f32, bf16, i32, i16 = mybir.dt.float32, mybir.dt.bfloat16, mybir.dt.int32, mybir.dt.int16
    f32r = mybir.dt.float32r
    ALU, ACT, AX = mybir.AluOpType, mybir.ActivationFunctionType, mybir.AxisListType
    ds = bass.ds

    def dram(name, shape, dt=f32):
        return nc.dram_tensor(name, shape, dt, kind="Internal").ap()

    dst_table = dram("dst_table", (DST_TILES * P, FIELDS))
    slot_table = dram("slot_table", (NP * RELATIONS, 1))
    uv_rows = dram("uv_rows", (2 * HEADS * NT, P))
    m_rows = dram("m_rows", (HEADS * NT, P))
    uv2_rows = dram("uv2_rows", (2 * NT, P))
    m2_rows = dram("m2_rows", (NT, P))
    inv_count = dram("inv_count", (NP * RELATIONS, 1))
    h1_dram = dram("h1_dram", (NP, HID))
    h_dram = dram("h_dram", (NP, DIM))
    ct_dram = dram("ct_dram", (P, NT * NP))
    msg_dram = dram("msg_dram", (REL_TILES * P, DIM))

    def row_of(rows, r):
        return rows[r * NT:(r + 1) * NT, :].rearrange("(o a) b -> o (a b)", o=1).to_broadcast([P, NP])

    def vector_row(v, n):
        return v.rearrange("(o n) -> o n", o=1).to_broadcast([P, n])

    top = ExitStack()
    with top:
        def holder(stack):
            def sb(name, shape, dt=f32):
                return stack.enter_context(nc.sbuf_tensor(name, shape, dt))
            return sb

        def sem(name):
            return top.enter_context(nc.semaphore(name))

        keep = holder(top)
        PS = top.enter_context(nc.psum_tensor("PS", [P, 8, 512], f32))
        PSf = PS[:, :, :].rearrange("p b n -> p (b n)")

        def banks(b, n):
            return PSf[:, b * 512:b * 512 + n]

        iota = keep("iota", [P, P])
        iota16 = keep("iota16", [P, NP], i16)
        pidx = keep("pidx", [P, 1])
        ident = keep("ident", [P, P])
        tri = keep("tri", [P, P])
        ones = keep("ones", [P, P])
        eps_ln = keep("eps_ln", [P, 1])
        region_x = keep("region_x", [P, NT * DIM])
        region_h = keep("region_h", [P, NT * HEADS * HCOLS])
        dinv = keep("dinv", [P, NT])
        etab = keep("etab", [P, DST_TILES, FIELDS])
        rtab = keep("rtab", [P, REL_ROOM])
        pair_tile = keep("pair_tile", [P, NT, RELATIONS], bf16)
        pair_place = keep("pair_place", [P, NT, RELATIONS], bf16)
        rel_base = keep("rel_base", [1, RELATIONS], i32)
        slot_flat = keep("slot_flat", [P, DST_TILES])
        slot_of = keep("slot_of", [P, DST_TILES], i32)
        tile_rel = keep("tile_rel", [1, REL_TILES], i32)
        next_rel = keep("next_rel", [1, REL_TILES], i32)
        n_rel_tiles = keep("n_rel_tiles", [1, 1], i32)
        n_groups = keep("n_groups", [1, 1], i32)
        group_tile = keep("group_tile", [1, GROUPS], i32)
        pos_dst = keep("pos_dst", [P, EC], i32)
        weight = keep("weight", [P, DST_TILES])
        uv = keep("uv", [P, 2 * HEADS, NT])
        uv2 = keep("uv2", [P, 2, NT])
        x_sb = region_x[:, :].rearrange("p (j i) -> p j i", i=DIM)
        x2 = x_sb
        mask = region_x[:, 0:NT * NP // 2].bitcast(bf16).rearrange("p (j s) -> p j s", s=NP)
        hA = region_h[:, :].rearrange("p (j h c) -> p j h c", h=HEADS, c=HCOLS)
        hB = region_h[:, 0:NT * (DIM + 1)].rearrange("p (j c) -> p j c", c=DIM + 1)
        acc = region_h[:, 0:NT * DIM].rearrange("p (j c) -> p j c", c=DIM)

        s_chain, links = sem("dve_chain"), [0]

        def chain(dve):
            def link(ins):
                links[0] += 1
                ins.then_inc(s_chain, 1)
                dve.wait_ge(s_chain, links[0])
            return link

        s_go = sem("gather_go")

        s_go_sp = sem("sync_go")

        s_moved, moves = sem("sync_dma_done"), [0]

        def all_moved(sp, n):
            moves[0] += n
            sp.wait_ge(s_moved, 16 * moves[0])

        def scatter_all(pool, table, rows, slots, stage_row, stage_idx, done, staged):
            def send(c, half):
                nc.gpsimd.tensor_copy(stage_row[:EP, half, :, :], rows[:EP, ds(c * SB, SB), :])
                nc.gpsimd.tensor_copy(stage_idx[:EP, half, :], slots[:EP, ds(c * SB, SB)]).then_inc(staged, 1)
                pool.wait_ge(staged, c + 1)
                pool.sem_inc(s_go, 1)
                for u in range(SB):
                    pool.indirect_dma_start(table, bass.IndirectOffsetOnAxis(stage_idx[:EP, half, u:u + 1], 0),
                                            stage_row[:EP, half, u, :], None).then_inc(done[half], 16)

            for half in range(2):
                send(half, half)
            with pool.Fori(1, EC // SB // 2) as i:
                for half in range(2):
                    pool.wait_ge(done[half], i * (16 * SB))
                    pool.sem_inc(s_go, 1)
                    send(i * 2 + half, half)
            for half in range(2):
                pool.wait_ge(done[half], EC * 8)

        def walk_columns(pool, groups, issue, collect, done):
            for half in range(2):
                issue(half, half)
            with pool.Fori(1, GROUPS // 4) as i:
                with pool.If(i * 4 < groups):
                    for half in range(2):
                        pool.wait_ge(done[half], i * (16 * SB))
                        pool.sem_inc(s_go, 1)
                        collect(i * 2 + (half - 2), half)
                        issue(i * 2 + half, half)
            steps = pool.snap((groups + 3) // 4)
            for half in range(2):
                pool.wait_ge(done[half], steps * (16 * SB))
                pool.sem_inc(s_go, 1)
                collect(steps * 2 + (half - 2), half)

        class Projection:
            def __init__(self, tag, k, widths):
                self.k, self.widths = k, widths
                self.turned = sem(tag + "_tile_turned")
                self.moved = sem(tag + "_tile_moved")
                self.multiplied = sem(tag + "_tile_multiplied")
                self.taken = sem(tag + "_tile_taken")

        def project_pe(pe, pj, source, input_ready, xT, rhs, beside=None):
            def turn(j):
                ready = input_ready[0]
                pe.wait_ge(ready[j % 2] if isinstance(ready, list) else ready, input_ready[1](j))
                if j:
                    pe.wait_ge(pj.moved, j)
                for k in range(pj.k):
                    last = nc.tensor.transpose(banks(0, 1024)[:, k * P:(k + 1) * P],
                                               source(j)[:, k * P:(k + 1) * P], ident[:, :])
                last.then_inc(pj.turned, 1)

            turn(0)
            for j in range(NT):
                if j + 1 < NT:
                    turn(j + 1)
                pe.wait_ge(pj.moved, j + 1)
                if j >= 2:
                    pe.wait_ge(pj.taken, j - 1)
                for k in range(pj.k):
                    at = 0
                    for w in pj.widths:
                        last = nc.tensor.matmul(banks(2 + 3 * (j % 2), 1536)[:, at:at + w],
                                                xT[:, j % 2, k, :], rhs[:, k, at:at + w],
                                                start=(k == 0), stop=(k == pj.k - 1))
                        at += w
                last.then_inc(pj.multiplied, 1)
                if beside is not None:
                    beside(j)

        def project_act(act, pj, xT, move=None):
            for j in range(NT):
                act.wait_ge(pj.turned, j + 1)
                if j >= 2:
                    act.wait_ge(pj.multiplied, j - 1)
                if move is None:
                    nc.scalar.copy(xT[:, j % 2, 0:pj.k, :].rearrange("p k n -> p (k n)"),
                                   banks(0, pj.k * P)).then_inc(pj.moved, 1)
                else:
                    move(j).then_inc(pj.moved, 1)

        with ExitStack() as st:
            sb = holder(st)
            w1 = sb("w1", [P, HEADS, DIM])
            attc = sb("attc", [P, HEADS, 2])
            w1T = sb("w1T", [P, KD, HID + 2 * HEADS])
            h0T = sb("h0T", [P, 2, KD, P])
            stats = sb("stats", [P, NT, 2, 6])
            mv = sb("mv", [P, NT, 2])
            rstd = sb("rstd", [P, NT])
            nmr = sb("nmr", [P, NT])
            rows_sb = sb("rows_sb", [80, 2, P])

            s_const, s_ids, s_x, s_w1, s_att = (sem(n) for n in
                                                ("const", "ids", "x_in", "w1_in", "att_in"))
            s_w1t, s_w1e, s_wa, s_mv, s_sd, s_ln, s_h0 = (sem(n) for n in (
                "w1_turned", "w1_moved", "att_folded", "ln_stats", "ln_sd", "ln_scale", "h0"))
            s_tot, s_pref, s_tabs, s_pad_rows = (sem(n) for n in
                                             ("bucket_tot", "bucket_prefix", "tables_blank", "pad_rows"))
            s_pos, s_stage = (sem(n) for n in ("edge_pos", "edge_staged"))
            s_scat = [sem(f"dst_scattered{u}") for u in range(2)]
            s_uvT, s_uve, s_pad = (sem(n) for n in ("uv_turned", "uv_moved", "x_pad"))
            pj = Projection("w1", KD, [512, 512, 2 * HEADS])

            with ExitStack() as st2:
                sb2 = holder(st2)
                ids = sb2("ids", [P, 3, EC], i32)
                cut = sb2("cut", [P, 2, EC], i32)
                keyd = sb2("keyd", [P, EC])
                keyx = sb2("keyx", [P, EC])
                edge0 = sb2("edge0", [P, 3], i32)
                pad_row = sb2("pad_row", [P, FIELDS])
                fields = sb2("fields", [P, EC, FIELDS])
                hot = sb2("hot", [P, NT, EC])
                run = sb2("run", [P, NT, EC])
                before = sb2("before", [P, NT])
                tot = sb2("tot", [P, NT])
                tiles = sb2("tiles", [P, NT])
                tilesi = sb2("tilesi", [P, NT], i32)
                base = sb2("base", [P, NT])
                off = sb2("off", [P, NT])
                cmpr = sb2("cmpr", [1, GROUPS])
                cmps = sb2("cmps", [1, GROUPS, NT])
                blank = sb2("blank", [P, DST_TILES, FIELDS])
                stage_row = sb2("stage_row", [P, 2, SB, FIELDS])
                stage_idx = sb2("stage_idx", [P, 2, SB], i32)

                with nc.Block() as block:
                    @block.sync
                    def _(sp):
                        for n, v in enumerate((src, dst, etype)):
                            sp.dma_start(ids[:EP, n, :], v.rearrange("(p c) -> p c", c=EC)).then_inc(s_ids, 16)
                        for n, v in enumerate((src, dst, etype)):
                            sp.dma_start(edge0[:, n:n + 1], v[0:1].rearrange("(o n) -> o n", o=1).to_broadcast([P, 1])).then_inc(s_ids, 16)
                        sp.dma_start(w1[:, :, :], W1.rearrange("(h c) i -> c h i", c=P)).then_inc(s_w1, 16)
                        with nc.allow_non_contiguous_dma(reason="attention vectors as columns"):
                            sp.dma_start(attc[:, :, 0], as1.rearrange("h c -> c h")).then_inc(s_att, 16)
                            sp.dma_start(attc[:, :, 1], ad1.rearrange("h c -> c h")).then_inc(s_att, 16)
                        sp.dma_start(x_sb[:, 0:NT - 1, :], x[0:(NT - 1) * P, :].rearrange("(j p) i -> p j i", p=P)).then_inc(s_x, 16)
                        sp.wait_ge(s_pad, 1)
                        sp.dma_start(x_sb[:LAST, NT - 1, :], x[(NT - 1) * P:NODES, :]).then_inc(s_x, 16)
                        sp.wait_ge(s_uve, 2)
                        for c in range(2):
                            sp.dma_start(uv_rows[80 * c:80 * c + 80, :], rows_sb[:, c, :]).then_inc(s_moved, 16)
                        all_moved(sp, 2)

                    @block.gpsimd
                    def _(pool):
                        pool.memset(x_sb[:, NT - 1, :], 0.0).then_inc(s_pad, 1)
                        pool.iota(iota16[:, :], [[1, NP]], base=0, channel_multiplier=0).then_inc(s_const, 1)
                        pool.iota(iota[:, :], [[1, P]], base=0, channel_multiplier=0,
                                  allow_small_or_imprecise_dtypes=True).then_inc(s_const, 1)
                        pool.iota(pidx[:, :], [[1, 1]], base=0, channel_multiplier=1,
                                  allow_small_or_imprecise_dtypes=True).then_inc(s_const, 1)
                        pool.wait_ge(s_pad_rows, 1)
                        pool.dma_start(dst_table.rearrange("(p a) f -> p (a f)", p=P),
                                       blank[:, :, :].rearrange("p a f -> p (a f)")).then_inc(s_tabs, 16)
                        pool.wait_ge(s_tabs, 16)
                        pool.wait_ge(s_pos, 1)
                        scatter_all(pool, dst_table, fields, pos_dst, stage_row, stage_idx, s_scat, s_stage)

                    @block.scalar
                    def _(act):
                        act.wait_ge(s_const, 3)
                        act.wait_ge(s_w1, 16)
                        for g in range(2 * KD):
                            act.wait_ge(s_w1t, g + 1)
                            nc.scalar.copy(w1T[:, g // 2, 512 * (g % 2):512 * (g % 2) + 512],
                                           banks(g % 2, 512)).then_inc(s_w1e, 1)
                        act.wait_ge(s_wa, 1)
                        nc.scalar.copy(w1T[:, :, HID:], banks(2, 16 * KD).rearrange("p (k c) -> p k c", k=KD)).then_inc(s_w1e, 1)
                        act.wait_ge(s_mv, 1)
                        nc.scalar.activation(rstd[:, :], mv[:, :, 1], ACT.Sqrt, bias=eps_ln[:, :]).then_inc(s_sd, 1)
                        act.wait_ge(s_ln, 1)
                        for j in range(NT):
                            nc.scalar.activation(x_sb[:, j, :], x_sb[:, j, :], ACT.Relu, bias=nmr[:, j:j + 1],
                                                 scale=rstd[:, j:j + 1]).then_inc(s_h0, 1)
                        project_act(act, pj, h0T)
                        for c in range(2):
                            act.wait_ge(s_uvT, c + 1)
                            nc.scalar.copy(rows_sb[:, c, :], banks(c, P)[:80, :]).then_inc(s_uve, 1)

                    @block.vector
                    def _(dve):
                        link = chain(dve)
                        v = nc.vector
                        v.memset(eps_ln[:, :], LN_EPS)
                        v.memset(hA[:, :, :, HEAD_DIM:], 1.0)
                        link(v.memset(ones[:, :], 1.0))
                        dve.wait_ge(s_const, 3)
                        v.tensor_scalar(tri[:, :], iota[:, 0:P], pidx[:, :], None, ALU.is_gt)
                        v.tensor_scalar(ident[:, :], iota[:, 0:P], pidx[:, :], None, ALU.is_equal).then_inc(s_const, 1)
                        dve.wait_ge(s_ids, 96)
                        v.tensor_single_scalar(cut[:EP, 0, :], ids[:EP, 1, :], 7, ALU.arith_shift_right)
                        link(v.tensor_single_scalar(cut[:EP, 1, :], ids[:EP, 1, :], P - 1, ALU.bitwise_and))
                        v.tensor_copy(keyd[:EP, :], cut[:EP, 0, :])
                        v.tensor_copy(fields[:EP, :, F_SRC], ids[:EP, 0, :])
                        v.tensor_copy(fields[:EP, :, F_DLOC], cut[:EP, 1, :])
                        v.tensor_copy(fields[:EP, :, F_REL], ids[:EP, 2, :])
                        v.tensor_copy(pad_row[:, F_SRC:F_SRC + 1], edge0[:, 0:1])
                        v.tensor_copy(pad_row[:, F_REL:F_REL + 1], edge0[:, 2:3])
                        v.tensor_copy(fields[:EP, :, F_DREL], ids[:EP, 1, :])
                        v.tensor_copy(pad_row[:, F_DREL:], edge0[:, 1:2])
                        link(v.memset(pad_row[:, F_DLOC:F_DLOC + 1], -1.0))
                        v.scalar_tensor_tensor(fields[:EP, :, F_DREL], fields[:EP, :, F_DREL], float(RELATIONS),
                                               fields[:EP, :, F_REL], ALU.mult, ALU.add)
                        link(v.scalar_tensor_tensor(pad_row[:, F_DREL:], pad_row[:, F_DREL:], float(RELATIONS),
                                                    pad_row[:, F_REL:F_REL + 1], ALU.mult, ALU.add))
                        v.tensor_copy(blank[:, :, :], pad_row[:, :].unsqueeze(1).to_broadcast([P, DST_TILES, FIELDS])).then_inc(s_pad_rows, 1)

                        def places(key, nb, unit_shift, pos):
                            h, r = hot[:EP, 0:nb, :], run[:EP, 0:nb, :]
                            link(v.tensor_tensor(h, key[:EP, :].unsqueeze(1).to_broadcast([EP, nb, EC]),
                                                 iota[:EP, 0:nb].unsqueeze(2).to_broadcast([EP, nb, EC]), ALU.is_equal))
                            hf, rf = h.rearrange("p b c -> p (b c)"), r.rearrange("p b c -> p (b c)")
                            link(v.tensor_tensor_scan(rf, hf, hf, 0.0, ALU.add, ALU.max))
                            link(v.memset(before[:EP, 0:1], 0.0))
                            link(v.tensor_copy(before[:EP, 1:nb], r[:, 0:nb - 1, EC - 1]))
                            v.tensor_tensor(tot[:EP, 0:nb], r[:, :, EC - 1], before[:EP, 0:nb], ALU.subtract).then_inc(s_tot, 1)
                            dve.wait_ge(s_pref, 1)
                            b = 3
                            link(v.tensor_scalar(tiles[:, 0:nb], banks(b, 128)[:, 64:64 + nb], float(2 ** unit_shift - 1), None, ALU.add))
                            link(v.tensor_copy(tilesi[:, 0:nb], tiles[:, 0:nb]))
                            link(v.tensor_single_scalar(tilesi[:, 0:nb], tilesi[:, 0:nb], unit_shift, ALU.arith_shift_right))
                            link(v.tensor_copy(tiles[:, 0:nb], tilesi[:, 0:nb]))
                            link(v.tensor_tensor_scan(base[:, 0:nb], tiles[:, 0:nb], tiles[:, 0:nb], 0.0, ALU.add, ALU.max))
                            link(v.tensor_tensor(base[:, 0:nb], base[:, 0:nb], tiles[:, 0:nb], ALU.subtract))
                            link(v.scalar_tensor_tensor(off[:EP, 0:nb], base[:EP, 0:nb], float(2 ** unit_shift),
                                                        banks(b, 64)[:EP, 0:nb], ALU.mult, ALU.add))
                            link(v.scalar_tensor_tensor(off[:EP, 0:nb], off[:EP, 0:nb], -1.0, before[:EP, 0:nb],
                                                        ALU.add, ALU.subtract))
                            link(v.tensor_tensor(r, r, off[:EP, 0:nb].unsqueeze(2).to_broadcast([EP, nb, EC]), ALU.add))
                            link(v.tensor_tensor(h, h, r, ALU.mult))
                            link(v.tensor_reduce(keyx[:EP, :], h.rearrange("p b c -> p c b"), AX.X, ALU.add))
                            link(v.tensor_copy(pos, keyx[:EP, :]))

                        def group_of(units, nb, result):
                            c = cmps[:, :, :]
                            link(v.tensor_tensor(c, base[0:1, 0:nb].unsqueeze(1).to_broadcast([1, units, nb]),
                                                 iota[0:1, 0:units].unsqueeze(2).to_broadcast([1, units, nb]), ALU.is_le))
                            link(v.tensor_reduce(cmpr[0:1, 0:units], c, AX.X, ALU.add))
                            link(v.tensor_scalar(cmpr[0:1, 0:units], cmpr[0:1, 0:units], -1.0, None, ALU.add))
                            link(v.tensor_copy(result, cmpr[0:1, 0:units]))

                        places(keyd, NT, 9, pos_dst[:EP, :])
                        group_of(GROUPS, NT, group_tile[:, :])
                        link(v.tensor_tensor(off[0:1, 0:NT], base[0:1, 0:NT], tiles[0:1, 0:NT], ALU.add))
                        v.tensor_copy(n_groups[:, :], off[0:1, NT - 1:NT]).then_inc(s_pos, 1)
                        dve.wait_ge(s_x, 32)
                        for j in range(NT):
                            for c in range(2):
                                last = v.bn_stats(stats[:, j, c, :], x_sb[:, j, c * 384:(c + 1) * 384])
                        link(last)
                        for j in range(NT):
                            last = v.bn_aggr(mv[:, j, :], stats[:, j, :, :].rearrange("p a b -> p (a b)"))
                        last.then_inc(s_mv, 1)
                        dve.wait_ge(s_sd, 1)
                        link(v.reciprocal(rstd[:, :], rstd[:, :]))
                        v.scalar_tensor_tensor(nmr[:, :], mv[:, :, 0], -1.0, rstd[:, :], ALU.mult, ALU.mult).then_inc(s_ln, 1)


                        for j in range(NT):
                            dve.wait_ge(pj.multiplied, j + 1)
                            v.tensor_copy(hA[:, j, :, 0:HEAD_DIM],
                                          banks(2 + 3 * (j % 2), HID).rearrange("p (h c) -> p h c", h=HEADS))
                            v.tensor_copy(uv[:, :, j], banks(2 + 3 * (j % 2), HID + 2 * HEADS)[:, HID:]).then_inc(pj.taken, 1)

                    @block.tensor
                    def _(pe):
                        pe.wait_ge(s_const, 4)
                        pe.wait_ge(s_tot, 1)
                        nc.tensor.matmul(banks(3, 64)[:EP, 0:NT], tri[:EP, :EP], tot[:EP, 0:NT], start=True, stop=True)
                        nc.tensor.matmul(banks(3, 128)[:, 64:64 + NT], ones[:EP, :], tot[:EP, 0:NT],
                                         start=True, stop=True).then_inc(s_pref, 1)
                        pe.wait_ge(s_w1, 16)
                        for g in range(2 * KD):
                            if g >= 2:
                                pe.wait_ge(s_w1e, g - 1)
                            for u in range(4):
                                h = 4 * (g % 2) + u
                                last = nc.tensor.transpose(banks(g % 2, 512)[:, u * P:(u + 1) * P],
                                                           w1[:, h, (g // 2) * P:(g // 2 + 1) * P], ident[:, :])
                            last.then_inc(s_w1t, 1)
                        pe.wait_ge(s_att, 32)
                        for k in range(KD):
                            for h in range(HEADS):
                                last = nc.tensor.matmul(banks(2, 96)[:, k * 16 + 2 * h:k * 16 + 2 * h + 2],
                                                        w1[:, h, k * P:(k + 1) * P], attc[:, h, :], start=True, stop=True)
                        last.then_inc(s_wa, 1)
                        pe.wait_ge(s_w1e, 2 * KD + 1)
                        pe.wait_ge(s_pos, 1)
                        project_pe(pe, pj, lambda j: x_sb[:, j, :], (s_h0, lambda j: j + 1), h0T, w1T)
                        pe.wait_ge(pj.taken, NT)
                        for c in range(2):
                            nc.tensor.transpose(banks(c, P)[:80, :], uv[:, :, :].rearrange("p c j -> p (c j)")[:, 80 * c:80 * c + 80],
                                                ident[:, :]).then_inc(s_uvT, 1)

        counts_life = ExitStack()
        CT = holder(counts_life)("CT", [P, NT, NP])
        with ExitStack() as st:
            sb = holder(st)
            C = sb("C", [P, NT, CC])
            with ExitStack() as st2:
                sb2 = holder(st2)
                hot_src = sb2("hot_src", [P, GT, CC], bf16)
                hot_dst = sb2("hot_dst", [P, GT, P], bf16)
                inv = sb2("inv", [P, NT, RELATIONS])
                deg = sb2("deg", [P, NT])
                zero16 = sb2("zero16", [P, NT * RELATIONS], bf16)
                present = sb2("present", [P, NT, RELATIONS])
                slots = sb2("slots", [P, NT, RELATIONS])
                in_tile = sb2("in_tile", [P, NT, RELATIONS])
                n_rel = sb2("n_rel", [P, RELATIONS])
                rtiles = sb2("rtiles", [P, RELATIONS])
                rtilesi = sb2("rtilesi", [P, RELATIONS], i32)
                rbase = sb2("rbase", [P, RELATIONS])
                pairi = region_x[:, NT * NP // 2:NT * NP // 2 + 2 * NT * RELATIONS].bitcast(i32).rearrange(
                    "p (o j r) -> p o j r", o=2, r=RELATIONS)
                started = sb2("started", [P, TABLE_COLS, RELATIONS])
                n_started = sb2("n_started", [P, TABLE_COLS])
                trel = sb2("trel", [1, REL_TILES])
                first = sb2("first", [1, REL_TILES])
                s_counts = sem("counts_done")
                s_et, s_z16, s_hot, s_used, s_add = (sem(n) for n in (
                    "etab_in", "zeros_ready", "hot_ready", "hot_used", "group_added"))
                s_inv, s_cT, s_cTe, s_deg, s_sd2 = (sem(n) for n in (
                    "inv_ready", "ct_turned", "ct_moved", "deg_ready", "deg_sqrt"))

                s_pc, s_pres, s_rpre, s_rn, s_slot, s_trel = (sem(n) for n in (
                    "pairs_counted", "pairs_present", "pairs_prefix", "rel_sizes_used", "slots_ready", "tile_rel_turned"))

                with nc.Block() as block:
                    @block.sync
                    def _(sp):
                        sp.dma_start(etab[:, :, :], dst_table.rearrange("(t p) f -> p t f", p=P)).then_inc(s_et, 16)
                        sp.wait_ge(s_inv, 1)
                        sp.dma_start(inv_count.rearrange("(j p r) o -> p j (r o)", p=P, r=RELATIONS), inv[:, :, :]).then_inc(s_moved, 16)
                        sp.wait_ge(s_slot, 1)
                        sp.dma_start(slot_table.rearrange("(j p r) o -> p j (r o)", p=P, r=RELATIONS), slots[:, :, :]).then_inc(s_moved, 16)
                        all_moved(sp, 2)

                    @block.scalar
                    def _(act):
                        act.wait_ge(s_deg, 1)
                        nc.scalar.activation(deg[:, :], deg[:, :], ACT.Sqrt).then_inc(s_sd2, 1)
                        for k in range(NT):
                            act.wait_ge(s_cT, k + 1)
                            nc.scalar.copy(CT[:, k, :], banks(3 * (k % 2), NP)).then_inc(s_cTe, 1)

                    @block.vector
                    def _(dve):
                        v = nc.vector
                        link = chain(dve)
                        v.memset(zero16[:, :], 0.0).then_inc(s_z16, 1)
                        link(v.memset(C[:, :, :].rearrange("p j c -> p (j c)"), 0.0))
                        dve.wait_ge(s_et, 16)
                        v.memset(rtab[:, :], 0.0)
                        v.scalar_tensor_tensor(slot_flat[:, :], etab[:, :, F_SRC], float(RELATIONS), etab[:, :, F_REL],
                                               ALU.mult, ALU.add)
                        groups = dve.value_load(n_groups[0:1, 0:1], min_val=0, max_val=GROUPS)
                        with dve.Fori(0, GROUPS // 2) as i:
                            with dve.If(i * 2 < groups):
                                for u in range(2 * GT):
                                    t = i * (2 * GT) + u
                                    dve.wait_ge(s_used, t + 1)
                                    e = etab[:, ds(t, 1), :].rearrange("p o f -> p (o f)")
                                    v.tensor_scalar(hot_src[:, u % GT, 0:NP], iota16[:, :], e[:, F_SRC:F_SRC + 1], None, ALU.is_equal)
                                    v.tensor_scalar(hot_src[:, u % GT, NP:], iota16[:, 0:RELATIONS], e[:, F_REL:F_REL + 1], None, ALU.is_equal)
                                    v.tensor_scalar(hot_dst[:, u % GT, :], iota16[:, 0:P], e[:, F_DLOC:F_DLOC + 1], None, ALU.is_equal).then_inc(s_hot, 1)
                                for g in range(2):
                                    at = dve.value_load(group_tile[0:1, ds(i * 2 + g, 1)], min_val=0, max_val=NT - 1)
                                    dve.wait_ge(s_used, i * (2 * GT) + (g + 1) * GT + GT)
                                    dve.wait_ge(s_add, i * 2 + (g + 2))
                                    c = C[:, ds(at, 1), :].rearrange("p o c -> p (o c)")
                                    v.tensor_tensor(c, c, banks(3 * g, CC), ALU.add).then_inc(s_add, 1)
                        dve.wait_ge(s_add, (groups + 1) // 2 * 2 + 2)
                        dve.sem_inc(s_counts, 1)
                        dve.wait_ge(s_pc, 1)
                        v.tensor_scalar(present[:, :, :].rearrange("p j r -> p (j r)"), banks(6, NT * RELATIONS), 0.0, None,
                                        ALU.is_gt).then_inc(s_pres, 1)
                        link(v.tensor_scalar(inv[:, :, :], C[:, :, NP:], 1.0, None, ALU.max))
                        v.reciprocal(inv[:, :, :], inv[:, :, :]).then_inc(s_inv, 1)
                        link(v.tensor_reduce(deg[:, :], C[:, :, 0:NP], AX.X, ALU.add))
                        v.tensor_scalar(deg[:, :], deg[:, :], 1.0, None, ALU.add).then_inc(s_deg, 1)
                        dve.wait_ge(s_rpre, 1)
                        link(v.tensor_copy(in_tile[:, :, :].rearrange("p j r -> p (j r)"), banks(6, NT * RELATIONS)))
                        link(v.memset(slots[:, 0, :], 0.0))
                        for j in range(1, NT):
                            link(v.tensor_tensor(slots[:, j, :], slots[:, j - 1, :], in_tile[:, j - 1, :], ALU.add))
                        link(v.tensor_tensor(n_rel[:, :], slots[:, NT - 1, :], in_tile[:, NT - 1, :], ALU.add))
                        link(v.tensor_scalar(rtiles[:, :], n_rel[:, :], float(P - 1), None, ALU.add))
                        link(v.tensor_copy(rtilesi[:, :], rtiles[:, :]))
                        link(v.tensor_single_scalar(rtilesi[:, :], rtilesi[:, :], 7, ALU.arith_shift_right))
                        link(v.tensor_copy(rtiles[:, :], rtilesi[:, :]))
                        link(v.tensor_scalar(rtiles[:, :], rtiles[:, :], 1.0, None, ALU.max))
                        link(v.tensor_tensor_scan(rbase[:, :], rtiles[:, :], rtiles[:, :], 0.0, ALU.add, ALU.max))
                        link(v.tensor_copy(n_rel_tiles[:, :], rbase[0:1, RELATIONS - 1:RELATIONS]))
                        link(v.tensor_tensor(rbase[:, :], rbase[:, :], rtiles[:, :], ALU.subtract))
                        v.tensor_copy(rel_base[:, :], rbase[0:1, :])
                        sflat = slots[:, :, :].rearrange("p j r -> p (j r)")
                        link(v.tensor_tensor(sflat, sflat, banks(7, NT * RELATIONS), ALU.add))
                        link(v.scalar_tensor_tensor(in_tile[:, :, :], slots[:, :, :], 1.0, present[:, :, :], ALU.add, ALU.mult))
                        link(v.tensor_scalar(in_tile[:, :, :], in_tile[:, :, :], -1.0, None, ALU.add))
                        link(v.tensor_copy(pairi[:, 0, :, :], in_tile[:, :, :]))
                        link(v.tensor_single_scalar(pairi[:, 1, :, :], pairi[:, 0, :, :], P - 1, ALU.bitwise_and))
                        link(v.tensor_single_scalar(pairi[:, 0, :, :], pairi[:, 0, :, :], 7, ALU.arith_shift_right))
                        v.tensor_copy(pair_tile[:, :, :], pairi[:, 0, :, :])
                        v.tensor_copy(pair_place[:, :, :], pairi[:, 1, :, :])
                        v.scalar_tensor_tensor(slots[:, :, :], rbase[:, :].unsqueeze(1).to_broadcast([P, NT, RELATIONS]),
                                               float(P), slots[:, :, :], ALU.mult, ALU.add).then_inc(s_slot, 1)
                        for n in range(TABLE_COLS):
                            last = v.tensor_scalar(started[:, n, :], rbase[:, :], float(-n * P), pidx[:, :], ALU.add, ALU.is_le)
                        link(last)
                        v.tensor_reduce(n_started[:, :], started[:, :, :], AX.X, ALU.add).then_inc(s_rn, 1)
                        for j in range(NT):
                            v.tensor_scalar(mask[:, j, :], C[:, j, 0:NP], 0.0, NEGATIVE, ALU.is_equal, ALU.mult)
                        dve.wait_ge(s_sd2, 1)
                        v.reciprocal(dinv[:, :], deg[:, :])
                        dve.wait_ge(s_trel, 1)
                        link(v.tensor_scalar(trel[:, :], banks(6, REL_TILES)[0:1, :], -1.0, None, ALU.add))
                        v.tensor_copy(tile_rel[:, :], trel[:, :])
                        link(v.memset(first[:, :], 1.0))
                        link(v.tensor_tensor(first[:, 1:], trel[:, 1:], trel[:, 0:REL_TILES - 1], ALU.not_equal))
                        link(v.scalar_tensor_tensor(first[:, :], trel[:, :], float(RELATIONS - 1), first[:, :], ALU.is_lt, ALU.mult))
                        link(v.scalar_tensor_tensor(first[:, :], trel[:, :], 1.0, first[:, :], ALU.add, ALU.mult))
                        v.tensor_copy(next_rel[:, :], first[:, :])

                    @block.tensor
                    def _(pe):
                        pe.wait_ge(s_z16, 1)
                        nc.tensor.matmul(banks(6, NT * RELATIONS), zero16[:, 0:P], zero16[:, :], start=True, stop=False)
                        pe.sem_inc(s_used, GT)
                        pe.sem_inc(s_add, 2)
                        groups = pe.value_load(n_groups[0:1, 0:1], min_val=0, max_val=GROUPS)
                        with pe.Fori(0, GROUPS // 2) as i:
                            with pe.If(i * 2 < groups):
                                for g in range(2):
                                    pe.wait_ge(s_add, i * 2 + (g + 1))
                                    for q in range(GT):
                                        u = g * GT + q
                                        pe.wait_ge(s_hot, i * (2 * GT) + (u + 1))
                                        for a in range(0, CC, 512):
                                            w = min(512, CC - a)
                                            last = nc.tensor.matmul(banks(3 * g, 1536)[:, a:a + w], hot_dst[:, q, :], hot_src[:, q, a:a + w],
                                                                    start=(q == 0), stop=(q == GT - 1))
                                        for j in range(NT):
                                            last = nc.tensor.matmul(banks(6, 512)[:, j * RELATIONS:(j + 1) * RELATIONS],
                                                                    hot_src[:, q, j * P:(j + 1) * P], hot_src[:, q, NP:],
                                                                    start=False, stop=False, skip_group_check=True)
                                        last.then_inc(s_used, 1)
                        nc.tensor.matmul(banks(6, NT * RELATIONS), zero16[:, 0:P], zero16[:, :], start=False, stop=True).then_inc(s_pc, 1)
                        pe.wait_ge(s_pres, 1)
                        pflat = present[:, :, :].rearrange("p j r -> p (j r)")
                        nc.tensor.matmul(banks(7, NT * RELATIONS), tri[:, :], pflat, start=True, stop=True)
                        nc.tensor.matmul(banks(6, NT * RELATIONS), ones[:, :], pflat, start=True, stop=True).then_inc(s_rpre, 1)
                        pe.wait_ge(s_counts, 1)
                        for k in range(NT):
                            if k >= 2:
                                pe.wait_ge(s_cTe, k - 1)
                            for j in range(NT):
                                last = nc.tensor.transpose(banks(3 * (k % 2), NP)[:, j * P:(j + 1) * P],
                                                           C[:, j, k * P:(k + 1) * P], ident[:, :])
                            last.then_inc(s_cT, 1)
                        pe.wait_ge(s_rn, 1)
                        for n in range(TABLE_COLS):
                            last = nc.tensor.matmul(banks(6, TABLE_COLS * P)[0:1, n * P:(n + 1) * P], n_started[:, n:n + 1],
                                                    ident[:, :], start=True, stop=True)
                        last.then_inc(s_trel, 1)


        SLOTS = 5
        with ExitStack() as st:
            sb = holder(st)
            rows_v = sb("rows_v", [P, 2, NP])
            rows_m = sb("rows_m", [P, 2, NP])
            tt = sb("tt", [P, SLOTS, NP])
            M = sb("M", [P, HEADS, NT])
            Mz = sb("Mz", [P, HEADS, NT])
            u_pos = sb("u_pos", [P, HEADS, NT])
            u_neg = sb("u_neg", [P, HEADS, NT])
            m_sb = sb("m_sb", [80, P])
            rden = sb("rden", [P, NT])
            hn = sb("hn", [P, 2, NT, HEAD_DIM])
            widx = sb("widx", [P, 2, SB], i32)
            got = sb("got", [P, 2, SB])
            s_row = [sem("row_u0"), sem("row_u1")]
            s_rowf, s_M, s_MT, s_Me = (sem(n) for n in ("row_free", "m_ready", "m_turned", "m_moved"))
            s_vm = [sem("vm_row0"), sem("vm_row1")]
            s_pre, s_sub, s_exp, s_mul, s_mm = (sem(n) for n in ("leaky", "shifted", "exped", "probs", "head_tile_done"))
            s_hn, s_den, s_hfree, s_rm = (sem(n) for n in ("head_out", "head_sums", "head_free", "rows_mixed"))
            s_hd = [sem("head_stored0"), sem("head_stored1")]
            s_ixs, s_sld, s_kept = sem("slot_idx_staged"), [sem(f"slots_gathered{u}") for u in range(2)], sem("slots_kept")

            with nc.Block() as block:
                @block.sync
                def _(sp):
                    for h in range(HEADS):
                        if h >= 2:
                            sp.wait_ge(s_rowf, h - 1)
                        sp.dma_start(rows_v[:, h % 2, :], row_of(uv_rows, 2 * h)).then_inc(s_row[h % 2], 16)
                    sp.wait_ge(s_Me, 1)
                    sp.dma_start(m_rows, m_sb[:, :]).then_inc(s_moved, 16)
                    all_moved(sp, 1)
                    vr = uv_rows.rearrange("(h c j) p -> h c (j p)", c=2, j=NT)
                    mr = m_rows.rearrange("(h j) p -> h (j p)", j=NT)
                    h1v = h1_dram.rearrange("(j p) (h c) -> h p j c", p=P, h=HEADS)

                    def load(h, g):
                        sp.dma_start(rows_v[:, g, :], vr[ds(h, 1), 1, :].to_broadcast([P, NP])).then_inc(s_vm[g], 16)
                        sp.dma_start(rows_m[:, g, :], mr[ds(h, 1), :].to_broadcast([P, NP])).then_inc(s_vm[g], 16)

                    def store(h, g):
                        sp.wait_ge(s_hn, h + 3)
                        sp.sem_inc(s_go_sp, 1)
                        sp.dma_start(h1v[ds(h, 1), :, :, :].rearrange("o p j c -> (o p) j c"), hn[:, g, :, :]).then_inc(s_hd[g], 16)

                    for g in range(2):
                        load(g, g)
                    with sp.Fori(0, HEADS // 2 - 1) as i:
                        for g in range(2):
                            store(i * 2 + g, g)
                            load(i * 2 + (g + 2), g)
                            sp.wait_ge(s_hd[g], i * 16 + 16)
                            sp.sem_inc(s_hfree, 1)
                    for g in range(2):
                        store(HEADS - 2 + g, g)
                    for g in range(2):
                        sp.wait_ge(s_hd[g], 8 * HEADS)

                @block.gpsimd
                def _(pool):
                    def gather(c, half):
                        nc.gpsimd.tensor_copy(widx[:, half, :], slot_flat[:, ds(c * SB, SB)]).then_inc(s_ixs, 1)
                        pool.wait_ge(s_ixs, c + 1)
                        pool.sem_inc(s_go, 1)
                        for u in range(SB):
                            pool.indirect_dma_start(got[:, half, u:u + 1], None, slot_table,
                                                    bass.IndirectOffsetOnAxis(widx[:, half, u:u + 1], 0)).then_inc(s_sld[half], 16)

                    def keep_slots(c, half):
                        nc.gpsimd.tensor_copy(slot_of[:, ds(c * SB, SB)], got[:, half, :]).then_inc(s_kept, 1)
                        pool.wait_ge(s_kept, c + 3)
                        pool.sem_inc(s_go, 1)

                    groups = pool.value_load(n_groups[0:1, 0:1], min_val=1, max_val=GROUPS)
                    pool.sem_inc(s_kept, 2)
                    walk_columns(pool, groups, gather, keep_slots, s_sld)

                @block.scalar
                def _(act):
                    act.wait_ge(s_MT, 1)
                    nc.scalar.copy(m_sb[:, :], banks(0, P)[:80, :]).then_inc(s_Me, 1)
                    with act.Fori(0, HEADS // 2) as i:
                        for g in range(2):
                            h = i * 2 + g
                            act.wait_ge(s_vm[g], i * 32 + 32)

                            def leaky(k):
                                act.wait_ge(s_mm, h * NT + (k + 1))
                                nc.scalar.activation(tt[:, k % SLOTS, :], rows_v[:, g, :], ACT.Relu,
                                                     bias=u_pos[:, ds(h, 1), k:k + 1].rearrange("p o k -> p (o k)"),
                                                     scale=1.0 - NEG_SLOPE).then_inc(s_pre, 1)
                            leaky(0)
                            for k in range(NT):
                                if k + 1 < NT:
                                    leaky(k + 1)
                                act.wait_ge(s_sub, h * NT + (k + 1))
                                nc.scalar.activation(tt[:, k % SLOTS, :], tt[:, k % SLOTS, :], ACT.Exp).then_inc(s_exp, 1)

                @block.vector
                def _(dve):
                    v = nc.vector
                    link = chain(dve)
                    for h in range(HEADS):
                        dve.wait_ge(s_row[h % 2], 16 * (h // 2 + 1))
                        for j in range(NT):
                            link(v.tensor_tensor_reduce(out=tt[:, 0, :], in0=mask[:, j, :], in1=rows_v[:, h % 2, :], scale=1.0,
                                                        scalar=NEGATIVE, op0=ALU.add, op1=ALU.max, accum_out=M[:, h, j:j + 1]))
                        dve.sem_inc(s_rowf, 1)
                    dve.wait_ge(s_rowf, HEADS)
                    uvc = uv[:, :, :].rearrange("p (h c) j -> p h c j", c=2)
                    v.tensor_scalar(u_pos[:, :, :], uvc[:, :, 0, :], 1.0 - NEG_SLOPE, None, ALU.mult)
                    v.tensor_scalar(u_neg[:, :, :], uvc[:, :, 0, :], NEG_SLOPE, None, ALU.mult)
                    link(v.scalar_tensor_tensor(M[:, :, :], M[:, :, :], NEGATIVE / 2, M[:, :, :], ALU.is_gt, ALU.mult))
                    link(v.tensor_tensor(M[:, :, :], M[:, :, :], uvc[:, :, 1, :], ALU.add))
                    link(v.tensor_scalar(Mz[:, :, :], M[:, :, :], NEG_SLOPE, None, ALU.mult))
                    v.tensor_tensor(Mz[:, :, :], Mz[:, :, :], M[:, :, :], ALU.max).then_inc(s_M, 1)
                    hd = HEAD_DIM
                    with dve.Fori(0, HEADS // 2) as i:
                        for g in range(2):
                            h = i * 2 + g
                            dve.wait_ge(s_vm[g], i * 32 + 32)
                            v.scalar_tensor_tensor(rows_m[:, g, :], rows_v[:, g, :], NEG_SLOPE, rows_m[:, g, :],
                                                   ALU.mult, ALU.subtract).then_inc(s_rm, 1)
                            dve.wait_ge(s_rm, h + 1)

                            def shift(k):
                                dve.wait_ge(s_pre, h * NT + (k + 1))
                                v.scalar_tensor_tensor(tt[:, k % SLOTS, :], tt[:, k % SLOTS, :],
                                                       u_neg[:, ds(h, 1), k:k + 1].rearrange("p o k -> p (o k)"),
                                                       rows_m[:, g, :], ALU.add, ALU.add).then_inc(s_sub, 1)
                            shift(0)
                            for k in range(NT):
                                if k + 1 < NT:
                                    shift(k + 1)
                                dve.wait_ge(s_exp, h * NT + (k + 1))
                                v.scalar_tensor_tensor(tt[:, k % SLOTS, :], tt[:, k % SLOTS, :], BIG, CT[:, k, :],
                                                       ALU.min, ALU.mult).then_inc(s_mul, 1)
                            dve.wait_ge(s_mm, h * NT + (NT + SLOTS))
                            dve.wait_ge(s_hfree, h + 1)
                            three = PS[:, 4 * g:4 * g + 3, 0:3 * HCOLS].rearrange("p q (t c) -> p q t c", c=HCOLS)
                            v.tensor_scalar(rden[:, 0:9].rearrange("p (q t) -> p q t", t=3), three[:, :, :, hd], SOFTMAX_EPS, None, ALU.add)
                            link_sem = v.tensor_scalar(rden[:, 9:10], banks(4 * g + 3, HCOLS)[:, hd:], SOFTMAX_EPS, None, ALU.add)
                            link_sem.then_inc(s_den, 1)
                            dve.wait_ge(s_den, h * 2 + 1)
                            v.reciprocal(rden[:, :], rden[:, :]).then_inc(s_den, 1)
                            dve.wait_ge(s_den, h * 2 + 2)
                            for q in range(3):
                                v.tensor_tensor(hn[:, g, 3 * q:3 * q + 3, :], three[:, q, :, 0:hd],
                                                rden[:, 3 * q:3 * q + 3].unsqueeze(2).to_broadcast([P, 3, hd]), ALU.mult)
                            v.tensor_scalar(hn[:, g, 9, :], banks(4 * g + 3, hd), rden[:, 9:10], None, ALU.mult).then_inc(s_hn, 1)

                @block.tensor
                def _(pe):
                    pe.sem_inc(s_mm, SLOTS)
                    pe.sem_inc(s_hn, 2)
                    pe.sem_inc(s_hfree, 2)
                    pe.wait_ge(s_M, 1)
                    nc.tensor.transpose(banks(0, P)[:80, :], Mz[:, :, :].rearrange("p h j -> p (h j)"), ident[:, :]).then_inc(s_MT, 1)
                    pe.wait_ge(s_Me, 1)
                    with pe.Fori(0, HEADS // 2) as i:
                        for g in range(2):
                            h = i * 2 + g
                            pe.wait_ge(s_hn, h + 1)
                            for k in range(NT):
                                pe.wait_ge(s_mul, h * NT + (k + 1))
                                for j in range(NT):
                                    last = nc.tensor.matmul(PS[:, 4 * g + j // 3, (j % 3) * HCOLS:(j % 3 + 1) * HCOLS],
                                                            tt[:, k % SLOTS, j * P:(j + 1) * P],
                                                            hA[:, k, ds(h, 1), :].rearrange("p o c -> p (o c)"),
                                                            start=(k == 0 and j % 3 == 0), stop=(k == NT - 1), skip_group_check=True)
                                last.then_inc(s_mm, 1)

        RQ = 4
        with ExitStack() as st:
            sb = holder(st)
            w2 = sb("w2", [P, KD, HID])
            att2 = sb("att2", [P, KD, 2])
            w2T = sb("w2T", [P, KH, DIM + 2])
            b1c = sb("b1c", [P, KH])
            h1 = sb("h1", [P, 2, HID])
            h1T = sb("h1T", [P, 2, KH, P])
            rows2 = sb("rows2", [2 * NT, P])
            iota_b = sb("iota_b", [P, P], bf16)
            hot_place = region_h[:, NT * (DIM + 1) + 2:NT * (DIM + 1) + 2 + RQ * NP // 2].bitcast(bf16).rearrange(
                "p (q j s) -> p q j s", q=RQ, s=P)
            hot_tile = sb("hot_tile", [P, RQ, NT, NT], bf16)
            tile_src = sb("tile_src", [P, RQ, NT, NT, 2], bf16)
            src_parts = sb("src_parts", [P, NT, NT, 2], bf16)
            s_hp, s_srcd, s_srct = (sem(n) for n in ("pairs_hot", "sources_done", "sources_taken"))
            s_w2, s_p2, s_w2t, s_w2e, s_wa2, s_uT2, s_ue2 = (sem(n) for n in (
                "w2_in", "att2_in", "w2_turned", "w2_moved", "att2_folded", "uv2_turned", "uv2_moved"))
            s_h1 = [sem("h1_in0"), sem("h1_in1")]
            pj2 = Projection("w2", KH, [512, DIM + 2 - 512])

            with nc.Block() as block:
                @block.sync
                def _(sp):
                    sp.dma_start(w2[:, :, :], W2.rearrange("(k p) c -> p k c", p=P)).then_inc(s_w2, 16)
                    with nc.allow_non_contiguous_dma(reason="vectors as columns"):
                        sp.dma_start(att2[:, :, 0], as2.rearrange("o (k p) -> p (o k)", p=P)).then_inc(s_p2, 16)
                        sp.dma_start(att2[:, :, 1], ad2.rearrange("o (k p) -> p (o k)", p=P)).then_inc(s_p2, 16)
                        sp.dma_start(b1c[:, :], b1.rearrange("(k p) -> p k", p=P)).then_inc(s_p2, 16)
                    for j in range(NT):
                        if j >= 2:
                            sp.wait_ge(pj2.turned, j - 1)
                        sp.dma_start(h1[:, j % 2, :], h1_dram[j * P:(j + 1) * P, :]).then_inc(s_h1[j % 2], 16)
                    sp.wait_ge(s_ue2, 1)
                    sp.dma_start(uv2_rows, rows2[:, :]).then_inc(s_moved, 16)
                    all_moved(sp, 1)

                @block.scalar
                def _(act):
                    for g in range(2 * KH):
                        act.wait_ge(s_w2t, g + 1)
                        nc.scalar.copy(w2T[:, g // 2, 384 * (g % 2):384 * (g % 2) + 384], banks(g % 2, 384)).then_inc(s_w2e, 1)
                    act.wait_ge(s_wa2, 1)
                    nc.scalar.copy(w2T[:, :, DIM:], banks(2, 2 * KH).rearrange("p (k c) -> p k c", k=KH)).then_inc(s_w2e, 1)
                    act.wait_ge(s_p2, 48)

                    def relu_bias(j):
                        for k in range(KH):
                            last = nc.scalar.activation(h1T[:, j % 2, k, :], banks(0, 1024)[:, k * P:(k + 1) * P],
                                                        ACT.Relu, bias=b1c[:, k:k + 1])
                        return last
                    project_act(act, pj2, h1T, relu_bias)
                    act.wait_ge(s_uT2, 1)
                    nc.scalar.copy(rows2[:, :], banks(0, P)[:2 * NT, :]).then_inc(s_ue2, 1)

                @block.vector
                def _(dve):
                    v = nc.vector
                    link = chain(dve)
                    v.memset(hB[:, :, DIM:], 1.0)
                    v.tensor_copy(iota_b[:, :], iota[:, :])
                    v.tensor_copy(src_parts[:, :, :, 0], pidx[:, 0:1].unsqueeze(2).to_broadcast([P, NT, NT]))
                    link(v.tensor_scalar(src_parts[:, :, :, 1], iota[:, 0:NT].unsqueeze(2).to_broadcast([P, NT, NT]),
                                         float(P), None, ALU.mult))

                    def relations(j):
                        return range(j * RQ, min(RELATIONS, (j + 1) * RQ))

                    def one_hots(j):
                        for q, r in enumerate(relations(j)):
                            v.tensor_tensor(hot_place[:, q, :, :], pair_place[:, :, r:r + 1].to_broadcast([P, NT, P]),
                                            iota_b[:, :].unsqueeze(1).to_broadcast([P, NT, P]), ALU.is_equal)
                            link(v.tensor_tensor(hot_tile[:, q, :, :], pair_tile[:, :, r:r + 1].to_broadcast([P, NT, NT]),
                                                 iota_b[:, 0:NT].unsqueeze(1).to_broadcast([P, NT, NT]), ALU.is_equal))
                            v.tensor_tensor(tile_src[:, q, :, :, :], hot_tile[:, q, :, :].unsqueeze(3).to_broadcast([P, NT, NT, 2]),
                                            src_parts[:, :, :, :], ALU.mult).then_inc(s_hp, 1)

                    one_hots(0)
                    for j in range(NT):
                        dve.wait_ge(pj2.multiplied, j + 1)
                        v.tensor_copy(hB[:, j, 0:DIM], banks(2 + 3 * (j % 2), DIM))
                        v.tensor_copy(uv2[:, :, j], banks(2 + 3 * (j % 2), DIM + 2)[:, DIM:]).then_inc(pj2.taken, 1)
                        if relations(j):
                            dve.wait_ge(s_srcd, relations(j)[-1] + 1)
                        for q, r in enumerate(relations(j)):
                            at = dve.value_load(rel_base[0:1, r:r + 1], min_val=0, max_val=REL_TILES - 1)
                            ins = v.tensor_reduce(rtab[:, ds(at, NT)], banks(4, RQ * 2 * NT)[:, q * 2 * NT:(q + 1) * 2 * NT].rearrange(
                                "p (a o) -> p a o", o=2), AX.X, ALU.add)
                            ins.then_inc(s_srct, 1)
                            dve.wait_ge(s_srct, r + 1)
                        one_hots(j + 1)

                @block.tensor
                def _(pe):
                    pe.wait_ge(s_w2, 16)
                    for g in range(2 * KH):
                        if g >= 2:
                            pe.wait_ge(s_w2e, g - 1)
                        for u in range(3):
                            o = 3 * (g % 2) + u
                            last = nc.tensor.transpose(banks(g % 2, 384)[:, u * P:(u + 1) * P],
                                                       w2[:, o, (g // 2) * P:(g // 2 + 1) * P], ident[:, :])
                        last.then_inc(s_w2t, 1)
                    pe.wait_ge(s_p2, 48)
                    for k in range(KH):
                        for o in range(KD):
                            last = nc.tensor.matmul(banks(2, 16)[:, 2 * k:2 * k + 2], w2[:, o, k * P:(k + 1) * P], att2[:, o, :],
                                                    start=(o == 0), stop=(o == KD - 1))
                    last.then_inc(s_wa2, 1)
                    pe.wait_ge(s_w2e, 2 * KH + 1)

                    def h1_ready(j):
                        return 16 * (j // 2 + 1)

                    def sources(j):
                        for r in range(j * RQ, min(RELATIONS, (j + 1) * RQ)):
                            pe.wait_ge(s_hp, r + 1)
                            if r % RQ == 0 and r:
                                pe.wait_ge(s_srct, r)
                            for k in range(NT):
                                last = nc.tensor.matmul(banks(4, 512)[:, (r % RQ) * 2 * NT:(r % RQ + 1) * 2 * NT], hot_place[:, r % RQ, k, :],
                                                        tile_src[:, r % RQ, k, :, :].rearrange("p a o -> p (a o)"),
                                                        start=(k == 0), stop=(k == NT - 1))
                            last.then_inc(s_srcd, 1)

                    project_pe(pe, pj2, lambda j: h1[:, j % 2, :], (s_h1, h1_ready), h1T, w2T, sources)
                    pe.wait_ge(pj2.taken, NT)
                    nc.tensor.transpose(banks(0, P)[:2 * NT, :], uv2[:, :, :].rearrange("p c j -> p (c j)"), ident[:, :]).then_inc(s_uT2, 1)

        with ExitStack() as st:
            sb = holder(st)
            s_cto = sem("ct_out")
            row_a = sb("row_a", [P, NP])
            row_m = sb("row_m", [P, NP])
            pr = sb("pr", [P, NT, NP])
            M2 = sb("M2", [P, NT])
            Mz2 = sb("Mz2", [P, NT])
            u2p = sb("u2p", [P, NT])
            u2n = sb("u2n", [P, NT])
            m2_sb = sb("m2_sb", [NT, P])
            rden2 = sb("rden2", [P, NT])
            b2row = sb("b2row", [P, DIM])
            s_ra, s_rm, s_M2, s_M2T, s_M2e, s_b2, s_x2, s_xb = (sem(n) for n in (
                "row2_in", "rowm2_in", "m2_ready", "m2_turned", "m2_moved", "b2_in", "x_again", "x_pad2"))
            widx5 = sb("widx5", [P, 2, SB], i32)
            wst = sb("wst", [P, 2, SB])
            s_wst, s_wkeep, s_wld = sem("w_staged"), sem("w_kept"), [sem(f"w_gathered{u}") for u in range(2)]
            s_pre2, s_sub2, s_exp2, s_mul2, s_mm2, s_tk2 = (sem(n) for n in (
                "leaky2", "shifted2", "exped2", "probs2", "tile_done2", "tile_taken2"))

            with nc.Block() as block:
                @block.sync
                def _(sp):
                    sp.dma_start(row_a[:, :], row_of(uv2_rows, 0)).then_inc(s_ra, 16)
                    sp.dma_start(b2row[:, :], vector_row(b2, DIM)).then_inc(s_b2, 16)
                    sp.dma_start(ct_dram, CT[:, :, :].rearrange("p k d -> p (k d)")).then_inc(s_cto, 16)
                    sp.wait_ge(s_M2, 1)
                    sp.dma_start(row_a[:, :], row_of(uv2_rows, 1)).then_inc(s_ra, 16)
                    sp.wait_ge(s_M2e, 1)
                    sp.dma_start(m2_rows, m2_sb[:, :]).then_inc(s_moved, 16)
                    all_moved(sp, 1)
                    sp.dma_start(row_m[:, :], row_of(m2_rows, 0)).then_inc(s_rm, 16)
                    sp.dma_start(x2[:, 0:NT - 1, :], x[0:(NT - 1) * P, :].rearrange("(j p) i -> p j i", p=P)).then_inc(s_x2, 16)
                    sp.wait_ge(s_xb, 1)
                    sp.dma_start(x2[:LAST, NT - 1, :], x[(NT - 1) * P:NODES, :]).then_inc(s_x2, 16)
                    sp.wait_ge(s_cto, 16)

                @block.gpsimd
                def _(pool):
                    def gather(c, half):
                        nc.gpsimd.tensor_copy(widx5[:, half, :], etab[:, ds(c * SB, SB), F_DREL]).then_inc(s_wst, 1)
                        pool.wait_ge(s_wst, c + 1)
                        pool.sem_inc(s_go, 1)
                        for u in range(SB):
                            pool.indirect_dma_start(wst[:, half, u:u + 1], None, inv_count,
                                                    bass.IndirectOffsetOnAxis(widx5[:, half, u:u + 1], 0)).then_inc(s_wld[half], 16)

                    def keep_weights(c, half):
                        nc.gpsimd.tensor_copy(weight[:, ds(c * SB, SB)], wst[:, half, :]).then_inc(s_wkeep, 1)
                        pool.wait_ge(s_wkeep, c + 3)
                        pool.sem_inc(s_go, 1)

                    groups = pool.value_load(n_groups[0:1, 0:1], min_val=1, max_val=GROUPS)
                    pool.sem_inc(s_wkeep, 2)
                    walk_columns(pool, groups, gather, keep_weights, s_wld)

                @block.scalar
                def _(act):
                    act.wait_ge(s_M2T, 1)
                    nc.scalar.copy(m2_sb[:, :], banks(0, P)[:NT, :]).then_inc(s_M2e, 1)
                    act.wait_ge(s_ra, 32)
                    for k in range(NT):
                        nc.scalar.activation(pr[:, k, :], row_a[:, :], ACT.Relu, bias=u2p[:, k:k + 1],
                                             scale=1.0 - NEG_SLOPE).then_inc(s_pre2, 1)
                    for k in range(NT):
                        act.wait_ge(s_sub2, k + 1)
                        nc.scalar.activation(pr[:, k, :], pr[:, k, :], ACT.Exp).then_inc(s_exp2, 1)

                @block.vector
                def _(dve):
                    v = nc.vector
                    link = chain(dve)
                    dve.wait_ge(s_ra, 16)
                    for j in range(NT):
                        link(v.tensor_tensor_reduce(out=pr[:, 0, :], in0=mask[:, j, :], in1=row_a[:, :], scale=1.0,
                                                    scalar=NEGATIVE, op0=ALU.add, op1=ALU.max, accum_out=M2[:, j:j + 1]))
                    v.memset(x2[:, NT - 1, :], 0.0).then_inc(s_xb, 1)
                    v.tensor_scalar(u2p[:, :], uv2[:, 0, :], 1.0 - NEG_SLOPE, None, ALU.mult)
                    v.tensor_scalar(u2n[:, :], uv2[:, 0, :], NEG_SLOPE, None, ALU.mult)
                    link(v.scalar_tensor_tensor(M2[:, :], M2[:, :], NEGATIVE / 2, M2[:, :], ALU.is_gt, ALU.mult))
                    link(v.tensor_tensor(M2[:, :], M2[:, :], uv2[:, 1, :], ALU.add))
                    link(v.tensor_scalar(Mz2[:, :], M2[:, :], NEG_SLOPE, None, ALU.mult))
                    v.tensor_tensor(Mz2[:, :], Mz2[:, :], M2[:, :], ALU.max).then_inc(s_M2, 1)
                    dve.wait_ge(s_rm, 16)
                    dve.wait_ge(s_ra, 32)
                    link(v.scalar_tensor_tensor(row_m[:, :], row_a[:, :], NEG_SLOPE, row_m[:, :], ALU.mult, ALU.subtract))

                    def shift(k):
                        dve.wait_ge(s_pre2, k + 1)
                        v.scalar_tensor_tensor(pr[:, k, :], pr[:, k, :], u2n[:, k:k + 1], row_m[:, :], ALU.add, ALU.add).then_inc(s_sub2, 1)
                    shift(0)
                    for k in range(NT):
                        if k + 1 < NT:
                            shift(k + 1)
                        dve.wait_ge(s_exp2, k + 1)
                        v.scalar_tensor_tensor(pr[:, k, :], pr[:, k, :], BIG, CT[:, k, :], ALU.min, ALU.mult).then_inc(s_mul2, 1)
                    dve.wait_ge(s_x2, 32)
                    dve.wait_ge(s_b2, 16)
                    for j in range(NT):
                        last = v.tensor_tensor(x2[:, j, :], x2[:, j, :], b2row[:, :], ALU.add)
                    link(last)
                    for j in range(NT):
                        o = banks(2 * (j % 4), DIM + 1)
                        dve.wait_ge(s_mm2, j + 1)
                        link(v.tensor_scalar(rden2[:, j:j + 1], o[:, DIM:], SOFTMAX_EPS, None, ALU.add))
                        link(v.reciprocal(rden2[:, j:j + 1], rden2[:, j:j + 1]))
                        v.scalar_tensor_tensor(x2[:, j, :], o[:, 0:DIM], rden2[:, j:j + 1], x2[:, j, :], ALU.mult, ALU.add).then_inc(s_tk2, 1)

                @block.tensor
                def _(pe):
                    pe.wait_ge(s_M2, 1)
                    nc.tensor.transpose(banks(0, P)[:NT, :], Mz2[:, :], ident[:, :]).then_inc(s_M2T, 1)
                    pe.wait_ge(s_M2e, 1)
                    for j in range(NT):
                        if j >= 4:
                            pe.wait_ge(s_tk2, j - 3)
                        for k in range(NT):
                            if j == 0:
                                pe.wait_ge(s_mul2, k + 1)
                            for a, w in ((0, 512), (512, DIM + 1 - 512)):
                                last = nc.tensor.matmul(banks(2 * (j % 4), 1024)[:, a:a + w], pr[:, k, j * P:(j + 1) * P],
                                                        hB[:, k, a:a + w], start=(k == 0), stop=(k == NT - 1))
                        last.then_inc(s_mm2, 1)

        counts_life.close()

        with ExitStack() as st:
            sb = holder(st)
            hR = sb("hR", [P, NT, DIM])
            wr = sb("wr", [P, KD, DIM])
            hT = sb("hT", [P, 2, KD, P])
            brow = sb("brow", [P, DIM])
            stats2 = sb("stats2", [P, NT, 2, 6])
            mv2 = sb("mv2", [P, NT, 2])
            rstd2 = sb("rstd2", [P, NT])
            nmr2 = sb("nmr2", [P, NT])
            s_wr, s_br, s_mvb, s_sdb, s_lnb, s_hb = (sem(n) for n in (
                "wroot_in", "brgcn_in", "ln2_stats", "ln2_sd", "ln2_scale", "h_ready"))
            pj3 = Projection("wroot", KD, [512, 256])

            with nc.Block() as block:
                @block.sync
                def _(sp):
                    sp.dma_start(wr[:, :, :], Wroot.rearrange("(k p) o -> p k o", p=P)).then_inc(s_wr, 16)
                    sp.dma_start(brow[:, :], vector_row(brg, DIM)).then_inc(s_br, 16)
                    for j in range(NT):
                        sp.wait_ge(s_hb, j + 1)
                        sp.dma_start(h_dram[j * P:(j + 1) * P, :], hR[:, j, :]).then_inc(s_moved, 16)
                    all_moved(sp, NT)

                @block.scalar
                def _(act):
                    act.wait_ge(s_mvb, 1)
                    nc.scalar.activation(rstd2[:, :], mv2[:, :, 1], ACT.Sqrt, bias=eps_ln[:, :]).then_inc(s_sdb, 1)
                    act.wait_ge(s_lnb, 1)
                    for j in range(NT):
                        nc.scalar.activation(hR[:, j, :], x2[:, j, :], ACT.Relu, bias=nmr2[:, j:j + 1],
                                             scale=rstd2[:, j:j + 1]).then_inc(s_hb, 1)
                    project_act(act, pj3, hT)

                @block.vector
                def _(dve):
                    v = nc.vector
                    link = chain(dve)
                    for j in range(NT):
                        for c in range(2):
                            last = v.bn_stats(stats2[:, j, c, :], x2[:, j, c * 384:(c + 1) * 384])
                    link(last)
                    for j in range(NT):
                        last = v.bn_aggr(mv2[:, j, :], stats2[:, j, :, :].rearrange("p a b -> p (a b)"))
                    last.then_inc(s_mvb, 1)
                    dve.wait_ge(s_sdb, 1)
                    link(v.reciprocal(rstd2[:, :], rstd2[:, :]))
                    dve.wait_ge(s_mvb, 1)
                    v.scalar_tensor_tensor(nmr2[:, :], mv2[:, :, 0], -1.0, rstd2[:, :], ALU.mult, ALU.mult).then_inc(s_lnb, 1)
                    dve.wait_ge(s_br, 16)
                    for j in range(NT):
                        dve.wait_ge(pj3.multiplied, j + 1)
                        v.tensor_tensor(acc[:, j, :], banks(2 + 3 * (j % 2), DIM), brow[:, :], ALU.add).then_inc(pj3.taken, 1)

                @block.tensor
                def _(pe):
                    pe.wait_ge(s_wr, 16)
                    project_pe(pe, pj3, lambda j: hR[:, j, :], (s_hb, lambda j: j + 1), hT, wr)

        with ExitStack() as st:
            sb = holder(st)
            wraw = sb("wraw", [P, KD, DIM])
            whi = sb("whi", [P, 2, KD, DIM], f32r)
            wlo = sb("wlo", [P, 2, KD, DIM], f32r)
            gx = sb("gx", [P, 2, DIM])
            ghi = sb("ghi", [P, 2, KD, P], f32r)
            glo = sb("glo", [P, 2, KD, P], f32r)
            mo = sb("mo", [P, 2, DIM])
            gidx = sb("gidx", [P, 2, 1], i32)
            s_w, s_idx, s_tn, s_tm, s_tl, s_mt, s_mo, s_whi, s_wlo = (sem(n) for n in (
                "wrel_in", "src_staged", "edges_turned", "edges_hi", "edges_lo", "messages_done", "messages_moved",
                "wrel_hi", "wrel_lo"))
            s_gx = [sem(f"edges_in{u}") for u in range(2)]
            s_ms = [sem(f"messages_stored{u}") for u in range(2)]
            TL = REL_TILES

            with nc.Block() as block:
                def pairs(eng):
                    return eng.value_load(n_rel_tiles[0:1, 0:1], min_val=1, max_val=TL)

                @block.sync
                def _(sp):
                    wv = Wrel.rearrange("r (k p) o -> p r k o", p=P)
                    sp.dma_start(wraw[:, :, :], wv[:, 0, :, :]).then_inc(s_w, 16)
                    with sp.Fori(1, RELATIONS) as r:
                        sp.wait_ge(s_wlo, r)
                        sp.sem_inc(s_go_sp, 1)
                        sp.dma_start(wraw[:, :, :], wv[:, ds(r, 1), :, :].rearrange("p o k n -> p (o k) n")).then_inc(s_w, 16)
                    sp.wait_ge(s_w, 16 * RELATIONS)

                @block.gpsimd
                def _(pool):
                    def gather(t, n, u):
                        pool.wait_ge(s_tn, n)
                        nc.gpsimd.tensor_copy(gidx[:, u, :], rtab[:, ds(t, 1)]).then_inc(s_idx, 1)
                        pool.wait_ge(s_idx, n)
                        pool.sem_inc(s_go, 1)
                        pool.indirect_dma_start(gx[:, u, :], None, h_dram,
                                                bass.IndirectOffsetOnAxis(gidx[:, u, :], 0)).then_inc(s_gx[u], 16)

                    tiles = pairs(pool)
                    gather(0, 1, 0)
                    with pool.Fori(0, TL // 2) as i:
                        with pool.If(i * 2 < tiles):
                            gather(i * 2 + 1, i * 2 + 2, 1)
                            gather(i * 2 + 2, i * 2 + 3, 0)

                @block.scalar
                def _(act):
                    mv_ = msg_dram.rearrange("(t p) o -> t p o", p=P)

                    def move(t, u):
                        act.wait_ge(s_tn, t + 3)
                        act.wait_ge(s_mt, t + 1)
                        nc.scalar.copy(ghi[:, u, :, :].rearrange("p k n -> p (k n)"), banks(6 * u, DIM)).then_inc(s_tm, 1)

                    def split(r, slot):
                        act.wait_ge(s_w, r * 16 + 16)
                        for k in range(0, KD, 2):
                            nc.scalar.copy(whi[:, slot, k:k + 2, :].rearrange("p o k n -> p (o k n)"),
                                           wraw[:, k:k + 2, :].rearrange("p k n -> p (k n)")).then_inc(s_whi, 1)

                    def store(t, u, waits=True):
                        if waits:
                            act.wait_ge(s_mo, t + 3)
                        act.dma_start(mv_[ds(t, 1), :, :].rearrange("o p n -> (o p) n"), mo[:, u, :]).then_inc(s_ms[u], 16)

                    tiles = pairs(act)
                    move(0, 0)
                    split(0, ds(0, 1))
                    with act.Fori(0, TL // 2) as i:
                        with act.If(i * 2 < tiles):
                            for u in range(2):
                                move(i * 2 + (u + 1), (u + 1) % 2)
                                nxt = act.value_load(next_rel[0:1, ds(i * 2 + u, 1)], min_val=0, max_val=RELATIONS - 1)
                                with act.If(nxt > 0):
                                    act.wait_ge(s_mt, i * 2 + (u + 2))
                                    split(nxt, ds(act.snap(nxt % 2), 1))
                                store(i * 2 + u, u)
                        with act.If(i * 2 >= tiles):
                            for u in range(2):
                                store(i * 2 + u, u, waits=False)
                    for u in range(2):
                        act.wait_ge(s_ms[u], 8 * TL)

                @block.vector
                def _(dve):
                    v = nc.vector

                    def rest(t, u):
                        dve.wait_ge(s_tm, t + 1)
                        v.tensor_tensor(glo[:, u, :, :].rearrange("p k n -> p (k n)"), banks(6 * u, DIM),
                                        ghi[:, u, :, :].rearrange("p k n -> p (k n)").bitcast(f32), ALU.subtract).then_inc(s_tl, 1)

                    def split(r, slot):
                        for k in range(0, KD, 2):
                            dve.wait_ge(s_whi, r * (KD // 2) + (k // 2 + 1))
                            last = v.tensor_tensor(wlo[:, slot, k:k + 2, :].rearrange("p o k n -> p (o k n)"),
                                                   wraw[:, k:k + 2, :].rearrange("p k n -> p (k n)"),
                                                   whi[:, slot, k:k + 2, :].rearrange("p o k n -> p (o k n)").bitcast(f32), ALU.subtract)
                        last.then_inc(s_wlo, 1)

                    def take(t, u):
                        dve.wait_ge(s_mt, t + 3)
                        v.tensor_copy(mo[:, u, :], banks(2 + 2 * u, DIM)).then_inc(s_mo, 1)

                    tiles = pairs(dve)
                    rest(0, 0)
                    split(0, ds(0, 1))
                    with dve.Fori(0, TL // 2) as i:
                        with dve.If(i * 2 < tiles):
                            for u in range(2):
                                rest(i * 2 + (u + 1), (u + 1) % 2)
                                nxt = dve.value_load(next_rel[0:1, ds(i * 2 + u, 1)], min_val=0, max_val=RELATIONS - 1)
                                with dve.If(nxt > 0):
                                    split(nxt, ds(dve.snap(nxt % 2), 1))
                                with dve.If(i > 0):
                                    dve.wait_ge(s_ms[u], i * 16)
                                    dve.sem_inc(s_go_sp, 1)
                                take(i * 2 + u, u)

                @block.tensor
                def _(pe):
                    for s in (s_tn, s_tl, s_mt, s_mo):
                        pe.sem_inc(s, 2)

                    def turn(t, n, u):
                        pe.wait_ge(s_gx[u], n)
                        pe.wait_ge(s_tl, t + 1)
                        for k in range(KD):
                            last = nc.tensor.transpose(banks(6 * u, DIM)[:, k * P:(k + 1) * P], gx[:, u, k * P:(k + 1) * P], ident[:, :])
                        last.then_inc(s_tn, 1)

                    def multiply(t, u):
                        r = pe.value_load(tile_rel[0:1, ds(t, 1)], min_val=0, max_val=RELATIONS - 1)
                        pe.wait_ge(s_wlo, r + 1)
                        slot = pe.snap(r % 2)
                        pe.wait_ge(s_tl, t + 3)
                        pe.wait_ge(s_mo, t + 1)
                        for k in range(KD):
                            for n, (g, w_) in enumerate(((ghi, whi), (ghi, wlo), (glo, whi))):
                                for a, w in ((0, 512), (512, 256)):
                                    last = nc.tensor.matmul(banks(2 + 2 * u, DIM)[:, a:a + w], g[:, u, k, :],
                                                            w_[:, ds(slot, 1), k, a:a + w].rearrange("p o n -> p (o n)"),
                                                            start=(k == 0 and n == 0), stop=(k == KD - 1 and n == 2))
                        last.then_inc(s_mt, 1)

                    tiles = pairs(pe)
                    turn(0, 16, 0)
                    with pe.Fori(0, TL // 2) as i:
                        with pe.If(i * 2 < tiles):
                            turn(i * 2 + 1, i * 16 + 16, 1)
                            multiply(i * 2, 0)
                            turn(i * 2 + 2, i * 16 + 32, 0)
                            multiply(i * 2 + 1, 1)

        with ExitStack() as st:
            sb = holder(st)
            RING = 2 * GT
            mg = sb("mg", [P, RING, DIM])
            mhi = sb("mhi", [P, GT, DIM], f32r)
            mlo = sb("mlo", [P, GT, DIM], f32r)
            hotd = sb("hotd", [P, GT, P], f32r)
            midx = sb("midx", [P, RING, 1], i32)
            s_mg = [sem(f"messages_in{u}") for u in range(RING)]
            s_ix, s_mh, s_ml, s_us, s_ad = (sem(n) for n in (
                "slots_staged", "messages_hi", "messages_lo", "messages_used", "sum_added"))

            with nc.Block() as block:
                def pairs(eng):
                    return eng.value_load(n_groups[0:1, 0:1], min_val=0, max_val=GROUPS)

                @block.gpsimd
                def _(pool):
                    groups = pairs(pool)
                    with pool.Fori(0, GROUPS // 2) as i:
                        with pool.If(i * 2 < groups):
                            for u in range(RING):
                                t = i * RING + u
                                pool.wait_ge(s_ml, t + 1)
                                nc.gpsimd.tensor_copy(midx[:, u, :], slot_of[:, ds(t, 1)]).then_inc(s_ix, 1)
                                pool.wait_ge(s_ix, t + 1)
                                pool.sem_inc(s_go, 1)
                                pool.indirect_dma_start(mg[:, u, :], None, msg_dram,
                                                        bass.IndirectOffsetOnAxis(midx[:, u, :], 0)).then_inc(s_mg[u], 16)

                @block.scalar
                def _(act):
                    groups = pairs(act)
                    with act.Fori(0, GROUPS // 2) as i:
                        with act.If(i * 2 < groups):
                            for u in range(RING):
                                act.wait_ge(s_mg[u], i * 16 + 16)
                                act.wait_ge(s_us, i * RING + (u + 1))
                                nc.scalar.activation(mhi[:, u % GT, :], mg[:, u, :], ACT.Identity,
                                                     scale=weight[:, ds(i * RING + u, 1)]).then_inc(s_mh, 1)

                @block.vector
                def _(dve):
                    v = nc.vector
                    groups = pairs(dve)
                    with dve.Fori(0, GROUPS // 2) as i:
                        with dve.If(i * 2 < groups):
                            for u in range(RING):
                                t = i * RING + u
                                dve.wait_ge(s_us, t + 1)
                                v.tensor_scalar(hotd[:, u % GT, :], iota16[:, 0:P], etab[:, ds(t, 1), F_DLOC], None, ALU.is_equal)
                                dve.wait_ge(s_mh, t + 1)
                                v.scalar_tensor_tensor(mlo[:, u % GT, :], mg[:, u, :], weight[:, ds(t, 1)],
                                                       mhi[:, u % GT, :].bitcast(f32), ALU.mult, ALU.subtract).then_inc(s_ml, 1)
                            for g in range(2):
                                at = dve.value_load(group_tile[0:1, ds(i * 2 + g, 1)], min_val=0, max_val=NT - 1)
                                dve.wait_ge(s_us, i * RING + (GT * (g + 1) + GT))
                                dve.wait_ge(s_ad, i * 2 + (g + 2))
                                a = acc[:, ds(at, 1), :].rearrange("p o c -> p (o c)")
                                v.tensor_tensor(a, a, banks(2 * g, DIM), ALU.add).then_inc(s_ad, 1)

                @block.tensor
                def _(pe):
                    pe.sem_inc(s_us, GT)
                    pe.sem_inc(s_ml, RING)
                    pe.sem_inc(s_ad, 2)
                    groups = pairs(pe)
                    with pe.Fori(0, GROUPS // 2) as i:
                        with pe.If(i * 2 < groups):
                            for g in range(2):
                                pe.wait_ge(s_ad, i * 2 + (g + 1))
                                for q in range(GT):
                                    pe.wait_ge(s_ml, i * RING + (g * GT + q + 1) + RING)
                                    for part in (mhi, mlo):
                                        for a, w in ((0, 512), (512, 256)):
                                            last = nc.tensor.matmul(banks(2 * g, DIM)[:, a:a + w], hotd[:, q, :], part[:, q, a:a + w],
                                                                    start=(q == 0 and part is mhi), stop=(q == GT - 1 and part is mlo))
                                    last.then_inc(s_us, 1)

        with ExitStack() as st:
            sb = holder(st)
            wg = sb("wg", [P, KD, DIM])
            cT = sb("cT", [P, 2, KD, P])
            Y = sb("Y", [P, NT, DIM])
            CT = sb("CT_again", [P, NT, NP])
            s_cti = sem("ct_again_in")
            bgrow = sb("bgrow", [P, DIM])
            s_wg, s_bg, s_self, s_res, s_fm, s_fo = (sem(n) for n in (
                "wgcn_in", "bgcn_in", "self_edges", "residual", "sums_done", "rows_ready"))
            pj4 = Projection("wgcn", KD, [512, 256])

            with nc.Block() as block:
                @block.sync
                def _(sp):
                    sp.dma_start(wg[:, :, :], Wgcn.rearrange("(k p) o -> p k o", p=P)).then_inc(s_wg, 16)
                    sp.dma_start(bgrow[:, :], vector_row(bgcn, DIM)).then_inc(s_bg, 16)
                    sp.dma_start(CT[:, :, :].rearrange("p k d -> p (k d)"), ct_dram).then_inc(s_cti, 16)
                    for j in range(NT):
                        n = P if j < NT - 1 else LAST
                        sp.wait_ge(s_fo, j + 1)
                        sp.dma_start(out[j * P:j * P + n, :], x2[:n, j, :]).then_inc(s_moved, 16)
                    all_moved(sp, NT)

                @block.scalar
                def _(act):
                    project_act(act, pj4, cT)

                @block.vector
                def _(dve):
                    v = nc.vector
                    dve.wait_ge(s_bg, 16)
                    for j in range(NT):
                        v.tensor_tensor(x2[:, j, :], x2[:, j, :], bgrow[:, :], ALU.add).then_inc(s_res, 1)
                    for j in range(NT):
                        dve.wait_ge(pj4.multiplied, j + 1)
                        v.tensor_scalar(Y[:, j, :], banks(2 + 3 * (j % 2), DIM), dinv[:, j:j + 1], None, ALU.mult).then_inc(pj4.taken, 1)
                    dve.wait_ge(s_cti, 16)
                    for k in range(NT):
                        v.tensor_tensor(CT[:, k, k * P:(k + 1) * P], CT[:, k, k * P:(k + 1) * P], ident[:, :], ALU.add).then_inc(s_self, 1)
                    dve.wait_ge(s_res, NT)
                    for j in range(NT):
                        dve.wait_ge(s_fm, j + 1)
                        v.scalar_tensor_tensor(x2[:, j, :], banks(2 * (j % 4), DIM), dinv[:, j:j + 1], x2[:, j, :], ALU.mult, ALU.add).then_inc(s_fo, 1)

                @block.tensor
                def _(pe):
                    pe.wait_ge(s_wg, 16)
                    project_pe(pe, pj4, lambda j: acc[:, j, :], (s_wg, lambda j: 16), cT, wg)
                    pe.wait_ge(s_self, NT)
                    pe.wait_ge(pj4.taken, NT)
                    for j in range(NT):
                        if j >= 4:
                            pe.wait_ge(s_fo, j - 3)
                        for k in range(NT):
                            for a, w in ((0, 512), (512, 256)):
                                last = nc.tensor.matmul(banks(2 * (j % 4), DIM)[:, a:a + w], CT[:, k, j * P:(j + 1) * P],
                                                        Y[:, k, a:a + w], start=(k == 0), stop=(k == NT - 1))
                        last.then_inc(s_fm, 1)


_INS = ['x', 'src', 'dst', 'edge_type_34', 'L0_gnn_W1', 'L0_gnn_att_src1', 'L0_gnn_att_dst1', 'L0_gnn_b1',
        'L0_gnn_W2', 'L0_gnn_att_src2', 'L0_gnn_att_dst2', 'L0_gnn_b2', 'L1_gnn_W_rel', 'L1_gnn_W_root',
        'L1_gnn_b_rgcn', 'L1_gnn_W_gcn', 'L1_gnn_b_gcn']


def kernel(**inputs):
    import numpy as _np
    import concourse.bacc as _bacc
    from concourse import mybir as _mybir
    from concourse.bass_utils import run_bass_kernel_spmd as _run

    nc = _bacc.Bacc("TRN2", target_bir_lowering=False, num_devices=1)
    arrays, args = {}, []
    for name in _INS:
        a = _np.ascontiguousarray(inputs[name])
        arrays[f"in_{name}_dram"] = a
        args.append(nc.dram_tensor(f"in_{name}_dram", a.shape, _mybir.dt.from_np(a.dtype), kind="ExternalInput").ap())
    args.append(nc.dram_tensor("out_0_dram", (NODES, DIM), _mybir.dt.float32, kind="ExternalOutput").ap())
    gnn_kernel(nc, *args)
    r = _run(nc, [arrays], core_ids=[0])
    return r.results[0]["out_0_dram"]
```

```python
import concourse.bass as bass
from concourse import mybir
from contextlib import ExitStack


P = 128
NODES = 1250
DIM = 768
EDGES = 20000
HEADS, HEAD_DIM = 8, 128
RELATIONS = 34
NEG_SLOPE = 0.2
SOFTMAX_EPS = 1e-16
LN_EPS = 1e-5
NEGATIVE = -1e30
BIG = 3e38

NT = -(-NODES // P)
LAST = NODES - (NT - 1) * P
NP = NT * P
KD = DIM // P
HID = HEADS * HEAD_DIM
KH = HID // P
HCOLS = HEAD_DIM + 1

EP, EC = 125, EDGES // 125
REL_TILES = (EDGES - RELATIONS) // P + 1 + RELATIONS
REL_TILES += REL_TILES % 2
REL_ROOM = REL_TILES + NT
SB = 8
GT = 4
GROUPS = (EDGES - NT) // (GT * P) + 1 + NT
GROUPS += -GROUPS % 4
DST_TILES = GROUPS * GT
F_SRC, F_DLOC, F_REL, F_DREL, FIELDS = 0, 1, 2, 3, 4
TABLE_COLS = -(-REL_TILES // P)
CC = NP + RELATIONS


def gnn_kernel(nc, x, src, dst, etype, W1, as1, ad1, b1, W2, as2, ad2, b2,
               Wrel, Wroot, brg, Wgcn, bgcn, out):
    f32, bf16, i32, i16 = mybir.dt.float32, mybir.dt.bfloat16, mybir.dt.int32, mybir.dt.int16
    f32r = mybir.dt.float32r
    ALU, ACT, AX = mybir.AluOpType, mybir.ActivationFunctionType, mybir.AxisListType
    ds = bass.ds

    def dram(name, shape, dt=f32):
        return nc.dram_tensor(name, shape, dt, kind="Internal").ap()

    dst_table = dram("dst_table", (DST_TILES * P, FIELDS))
    slot_table = dram("slot_table", (NP * RELATIONS, 1))
    uv_rows = dram("uv_rows", (2 * HEADS * NT, P))
    m_rows = dram("m_rows", (HEADS * NT, P))
    uv2_rows = dram("uv2_rows", (2 * NT, P))
    m2_rows = dram("m2_rows", (NT, P))
    inv_count = dram("inv_count", (NP * RELATIONS, 1))
    h1_dram = dram("h1_dram", (NP, HID))
    h_dram = dram("h_dram", (NP, DIM))
    ct_dram = dram("ct_dram", (P, NT * NP))
    msg_dram = dram("msg_dram", (REL_TILES * P, DIM))

    def row_of(rows, r):
        return rows[r * NT:(r + 1) * NT, :].rearrange("(o a) b -> o (a b)", o=1).to_broadcast([P, NP])

    def vector_row(v, n):
        return v.rearrange("(o n) -> o n", o=1).to_broadcast([P, n])

    top = ExitStack()
    with top:
        def holder(stack):
            def sb(name, shape, dt=f32):
                return stack.enter_context(nc.sbuf_tensor(name, shape, dt))
            return sb

        def sem(name):
            return top.enter_context(nc.semaphore(name))

        keep = holder(top)
        PS = top.enter_context(nc.psum_tensor("PS", [P, 8, 512], f32))
        PSf = PS[:, :, :].rearrange("p b n -> p (b n)")

        def banks(b, n):
            return PSf[:, b * 512:b * 512 + n]

        iota = keep("iota", [P, P])
        iota16 = keep("iota16", [P, NP], i16)
        pidx = keep("pidx", [P, 1])
        ident = keep("ident", [P, P])
        tri = keep("tri", [P, P])
        ones = keep("ones", [P, P])
        eps_ln = keep("eps_ln", [P, 1])
        region_x = keep("region_x", [P, NT * DIM])
        region_h = keep("region_h", [P, NT * HEADS * HCOLS])
        dinv = keep("dinv", [P, NT])
        etab = keep("etab", [P, DST_TILES, FIELDS])
        rtab = keep("rtab", [P, REL_ROOM])
        pair_tile = keep("pair_tile", [P, NT, RELATIONS], bf16)
        pair_place = keep("pair_place", [P, NT, RELATIONS], bf16)
        rel_base = keep("rel_base", [1, RELATIONS], i32)
        slot_flat = keep("slot_flat", [P, DST_TILES])
        slot_of = keep("slot_of", [P, DST_TILES], i32)
        tile_rel = keep("tile_rel", [1, REL_TILES], i32)
        next_rel = keep("next_rel", [1, REL_TILES], i32)
        n_rel_tiles = keep("n_rel_tiles", [1, 1], i32)
        n_groups = keep("n_groups", [1, 1], i32)
        group_tile = keep("group_tile", [1, GROUPS + 1], i32)
        pos_dst = keep("pos_dst", [P, EC], i32)
        weight = keep("weight", [P, DST_TILES])
        uv = keep("uv", [P, 2 * HEADS, NT])
        uv2 = keep("uv2", [P, 2, NT])
        x_sb = region_x[:, :].rearrange("p (j i) -> p j i", i=DIM)
        x2 = x_sb
        mask = region_x[:, 0:NT * NP // 2].bitcast(bf16).rearrange("p (j s) -> p j s", s=NP)
        hA = region_h[:, :].rearrange("p (j h c) -> p j h c", h=HEADS, c=HCOLS)
        hB = region_h[:, 0:NT * (DIM + 1)].rearrange("p (j c) -> p j c", c=DIM + 1)
        acc = region_h[:, 0:NT * DIM].rearrange("p (j c) -> p j c", c=DIM)

        s_chain, links = sem("dve_chain"), [0]

        def chain(dve):
            def link(ins):
                links[0] += 1
                ins.then_inc(s_chain, 1)
                dve.wait_ge(s_chain, links[0])
            return link

        s_turned, s_rows = sem("rows_turned"), sem("rows_moved")
        s_biases = sem("bias_rows_in")
        s_pad = sem("x_pad")
        s_sqrt = sem("sqrt_ready")

        s_go = sem("gather_go")

        s_go_sp = sem("sync_go")

        s_moved, moves = sem("sync_dma_done"), [0]

        def all_moved(sp, n):
            moves[0] += n
            sp.wait_ge(s_moved, 16 * moves[0])

        def scatter_all(pool, table, rows, slots, stage_row, stage_idx, done, staged):
            def send(c, half):
                nc.gpsimd.tensor_copy(stage_row[:EP, half, :, :], rows[:EP, ds(c * SB, SB), :])
                nc.gpsimd.tensor_copy(stage_idx[:EP, half, :], slots[:EP, ds(c * SB, SB)]).then_inc(staged, 1)
                pool.wait_ge(staged, c + 1)
                pool.sem_inc(s_go, 1)
                for u in range(SB):
                    pool.indirect_dma_start(table, bass.IndirectOffsetOnAxis(stage_idx[:EP, half, u:u + 1], 0),
                                            stage_row[:EP, half, u, :], None).then_inc(done[half], 16)

            for half in range(2):
                send(half, half)
            with pool.Fori(1, EC // SB // 2) as i:
                for half in range(2):
                    pool.wait_ge(done[half], i * (16 * SB))
                    pool.sem_inc(s_go, 1)
                    send(i * 2 + half, half)
            for half in range(2):
                pool.wait_ge(done[half], EC * 8)

        def walk_columns(pool, groups, issue, collect, done):
            for half in range(2):
                issue(half, half)
            with pool.Fori(1, GROUPS // 4) as i:
                with pool.If(i * 4 < groups):
                    for half in range(2):
                        pool.wait_ge(done[half], i * (16 * SB))
                        pool.sem_inc(s_go, 1)
                        collect(i * 2 + (half - 2), half)
                        issue(i * 2 + half, half)
            steps = pool.snap((groups + 3) // 4)
            for half in range(2):
                pool.wait_ge(done[half], steps * (16 * SB))
                pool.sem_inc(s_go, 1)
                collect(steps * 2 + (half - 2), half)

        class Projection:
            def __init__(self, tag, k, widths):
                self.k, self.widths = k, widths
                self.turned = sem(tag + "_tile_turned")
                self.moved = sem(tag + "_tile_moved")
                self.multiplied = sem(tag + "_tile_multiplied")
                self.taken = sem(tag + "_tile_taken")

        def project_pe(pe, pj, source, input_ready, xT, rhs, beside=None):
            def turn(j):
                ready = input_ready[0]
                pe.wait_ge(ready[j % 2] if isinstance(ready, list) else ready, input_ready[1](j))
                if j:
                    pe.wait_ge(pj.moved, j)
                for k in range(pj.k):
                    last = nc.tensor.transpose(banks(0, 1024)[:, k * P:(k + 1) * P],
                                               source(j)[:, k * P:(k + 1) * P], ident[:, :])
                last.then_inc(pj.turned, 1)

            turn(0)
            for j in range(NT):
                if j + 1 < NT:
                    turn(j + 1)
                pe.wait_ge(pj.moved, j + 1)
                if j >= 2:
                    pe.wait_ge(pj.taken, j - 1)
                for k in range(pj.k):
                    at = 0
                    for w in pj.widths:
                        last = nc.tensor.matmul(banks(2 + 3 * (j % 2), 1536)[:, at:at + w],
                                                xT[:, j % 2, k, :], rhs[:, k, at:at + w],
                                                start=(k == 0), stop=(k == pj.k - 1))
                        at += w
                last.then_inc(pj.multiplied, 1)
                if beside is not None:
                    beside(j)

        def project_act(act, pj, xT, move=None):
            for j in range(NT):
                act.wait_ge(pj.turned, j + 1)
                if j >= 2:
                    act.wait_ge(pj.multiplied, j - 1)
                if move is None:
                    nc.scalar.copy(xT[:, j % 2, 0:pj.k, :].rearrange("p k n -> p (k n)"),
                                   banks(0, pj.k * P)).then_inc(pj.moved, 1)
                else:
                    move(j).then_inc(pj.moved, 1)

        class SplitProjection(Projection):
            def __init__(self, tag, k, widths):
                super().__init__(tag, k, widths)
                self.high = sem(tag + "_tile_high")

        def split_weights_high(act, raw, hi, ready):
            for k in range(0, KD, 2):
                nc.scalar.copy(hi[:, k:k + 2, :].rearrange("p k n -> p (k n)"),
                               raw[:, k:k + 2, :].rearrange("p k n -> p (k n)")).then_inc(ready, 1)

        def split_weights_low(dve, raw, hi, lo, high_ready, ready):
            for k in range(0, KD, 2):
                dve.wait_ge(high_ready, k // 2 + 1)
                last = nc.vector.tensor_tensor(lo[:, k:k + 2, :].rearrange("p k n -> p (k n)"),
                                               raw[:, k:k + 2, :].rearrange("p k n -> p (k n)"),
                                               hi[:, k:k + 2, :].rearrange("p k n -> p (k n)").bitcast(f32), ALU.subtract)
            last.then_inc(ready, 1)

        def split_project_pe(pe, pj, source, input_ready, xhi, xlo, whi, wlo):
            def turn(j):
                pe.wait_ge(input_ready[0], input_ready[1](j))
                if j:
                    pe.wait_ge(pj.moved, j)
                for k in range(pj.k):
                    last = nc.tensor.transpose(banks(0, 1024)[:, k * P:(k + 1) * P],
                                               source(j)[:, k * P:(k + 1) * P], ident[:, :])
                last.then_inc(pj.turned, 1)

            turn(0)
            for j in range(NT):
                if j + 1 < NT:
                    turn(j + 1)
                pe.wait_ge(pj.moved, j + 1)
                if j >= 2:
                    pe.wait_ge(pj.taken, j - 1)
                for k in range(pj.k):
                    for n, (x_, w_) in enumerate(((xhi, whi), (xhi, wlo), (xlo, whi))):
                        at = 0
                        for w in pj.widths:
                            last = nc.tensor.matmul(banks(2 + 3 * (j % 2), 1536)[:, at:at + w],
                                                    x_[:, j % 2, k, :], w_[:, k, at:at + w],
                                                    start=(k == 0 and n == 0), stop=(k == pj.k - 1 and n == 2))
                            at += w
                last.then_inc(pj.multiplied, 1)

        def move_high(act, pj, xhi, j):
            act.wait_ge(pj.turned, j + 1)
            if j >= 2:
                act.wait_ge(pj.multiplied, j - 1)
            nc.scalar.copy(xhi[:, j % 2, :, :].rearrange("p k n -> p (k n)"), banks(0, pj.k * P)).then_inc(pj.high, 1)

        def move_low(dve, pj, xhi, xlo, j):
            dve.wait_ge(pj.high, j + 1)
            nc.vector.tensor_tensor(xlo[:, j % 2, :, :].rearrange("p k n -> p (k n)"), banks(0, pj.k * P),
                                    xhi[:, j % 2, :, :].rearrange("p k n -> p (k n)").bitcast(f32),
                                    ALU.subtract).then_inc(pj.moved, 1)

        with ExitStack() as st:
            sb = holder(st)
            w1 = sb("w1", [P, HEADS, DIM])
            attc = sb("attc", [P, HEADS, 2])
            w1T = sb("w1T", [P, KD, HID + 2 * HEADS])
            h0T = sb("h0T", [P, 2, KD, P])
            stats = sb("stats", [P, NT, 2, 6])
            mv = sb("mv", [P, NT, 2])
            rstd = sb("rstd", [P, NT])
            nmr = sb("nmr", [P, NT])
            rows_sb = sb("rows_sb", [80, 2, P])

            s_const, s_ids, s_x, s_w1, s_att = (sem(n) for n in
                                                ("const", "ids", "x_in", "w1_in", "att_in"))
            s_w1t, s_w1e, s_wa, s_mv, s_ln, s_h0 = (sem(n) for n in (
                "w1_turned", "w1_moved", "att_folded", "ln_stats", "ln_scale", "h0"))
            s_tot, s_pref, s_tabs, s_pad_rows = (sem(n) for n in
                                             ("bucket_tot", "bucket_prefix", "tables_blank", "pad_rows"))
            s_pos, s_stage = (sem(n) for n in ("edge_pos", "edge_staged"))
            s_scat = [sem(f"dst_scattered{u}") for u in range(2)]
            pj = Projection("w1", KD, [512, 512, 2 * HEADS])

            with ExitStack() as st2:
                sb2 = holder(st2)
                ids = sb2("ids", [P, 3, EC], i32)
                cut = sb2("cut", [P, 2, EC], i32)
                keyd = sb2("keyd", [P, EC])
                keyx = sb2("keyx", [P, EC])
                edge0 = sb2("edge0", [P, 3], i32)
                pad_row = sb2("pad_row", [P, FIELDS])
                fields = sb2("fields", [P, EC, FIELDS])
                hot = sb2("hot", [P, NT, EC])
                run = sb2("run", [P, NT, EC])
                before = sb2("before", [P, NT])
                tot = sb2("tot", [P, NT])
                tiles = sb2("tiles", [P, NT])
                tilesi = sb2("tilesi", [P, NT], i32)
                base = sb2("base", [P, NT])
                off = sb2("off", [P, NT])
                cmpr = sb2("cmpr", [1, GROUPS])
                cmps = sb2("cmps", [1, GROUPS, NT])
                blank = sb2("blank", [P, DST_TILES, FIELDS])
                stage_row = sb2("stage_row", [P, 2, SB, FIELDS])
                stage_idx = sb2("stage_idx", [P, 2, SB], i32)

                with nc.Block() as block:
                    @block.sync
                    def _(sp):
                        for n, v in enumerate((src, dst, etype)):
                            sp.dma_start(ids[:EP, n, :], v.rearrange("(p c) -> p c", c=EC)).then_inc(s_ids, 16)
                        for n, v in enumerate((src, dst, etype)):
                            sp.dma_start(edge0[:, n:n + 1], v[0:1].rearrange("(o n) -> o n", o=1).to_broadcast([P, 1])).then_inc(s_ids, 16)
                        sp.wait_ge(s_pad_rows, 1)
                        sp.dma_start(dst_table.rearrange("(p a) f -> p (a f)", p=P),
                                     blank[:, :, :].rearrange("p a f -> p (a f)")).then_inc(s_tabs, 16)
                        sp.dma_start(w1[:, :, :], W1.rearrange("(h c) i -> c h i", c=P)).then_inc(s_w1, 16)
                        with nc.allow_non_contiguous_dma(reason="attention vectors as columns"):
                            sp.dma_start(attc[:, :, 0], as1.rearrange("h c -> c h")).then_inc(s_att, 16)
                            sp.dma_start(attc[:, :, 1], ad1.rearrange("h c -> c h")).then_inc(s_att, 16)
                        sp.dma_start(x_sb[:, 0:NT - 1, :], x[0:(NT - 1) * P, :].rearrange("(j p) i -> p j i", p=P)).then_inc(s_x, 16)
                        sp.wait_ge(s_pad, 1)
                        sp.dma_start(x_sb[:LAST, NT - 1, :], x[(NT - 1) * P:NODES, :]).then_inc(s_x, 16)
                        sp.wait_ge(s_rows, 2)
                        for c in range(2):
                            sp.dma_start(uv_rows[80 * c:80 * c + 80, :], rows_sb[:, c, :]).then_inc(s_moved, 16)
                        all_moved(sp, 2)

                    @block.gpsimd
                    def _(pool):
                        pool.memset(x_sb[:, NT - 1, :], 0.0).then_inc(s_pad, 1)
                        pool.iota(iota16[:, :], [[1, NP]], base=0, channel_multiplier=0).then_inc(s_const, 1)
                        pool.iota(iota[:, :], [[1, P]], base=0, channel_multiplier=0,
                                  allow_small_or_imprecise_dtypes=True).then_inc(s_const, 1)
                        pool.iota(pidx[:, :], [[1, 1]], base=0, channel_multiplier=1,
                                  allow_small_or_imprecise_dtypes=True).then_inc(s_const, 1)
                        pool.wait_ge(s_tabs, 16)
                        pool.wait_ge(s_pos, 1)
                        scatter_all(pool, dst_table, fields, pos_dst, stage_row, stage_idx, s_scat, s_stage)

                    @block.scalar
                    def _(act):
                        act.wait_ge(s_const, 3)
                        act.wait_ge(s_w1, 16)
                        for g in range(2 * KD):
                            act.wait_ge(s_w1t, g + 1)
                            nc.scalar.copy(w1T[:, g // 2, 512 * (g % 2):512 * (g % 2) + 512],
                                           banks(g % 2, 512)).then_inc(s_w1e, 1)
                        act.wait_ge(s_wa, 1)
                        nc.scalar.copy(w1T[:, :, HID:], banks(2, 16 * KD).rearrange("p (k c) -> p k c", k=KD)).then_inc(s_w1e, 1)
                        act.wait_ge(s_mv, 1)
                        nc.scalar.activation(rstd[:, :], mv[:, :, 1], ACT.Sqrt, bias=eps_ln[:, :]).then_inc(s_sqrt, 1)
                        act.wait_ge(s_ln, 1)
                        for j in range(NT):
                            nc.scalar.activation(x_sb[:, j, :], x_sb[:, j, :], ACT.Relu, bias=nmr[:, j:j + 1],
                                                 scale=rstd[:, j:j + 1]).then_inc(s_h0, 1)
                        project_act(act, pj, h0T)
                        for c in range(2):
                            act.wait_ge(s_turned, c + 1)
                            nc.scalar.copy(rows_sb[:, c, :], banks(c, P)[:80, :]).then_inc(s_rows, 1)

                    @block.vector
                    def _(dve):
                        link = chain(dve)
                        v = nc.vector
                        v.memset(eps_ln[:, :], LN_EPS)
                        v.memset(hA[:, :, :, HEAD_DIM:], 1.0)
                        link(v.memset(ones[:, :], 1.0))
                        dve.wait_ge(s_const, 3)
                        v.tensor_scalar(tri[:, :], iota[:, 0:P], pidx[:, :], None, ALU.is_gt)
                        v.tensor_scalar(ident[:, :], iota[:, 0:P], pidx[:, :], None, ALU.is_equal).then_inc(s_const, 1)
                        dve.wait_ge(s_ids, 96)
                        v.tensor_single_scalar(cut[:EP, 0, :], ids[:EP, 1, :], 7, ALU.arith_shift_right)
                        link(v.tensor_single_scalar(cut[:EP, 1, :], ids[:EP, 1, :], P - 1, ALU.bitwise_and))
                        v.tensor_copy(keyd[:EP, :], cut[:EP, 0, :])
                        v.tensor_copy(fields[:EP, :, F_SRC], ids[:EP, 0, :])
                        v.tensor_copy(fields[:EP, :, F_DLOC], cut[:EP, 1, :])
                        v.tensor_copy(fields[:EP, :, F_REL], ids[:EP, 2, :])
                        v.tensor_copy(pad_row[:, F_SRC:F_SRC + 1], edge0[:, 0:1])
                        v.tensor_copy(pad_row[:, F_REL:F_REL + 1], edge0[:, 2:3])
                        v.tensor_copy(fields[:EP, :, F_DREL], ids[:EP, 1, :])
                        v.tensor_copy(pad_row[:, F_DREL:], edge0[:, 1:2])
                        link(v.memset(pad_row[:, F_DLOC:F_DLOC + 1], -1.0))
                        v.scalar_tensor_tensor(fields[:EP, :, F_DREL], fields[:EP, :, F_DREL], float(RELATIONS),
                                               fields[:EP, :, F_REL], ALU.mult, ALU.add)
                        link(v.scalar_tensor_tensor(pad_row[:, F_DREL:], pad_row[:, F_DREL:], float(RELATIONS),
                                                    pad_row[:, F_REL:F_REL + 1], ALU.mult, ALU.add))
                        v.tensor_copy(blank[:, :, :], pad_row[:, :].unsqueeze(1).to_broadcast([P, DST_TILES, FIELDS])).then_inc(s_pad_rows, 1)

                        def places(key, nb, unit_shift, pos):
                            h, r = hot[:EP, 0:nb, :], run[:EP, 0:nb, :]
                            link(v.tensor_tensor(h, key[:EP, :].unsqueeze(1).to_broadcast([EP, nb, EC]),
                                                 iota[:EP, 0:nb].unsqueeze(2).to_broadcast([EP, nb, EC]), ALU.is_equal))
                            hf, rf = h.rearrange("p b c -> p (b c)"), r.rearrange("p b c -> p (b c)")
                            link(v.tensor_tensor_scan(rf, hf, hf, 0.0, ALU.add, ALU.max))
                            link(v.memset(before[:EP, 0:1], 0.0))
                            link(v.tensor_copy(before[:EP, 1:nb], r[:, 0:nb - 1, EC - 1]))
                            v.tensor_tensor(tot[:EP, 0:nb], r[:, :, EC - 1], before[:EP, 0:nb], ALU.subtract).then_inc(s_tot, 1)
                            dve.wait_ge(s_pref, 1)
                            b = 3
                            link(v.tensor_scalar(tiles[:, 0:nb], banks(b, 128)[:, 64:64 + nb], float(2 ** unit_shift - 1), None, ALU.add))
                            link(v.tensor_copy(tilesi[:, 0:nb], tiles[:, 0:nb]))
                            link(v.tensor_single_scalar(tilesi[:, 0:nb], tilesi[:, 0:nb], unit_shift, ALU.arith_shift_right))
                            link(v.tensor_copy(tiles[:, 0:nb], tilesi[:, 0:nb]))
                            link(v.tensor_tensor_scan(base[:, 0:nb], tiles[:, 0:nb], tiles[:, 0:nb], 0.0, ALU.add, ALU.max))
                            link(v.tensor_tensor(base[:, 0:nb], base[:, 0:nb], tiles[:, 0:nb], ALU.subtract))
                            link(v.scalar_tensor_tensor(off[:EP, 0:nb], base[:EP, 0:nb], float(2 ** unit_shift),
                                                        banks(b, 64)[:EP, 0:nb], ALU.mult, ALU.add))
                            link(v.scalar_tensor_tensor(off[:EP, 0:nb], off[:EP, 0:nb], -1.0, before[:EP, 0:nb],
                                                        ALU.add, ALU.subtract))
                            link(v.tensor_tensor(r, r, off[:EP, 0:nb].unsqueeze(2).to_broadcast([EP, nb, EC]), ALU.add))
                            link(v.tensor_tensor(h, h, r, ALU.mult))
                            link(v.tensor_reduce(keyx[:EP, :], h.rearrange("p b c -> p c b"), AX.X, ALU.add))
                            link(v.tensor_copy(pos, keyx[:EP, :]))

                        def group_of(units, nb, result):
                            c = cmps[:, :, :]
                            link(v.tensor_tensor(c, base[0:1, 0:nb].unsqueeze(1).to_broadcast([1, units, nb]),
                                                 iota[0:1, 0:units].unsqueeze(2).to_broadcast([1, units, nb]), ALU.is_le))
                            link(v.tensor_reduce(cmpr[0:1, 0:units], c, AX.X, ALU.add))
                            link(v.tensor_scalar(cmpr[0:1, 0:units], cmpr[0:1, 0:units], -1.0, None, ALU.add))
                            link(v.tensor_copy(result, cmpr[0:1, 0:units]))

                        places(keyd, NT, 9, pos_dst[:EP, :])
                        v.tensor_single_scalar(cut[:EP, 0, :], pos_dst[:EP, :], 7, ALU.arith_shift_right)
                        link(v.tensor_single_scalar(cut[:EP, 1, :], pos_dst[:EP, :], P - 1, ALU.bitwise_and))
                        v.tensor_copy(keyd[:EP, :], cut[:EP, 0, :])
                        link(v.tensor_copy(keyx[:EP, :], cut[:EP, 1, :]))
                        link(v.scalar_tensor_tensor(keyx[:EP, :], keyx[:EP, :], float(DST_TILES), keyd[:EP, :], ALU.mult, ALU.add))
                        v.tensor_copy(pos_dst[:EP, :], keyx[:EP, :]).then_inc(s_pos, 1)
                        group_of(GROUPS, NT, group_tile[:, 1:])
                        link(v.tensor_tensor(off[0:1, 0:NT], base[0:1, 0:NT], tiles[0:1, 0:NT], ALU.add))
                        v.tensor_copy(n_groups[:, :], off[0:1, NT - 1:NT])
                        dve.wait_ge(s_x, 32)
                        for j in range(NT):
                            for c in range(2):
                                last = v.bn_stats(stats[:, j, c, :], x_sb[:, j, c * 384:(c + 1) * 384])
                        link(last)
                        for j in range(NT):
                            last = v.bn_aggr(mv[:, j, :], stats[:, j, :, :].rearrange("p a b -> p (a b)"))
                        last.then_inc(s_mv, 1)
                        dve.wait_ge(s_sqrt, 1)
                        link(v.reciprocal(rstd[:, :], rstd[:, :]))
                        v.scalar_tensor_tensor(nmr[:, :], mv[:, :, 0], -1.0, rstd[:, :], ALU.mult, ALU.mult).then_inc(s_ln, 1)


                        for j in range(NT):
                            dve.wait_ge(pj.multiplied, j + 1)
                            v.tensor_copy(hA[:, j, :, 0:HEAD_DIM],
                                          banks(2 + 3 * (j % 2), HID).rearrange("p (h c) -> p h c", h=HEADS))
                            v.tensor_copy(uv[:, :, j], banks(2 + 3 * (j % 2), HID + 2 * HEADS)[:, HID:]).then_inc(pj.taken, 1)

                    @block.tensor
                    def _(pe):
                        pe.wait_ge(s_const, 4)
                        pe.wait_ge(s_tot, 1)
                        nc.tensor.matmul(banks(3, 64)[:EP, 0:NT], tri[:EP, :EP], tot[:EP, 0:NT], start=True, stop=True)
                        nc.tensor.matmul(banks(3, 128)[:, 64:64 + NT], ones[:EP, :], tot[:EP, 0:NT],
                                         start=True, stop=True).then_inc(s_pref, 1)
                        pe.wait_ge(s_w1, 16)
                        for g in range(2 * KD):
                            if g >= 2:
                                pe.wait_ge(s_w1e, g - 1)
                            for u in range(4):
                                h = 4 * (g % 2) + u
                                last = nc.tensor.transpose(banks(g % 2, 512)[:, u * P:(u + 1) * P],
                                                           w1[:, h, (g // 2) * P:(g // 2 + 1) * P], ident[:, :])
                            last.then_inc(s_w1t, 1)
                        pe.wait_ge(s_att, 32)
                        for k in range(KD):
                            for h in range(HEADS):
                                last = nc.tensor.matmul(banks(2, 96)[:, k * 16 + 2 * h:k * 16 + 2 * h + 2],
                                                        w1[:, h, k * P:(k + 1) * P], attc[:, h, :], start=True, stop=True)
                        last.then_inc(s_wa, 1)
                        pe.wait_ge(s_w1e, 2 * KD + 1)
                        pe.wait_ge(s_pos, 1)
                        project_pe(pe, pj, lambda j: x_sb[:, j, :], (s_h0, lambda j: j + 1), h0T, w1T)
                        pe.wait_ge(pj.taken, NT)
                        for c in range(2):
                            nc.tensor.transpose(banks(c, P)[:80, :], uv[:, :, :].rearrange("p c j -> p (c j)")[:, 80 * c:80 * c + 80],
                                                ident[:, :]).then_inc(s_turned, 1)

        counts_life = ExitStack()
        CT = holder(counts_life)("CT", [P, NT, NP])
        with ExitStack() as st:
            sb = holder(st)
            C = sb("C", [P, NT, CC])
            with ExitStack() as st2:
                sb2 = holder(st2)
                hot_src = sb2("hot_src", [P, GT, CC], bf16)
                hot_dst = sb2("hot_dst", [P, GT, P], bf16)
                far_dst = sb2("far_dst", [P, GT, P], bf16)
                inv = region_x[:, NT * DIM - NT * RELATIONS:].rearrange("p (j r) -> p j r", r=RELATIONS)
                deg = sb2("deg", [P, NT])
                zero16 = sb2("zero16", [P, NT * RELATIONS], bf16)
                present = sb2("present", [P, NT, RELATIONS])
                slots = sb2("slots", [P, NT, RELATIONS])
                in_tile = sb2("in_tile", [P, NT, RELATIONS])
                n_rel = sb2("n_rel", [P, RELATIONS])
                rtiles = sb2("rtiles", [P, RELATIONS])
                rtilesi = sb2("rtilesi", [P, RELATIONS], i32)
                rbase = sb2("rbase", [P, RELATIONS])
                pairi = region_x[:, NT * NP // 2:NT * NP // 2 + 2 * NT * RELATIONS].bitcast(i32).rearrange(
                    "p (o j r) -> p o j r", o=2, r=RELATIONS)
                started = sb2("started", [P, TABLE_COLS, RELATIONS])
                n_started = sb2("n_started", [P, TABLE_COLS])
                trel = sb2("trel", [1, REL_TILES])
                first = sb2("first", [1, REL_TILES])
                s_counts = sem("counts_done")
                s_et, s_z16, s_c0, s_far, s_hotd, s_hot, s_used, s_add = (sem(n) for n in (
                    "etab_in", "zeros_ready", "counts_blank", "distances", "dst_hot_ready", "hot_ready", "hot_used", "group_added"))
                s_tables, s_cT, s_cTe, s_deg = (sem(n) for n in (
                    "tables_ready", "ct_turned", "ct_moved", "deg_ready"))

                s_pc, s_pres, s_rpre, s_rn, s_trel = (sem(n) for n in (
                    "pairs_counted", "pairs_present", "pairs_prefix", "rel_sizes_used", "tile_rel_turned"))

                with nc.Block() as block:
                    @block.sync
                    def _(sp):
                        sp.dma_start(etab[:, :, :], dst_table.rearrange("(p t) f -> p t f", p=P)).then_inc(s_et, 16)
                        sp.wait_ge(s_tables, 1)
                        sp.dma_start(inv_count.rearrange("(j p r) o -> p j (r o)", p=P, r=RELATIONS), inv[:, :, :]).then_inc(s_moved, 16)
                        sp.wait_ge(s_tables, 2)
                        sp.dma_start(slot_table.rearrange("(j p r) o -> p j (r o)", p=P, r=RELATIONS), slots[:, :, :]).then_inc(s_moved, 16)
                        all_moved(sp, 2)

                    @block.gpsimd
                    def _(pool):
                        pool.memset(C[:, :, :].rearrange("p j c -> p (j c)"), 0.0).then_inc(s_c0, 1)

                    @block.scalar
                    def _(act):
                        act.wait_ge(s_et, 16)
                        groups = act.value_load(n_groups[0:1, 0:1], min_val=0, max_val=GROUPS)
                        with act.Fori(0, GROUPS // 2) as i:
                            with act.If(i * 2 < groups):
                                for g in range(2):
                                    def distances(u):
                                        e = etab[:, ds(i * (2 * GT) + u, 1), :].rearrange("p o f -> p (o f)")
                                        nc.scalar.activation(far_dst[:, u % GT, :], iota[:, :], ACT.Abs,
                                                             bias=e[:, F_DLOC:F_DLOC + 1], scale=-1.0).then_inc(s_far, 1)

                                    act.wait_ge(s_hotd, i * (2 * GT) + (g * GT + 1))
                                    for q in range(GT):
                                        distances(g * GT + q)
                                    for q in range(GT):
                                        t = i * (2 * GT) + (g * GT + q)
                                        act.wait_ge(s_far, t + 1)
                                        act.wait_ge(s_used, t + 1)
                                        nc.scalar.activation(hot_dst[:, q, :], far_dst[:, q, :], ACT.Relu,
                                                             bias=ones[:, 0:1], scale=-1.0).then_inc(s_hotd, 1)
                        act.wait_ge(s_deg, 1)
                        nc.scalar.activation(deg[:, :], deg[:, :], ACT.Sqrt).then_inc(s_sqrt, 1)
                        for k in range(NT):
                            act.wait_ge(s_cT, k + 1)
                            nc.scalar.copy(CT[:, k, :], banks(3 * (k % 2), NP)).then_inc(s_cTe, 1)

                    @block.vector
                    def _(dve):
                        v = nc.vector
                        link = chain(dve)
                        v.memset(zero16[:, :], 0.0).then_inc(s_z16, 1)
                        dve.wait_ge(s_et, 16)
                        v.memset(rtab[:, :], 0.0)
                        v.scalar_tensor_tensor(slot_flat[:, :], etab[:, :, F_SRC], float(RELATIONS), etab[:, :, F_REL],
                                               ALU.mult, ALU.add)
                        groups = dve.value_load(n_groups[0:1, 0:1], min_val=0, max_val=GROUPS)

                        def add(n1, used, added, g):
                            at = dve.value_load(group_tile[0:1, ds(n1, 1)], min_val=0, max_val=NT - 1)
                            dve.wait_ge(s_used, used)
                            dve.wait_ge(s_add, added)
                            c = C[:, ds(at, 1), :].rearrange("p o c -> p (o c)")
                            v.tensor_tensor(c, c, banks(3 * g, CC), ALU.add).then_inc(s_add, 1)

                        with dve.Fori(0, GROUPS // 2) as i:
                            with dve.If(i * 2 < groups):
                                for u in range(2 * GT):
                                    t = i * (2 * GT) + u
                                    dve.wait_ge(s_used, t + 1)
                                    e = etab[:, ds(t, 1), :].rearrange("p o f -> p (o f)")
                                    v.tensor_scalar(hot_src[:, u % GT, 0:NP], iota16[:, :], e[:, F_SRC:F_SRC + 1], None, ALU.is_equal)
                                    v.tensor_scalar(hot_src[:, u % GT, NP:], iota16[:, 0:RELATIONS], e[:, F_REL:F_REL + 1], None,
                                                    ALU.is_equal).then_inc(s_hot, 1)
                                    if u == GT - 1:
                                        with dve.If(i > 0):
                                            add(i * 2, i * (2 * GT) + GT, i * 2 + 1, 1)
                                dve.wait_ge(s_c0, 1)
                                add(i * 2 + 1, i * (2 * GT) + 2 * GT, i * 2 + 2, 0)
                        both = dve.snap((groups + 1) // 2)
                        add(both * 2, both * (2 * GT) + GT, both * 2 + 1, 1)
                        dve.wait_ge(s_add, both * 2 + 2)
                        dve.sem_inc(s_counts, 1)
                        dve.wait_ge(s_pc, 1)
                        v.tensor_scalar(present[:, :, :].rearrange("p j r -> p (j r)"), banks(6, NT * RELATIONS), 0.0, None,
                                        ALU.is_gt).then_inc(s_pres, 1)
                        link(v.tensor_scalar(inv[:, :, :], C[:, :, NP:], 1.0, None, ALU.max))
                        v.reciprocal(inv[:, :, :], inv[:, :, :]).then_inc(s_tables, 1)
                        link(v.tensor_reduce(deg[:, :], C[:, :, 0:NP], AX.X, ALU.add))
                        v.tensor_scalar(deg[:, :], deg[:, :], 1.0, None, ALU.add).then_inc(s_deg, 1)
                        dve.wait_ge(s_rpre, 1)
                        link(v.tensor_copy(in_tile[:, :, :].rearrange("p j r -> p (j r)"), banks(6, NT * RELATIONS)))
                        link(v.memset(slots[:, 0, :], 0.0))
                        for j in range(1, NT):
                            link(v.tensor_tensor(slots[:, j, :], slots[:, j - 1, :], in_tile[:, j - 1, :], ALU.add))
                        link(v.tensor_tensor(n_rel[:, :], slots[:, NT - 1, :], in_tile[:, NT - 1, :], ALU.add))
                        link(v.tensor_scalar(rtiles[:, :], n_rel[:, :], float(P - 1), None, ALU.add))
                        link(v.tensor_copy(rtilesi[:, :], rtiles[:, :]))
                        link(v.tensor_single_scalar(rtilesi[:, :], rtilesi[:, :], 7, ALU.arith_shift_right))
                        link(v.tensor_copy(rtiles[:, :], rtilesi[:, :]))
                        link(v.tensor_scalar(rtiles[:, :], rtiles[:, :], 1.0, None, ALU.max))
                        link(v.tensor_tensor_scan(rbase[:, :], rtiles[:, :], rtiles[:, :], 0.0, ALU.add, ALU.max))
                        link(v.tensor_copy(n_rel_tiles[:, :], rbase[0:1, RELATIONS - 1:RELATIONS]))
                        link(v.tensor_tensor(rbase[:, :], rbase[:, :], rtiles[:, :], ALU.subtract))
                        v.tensor_copy(rel_base[:, :], rbase[0:1, :])
                        sflat = slots[:, :, :].rearrange("p j r -> p (j r)")
                        link(v.tensor_tensor(sflat, sflat, banks(7, NT * RELATIONS), ALU.add))
                        link(v.scalar_tensor_tensor(in_tile[:, :, :], slots[:, :, :], 1.0, present[:, :, :], ALU.add, ALU.mult))
                        link(v.tensor_scalar(in_tile[:, :, :], in_tile[:, :, :], -1.0, None, ALU.add))
                        link(v.tensor_copy(pairi[:, 0, :, :], in_tile[:, :, :]))
                        link(v.tensor_single_scalar(pairi[:, 1, :, :], pairi[:, 0, :, :], P - 1, ALU.bitwise_and))
                        link(v.tensor_single_scalar(pairi[:, 0, :, :], pairi[:, 0, :, :], 7, ALU.arith_shift_right))
                        v.tensor_copy(pair_tile[:, :, :], pairi[:, 0, :, :])
                        v.tensor_copy(pair_place[:, :, :], pairi[:, 1, :, :])
                        v.scalar_tensor_tensor(slots[:, :, :], rbase[:, :].unsqueeze(1).to_broadcast([P, NT, RELATIONS]),
                                               float(P), slots[:, :, :], ALU.mult, ALU.add).then_inc(s_tables, 1)
                        for n in range(TABLE_COLS):
                            last = v.tensor_scalar(started[:, n, :], rbase[:, :], float(-n * P), pidx[:, :], ALU.add, ALU.is_le)
                        link(last)
                        v.tensor_reduce(n_started[:, :], started[:, :, :], AX.X, ALU.add).then_inc(s_rn, 1)
                        for j in range(NT):
                            v.tensor_scalar(mask[:, j, :], C[:, j, 0:NP], 0.0, NEGATIVE, ALU.is_equal, ALU.mult)
                        dve.wait_ge(s_sqrt, 2)
                        v.reciprocal(dinv[:, :], deg[:, :])
                        dve.wait_ge(s_trel, 1)
                        link(v.tensor_scalar(trel[:, :], banks(6, REL_TILES)[0:1, :], -1.0, None, ALU.add))
                        v.tensor_copy(tile_rel[:, :], trel[:, :])
                        link(v.memset(first[:, :], 1.0))
                        link(v.tensor_tensor(first[:, 1:], trel[:, 1:], trel[:, 0:REL_TILES - 1], ALU.not_equal))
                        link(v.scalar_tensor_tensor(first[:, :], trel[:, :], float(RELATIONS - 1), first[:, :], ALU.is_lt, ALU.mult))
                        link(v.scalar_tensor_tensor(first[:, :], trel[:, :], 1.0, first[:, :], ALU.add, ALU.mult))
                        v.tensor_copy(next_rel[:, :], first[:, :])

                    @block.tensor
                    def _(pe):
                        pe.wait_ge(s_z16, 1)
                        nc.tensor.matmul(banks(6, NT * RELATIONS), zero16[:, 0:P], zero16[:, :], start=True, stop=False)
                        pe.sem_inc(s_used, GT)
                        pe.sem_inc(s_hotd, 1)
                        pe.sem_inc(s_add, 2)
                        groups = pe.value_load(n_groups[0:1, 0:1], min_val=0, max_val=GROUPS)
                        with pe.Fori(0, GROUPS // 2) as i:
                            with pe.If(i * 2 < groups):
                                for g in range(2):
                                    pe.wait_ge(s_add, i * 2 + (g + 1))
                                    for q in range(GT):
                                        u = g * GT + q
                                        pe.wait_ge(s_hot, i * (2 * GT) + (u + 1))
                                        pe.wait_ge(s_hotd, i * (2 * GT) + (u + 2))
                                        for a in range(0, CC, 512):
                                            w = min(512, CC - a)
                                            last = nc.tensor.matmul(banks(3 * g, 1536)[:, a:a + w], hot_dst[:, q, :], hot_src[:, q, a:a + w],
                                                                    start=(q == 0), stop=(q == GT - 1))
                                        for j in range(NT):
                                            last = nc.tensor.matmul(banks(6, 512)[:, j * RELATIONS:(j + 1) * RELATIONS],
                                                                    hot_src[:, q, j * P:(j + 1) * P], hot_src[:, q, NP:],
                                                                    start=False, stop=False, skip_group_check=True)
                                        last.then_inc(s_used, 1)
                        nc.tensor.matmul(banks(6, NT * RELATIONS), zero16[:, 0:P], zero16[:, :], start=False, stop=True).then_inc(s_pc, 1)
                        pe.wait_ge(s_pres, 1)
                        pflat = present[:, :, :].rearrange("p j r -> p (j r)")
                        nc.tensor.matmul(banks(7, NT * RELATIONS), tri[:, :], pflat, start=True, stop=True)
                        nc.tensor.matmul(banks(6, NT * RELATIONS), ones[:, :], pflat, start=True, stop=True).then_inc(s_rpre, 1)
                        pe.wait_ge(s_counts, 1)
                        for k in range(NT):
                            if k >= 2:
                                pe.wait_ge(s_cTe, k - 1)
                            for j in range(NT):
                                last = nc.tensor.transpose(banks(3 * (k % 2), NP)[:, j * P:(j + 1) * P],
                                                           C[:, j, k * P:(k + 1) * P], ident[:, :])
                            last.then_inc(s_cT, 1)
                        pe.wait_ge(s_rn, 1)
                        for n in range(TABLE_COLS):
                            last = nc.tensor.matmul(banks(6, TABLE_COLS * P)[0:1, n * P:(n + 1) * P], n_started[:, n:n + 1],
                                                    ident[:, :], start=True, stop=True)
                        last.then_inc(s_trel, 1)


        SLOTS = 5
        with ExitStack() as st:
            sb = holder(st)
            rows_v = sb("rows_v", [P, 2, NP])
            rows_m = sb("rows_m", [P, 2, NP])
            tt = sb("tt", [P, SLOTS, NP])
            M = sb("M", [P, HEADS, NT])
            Mz = sb("Mz", [P, HEADS, NT])
            u_pos = sb("u_pos", [P, HEADS, NT])
            u_neg = sb("u_neg", [P, HEADS, NT])
            m_sb = sb("m_sb", [80, P])
            rden = sb("rden", [P, NT])
            hn = sb("hn", [P, 2, NT, HEAD_DIM])
            widx = sb("widx", [P, 2, SB], i32)
            got = sb("got", [P, 2, SB])
            s_row = [sem("row_u0"), sem("row_u1")]
            s_rowf, s_M, s_fill = (sem(n) for n in ("row_free", "m_ready", "unused_filled"))
            s_vm = [sem("vm_row0"), sem("vm_row1")]
            s_pre, s_sub, s_exp, s_mul, s_mm = (sem(n) for n in ("leaky", "shifted", "exped", "probs", "head_tile_done"))
            s_hn, s_den, s_hfree, s_rm = (sem(n) for n in ("head_out", "head_sums", "head_free", "rows_mixed"))
            s_hd = [sem("head_stored0"), sem("head_stored1")]
            s_ixs, s_sld, s_kept = sem("slot_idx_staged"), [sem(f"slots_gathered{u}") for u in range(2)], sem("slots_kept")

            with nc.Block() as block:
                @block.sync
                def _(sp):
                    for h in range(HEADS):
                        if h >= 2:
                            sp.wait_ge(s_rowf, h - 1)
                        sp.dma_start(rows_v[:, h % 2, :], row_of(uv_rows, 2 * h)).then_inc(s_row[h % 2], 16)
                    sp.wait_ge(s_rows, 3)
                    sp.dma_start(m_rows, m_sb[:, :]).then_inc(s_moved, 16)
                    all_moved(sp, 1)
                    vr = uv_rows.rearrange("(h c j) p -> h c (j p)", c=2, j=NT)
                    mr = m_rows.rearrange("(h j) p -> h (j p)", j=NT)
                    h1v = h1_dram.rearrange("(j p) (h c) -> h p j c", p=P, h=HEADS)

                    def load(h, g):
                        sp.dma_start(rows_v[:, g, :], vr[ds(h, 1), 1, :].to_broadcast([P, NP])).then_inc(s_vm[g], 16)
                        sp.dma_start(rows_m[:, g, :], mr[ds(h, 1), :].to_broadcast([P, NP])).then_inc(s_vm[g], 16)

                    def store(h, g):
                        sp.wait_ge(s_hn, h + 3)
                        sp.sem_inc(s_go_sp, 1)
                        sp.dma_start(h1v[ds(h, 1), :, :, :].rearrange("o p j c -> (o p) j c"), hn[:, g, :, :]).then_inc(s_hd[g], 16)

                    for g in range(2):
                        load(g, g)
                    with sp.Fori(0, HEADS // 2 - 1) as i:
                        for g in range(2):
                            store(i * 2 + g, g)
                            load(i * 2 + (g + 2), g)
                            sp.wait_ge(s_hd[g], i * 16 + 16)
                            sp.sem_inc(s_hfree, 1)
                    for g in range(2):
                        store(HEADS - 2 + g, g)
                    for g in range(2):
                        sp.wait_ge(s_hd[g], 8 * HEADS)

                @block.gpsimd
                def _(pool):
                    def gather(c, half):
                        nc.gpsimd.tensor_copy(widx[:, half, :], slot_flat[:, ds(c * SB, SB)]).then_inc(s_ixs, 1)
                        pool.wait_ge(s_ixs, c + 1)
                        pool.sem_inc(s_go, 1)
                        for u in range(SB):
                            pool.indirect_dma_start(got[:, half, u:u + 1], None, slot_table,
                                                    bass.IndirectOffsetOnAxis(widx[:, half, u:u + 1], 0)).then_inc(s_sld[half], 16)

                    def keep_slots(c, half):
                        nc.gpsimd.tensor_copy(slot_of[:, ds(c * SB, SB)], got[:, half, :]).then_inc(s_kept, 1)
                        pool.wait_ge(s_kept, c + 3)
                        pool.sem_inc(s_go, 1)

                    groups = pool.value_load(n_groups[0:1, 0:1], min_val=1, max_val=GROUPS)
                    pool.sem_inc(s_kept, 2)
                    walk_columns(pool, groups, gather, keep_slots, s_sld)

                @block.scalar
                def _(act):
                    fill = msg_dram.rearrange("(t p) o -> t p o", p=P)
                    used = act.value_load(n_rel_tiles[0:1, 0:1], min_val=1, max_val=REL_TILES)
                    with act.Fori(0, REL_TILES // 2) as i:
                        with act.If(i * 2 >= used):
                            for u in range(2):
                                act.dma_start(fill[ds(i * 2 + u, 1), :, :].rearrange("o p n -> (o p) n"),
                                              region_h[:, 0:DIM]).then_inc(s_fill, 16)
                        with act.If(i * 2 < used):
                            act.sem_inc(s_fill, 32)
                    act.wait_ge(s_turned, 3)
                    nc.scalar.copy(m_sb[:, :], banks(0, P)[:80, :]).then_inc(s_rows, 1)
                    with act.Fori(0, HEADS // 2) as i:
                        for g in range(2):
                            h = i * 2 + g
                            act.wait_ge(s_vm[g], i * 32 + 32)

                            def leaky(k):
                                act.wait_ge(s_mm, h * NT + (k + 1))
                                nc.scalar.activation(tt[:, k % SLOTS, :], rows_v[:, g, :], ACT.Relu,
                                                     bias=u_pos[:, ds(h, 1), k:k + 1].rearrange("p o k -> p (o k)"),
                                                     scale=1.0 - NEG_SLOPE).then_inc(s_pre, 1)
                            leaky(0)
                            for k in range(NT):
                                if k + 1 < NT:
                                    leaky(k + 1)
                                act.wait_ge(s_sub, h * NT + (k + 1))
                                nc.scalar.activation(tt[:, k % SLOTS, :], tt[:, k % SLOTS, :], ACT.Exp).then_inc(s_exp, 1)
                    act.wait_ge(s_fill, 16 * REL_TILES)

                @block.vector
                def _(dve):
                    v = nc.vector
                    link = chain(dve)
                    for h in range(HEADS):
                        dve.wait_ge(s_row[h % 2], 16 * (h // 2 + 1))
                        for j in range(NT):
                            link(v.tensor_tensor_reduce(out=tt[:, 0, :], in0=mask[:, j, :], in1=rows_v[:, h % 2, :], scale=1.0,
                                                        scalar=NEGATIVE, op0=ALU.add, op1=ALU.max, accum_out=M[:, h, j:j + 1]))
                        dve.sem_inc(s_rowf, 1)
                    dve.wait_ge(s_rowf, HEADS)
                    uvc = uv[:, :, :].rearrange("p (h c) j -> p h c j", c=2)
                    v.tensor_scalar(u_pos[:, :, :], uvc[:, :, 0, :], 1.0 - NEG_SLOPE, None, ALU.mult)
                    v.tensor_scalar(u_neg[:, :, :], uvc[:, :, 0, :], NEG_SLOPE, None, ALU.mult)
                    link(v.scalar_tensor_tensor(M[:, :, :], M[:, :, :], NEGATIVE / 2, M[:, :, :], ALU.is_gt, ALU.mult))
                    link(v.tensor_tensor(M[:, :, :], M[:, :, :], uvc[:, :, 1, :], ALU.add))
                    link(v.tensor_scalar(Mz[:, :, :], M[:, :, :], NEG_SLOPE, None, ALU.mult))
                    v.tensor_tensor(Mz[:, :, :], Mz[:, :, :], M[:, :, :], ALU.max).then_inc(s_M, 1)
                    hd = HEAD_DIM

                    def normalise(g, complete, free, summed):
                        dve.wait_ge(s_mm, complete)
                        dve.wait_ge(s_hfree, free)
                        three = PS[:, 4 * g:4 * g + 3, 0:3 * HCOLS].rearrange("p q (t c) -> p q t c", c=HCOLS)
                        v.tensor_scalar(rden[:, 0:9].rearrange("p (q t) -> p q t", t=3), three[:, :, :, hd], SOFTMAX_EPS, None, ALU.add)
                        v.tensor_scalar(rden[:, 9:10], banks(4 * g + 3, HCOLS)[:, hd:], SOFTMAX_EPS, None, ALU.add).then_inc(s_den, 1)
                        dve.wait_ge(s_den, summed)
                        v.reciprocal(rden[:, :], rden[:, :]).then_inc(s_den, 1)
                        dve.wait_ge(s_den, summed + 1)
                        for q in range(3):
                            v.tensor_tensor(hn[:, g, 3 * q:3 * q + 3, :], three[:, q, :, 0:hd],
                                            rden[:, 3 * q:3 * q + 3].unsqueeze(2).to_broadcast([P, 3, hd]), ALU.mult)
                        v.tensor_scalar(hn[:, g, 9, :], banks(4 * g + 3, hd), rden[:, 9:10], None, ALU.mult).then_inc(s_hn, 1)

                    with dve.Fori(0, HEADS // 2) as i:
                        for g in range(2):
                            h = i * 2 + g
                            dve.wait_ge(s_vm[g], i * 32 + 32)
                            v.scalar_tensor_tensor(rows_m[:, g, :], rows_v[:, g, :], NEG_SLOPE, rows_m[:, g, :],
                                                   ALU.mult, ALU.subtract).then_inc(s_rm, 1)
                            dve.wait_ge(s_rm, h + 1)

                            def shift(k):
                                dve.wait_ge(s_pre, h * NT + (k + 1))
                                v.scalar_tensor_tensor(tt[:, k % SLOTS, :], tt[:, k % SLOTS, :],
                                                       u_neg[:, ds(h, 1), k:k + 1].rearrange("p o k -> p (o k)"),
                                                       rows_m[:, g, :], ALU.add, ALU.add).then_inc(s_sub, 1)
                            shift(0)
                            for k in range(NT):
                                if k + 1 < NT:
                                    shift(k + 1)
                                dve.wait_ge(s_exp, h * NT + (k + 1))
                                v.scalar_tensor_tensor(tt[:, k % SLOTS, :], tt[:, k % SLOTS, :], BIG, CT[:, k, :],
                                                       ALU.min, ALU.mult).then_inc(s_mul, 1)
                                if k == 1 and g == 0:
                                    with dve.If(i > 0):
                                        normalise(1, i * (2 * NT) + SLOTS, i * 2, i * 4 + 1)
                                if k == 1 and g == 1:
                                    normalise(0, i * (2 * NT) + (NT + SLOTS), i * 2 + 1, i * 4 + 3)
                    normalise(1, HEADS * NT + SLOTS, HEADS, 2 * HEADS + 1)

                @block.tensor
                def _(pe):
                    pe.sem_inc(s_mm, SLOTS)
                    pe.sem_inc(s_hn, 2)
                    pe.sem_inc(s_hfree, 2)
                    pe.sem_inc(s_den, 2)
                    pe.wait_ge(s_M, 1)
                    nc.tensor.transpose(banks(0, P)[:80, :], Mz[:, :, :].rearrange("p h j -> p (h j)"), ident[:, :]).then_inc(s_turned, 1)
                    pe.wait_ge(s_rows, 3)
                    with pe.Fori(0, HEADS // 2) as i:
                        for g in range(2):
                            h = i * 2 + g
                            pe.wait_ge(s_hn, h + 1)
                            for k in range(NT):
                                pe.wait_ge(s_mul, h * NT + (k + 1))
                                for j in range(NT):
                                    last = nc.tensor.matmul(PS[:, 4 * g + j // 3, (j % 3) * HCOLS:(j % 3 + 1) * HCOLS],
                                                            tt[:, k % SLOTS, j * P:(j + 1) * P],
                                                            hA[:, k, ds(h, 1), :].rearrange("p o c -> p (o c)"),
                                                            start=(k == 0 and j % 3 == 0), stop=(k == NT - 1), skip_group_check=True)
                                last.then_inc(s_mm, 1)

        RQ = 4
        with ExitStack() as st:
            sb = holder(st)
            w2 = sb("w2", [P, KD, HID])
            att2 = sb("att2", [P, KD, 2])
            w2T = sb("w2T", [P, KH, DIM + 2])
            b1c = sb("b1c", [P, KH])
            h1 = sb("h1", [P, 2, HID])
            h1T = sb("h1T", [P, 2, KH, P])
            rows2 = sb("rows2", [2 * NT, P])
            iota_b = sb("iota_b", [P, P], bf16)
            hot_place = region_h[:, NT * (DIM + 1) + 2:NT * (DIM + 1) + 2 + RQ * NP // 2].bitcast(bf16).rearrange(
                "p (q j s) -> p q j s", q=RQ, s=P)
            hot_tile = sb("hot_tile", [P, RQ, NT, NT], bf16)
            tile_src = sb("tile_src", [P, RQ, NT, NT, 2], bf16)
            src_parts = sb("src_parts", [P, NT, NT, 2], bf16)
            s_hp, s_srcd, s_srct = (sem(n) for n in ("pairs_hot", "sources_done", "sources_taken"))
            s_w2, s_p2, s_w2t, s_w2e, s_wa2 = (sem(n) for n in (
                "w2_in", "att2_in", "w2_turned", "w2_moved", "att2_folded"))
            s_h1 = [sem("h1_in0"), sem("h1_in1")]
            pj2 = Projection("w2", KH, [512, DIM + 2 - 512])

            with nc.Block() as block:
                @block.sync
                def _(sp):
                    sp.dma_start(w2[:, :, :], W2.rearrange("(k p) c -> p k c", p=P)).then_inc(s_w2, 16)
                    with nc.allow_non_contiguous_dma(reason="vectors as columns"):
                        sp.dma_start(att2[:, :, 0], as2.rearrange("o (k p) -> p (o k)", p=P)).then_inc(s_p2, 16)
                        sp.dma_start(att2[:, :, 1], ad2.rearrange("o (k p) -> p (o k)", p=P)).then_inc(s_p2, 16)
                        sp.dma_start(b1c[:, :], b1.rearrange("(k p) -> p k", p=P)).then_inc(s_p2, 16)
                    for j in range(NT):
                        if j >= 2:
                            sp.wait_ge(pj2.turned, j - 1)
                        sp.dma_start(h1[:, j % 2, :], h1_dram[j * P:(j + 1) * P, :]).then_inc(s_h1[j % 2], 16)
                    sp.wait_ge(s_rows, 4)
                    sp.dma_start(uv2_rows, rows2[:, :]).then_inc(s_moved, 16)
                    all_moved(sp, 1)

                @block.scalar
                def _(act):
                    for g in range(2 * KH):
                        act.wait_ge(s_w2t, g + 1)
                        nc.scalar.copy(w2T[:, g // 2, 384 * (g % 2):384 * (g % 2) + 384], banks(g % 2, 384)).then_inc(s_w2e, 1)
                    act.wait_ge(s_wa2, 1)
                    nc.scalar.copy(w2T[:, :, DIM:], banks(2, 2 * KH).rearrange("p (k c) -> p k c", k=KH)).then_inc(s_w2e, 1)
                    act.wait_ge(s_p2, 48)

                    def relu_bias(j):
                        for k in range(KH):
                            last = nc.scalar.activation(h1T[:, j % 2, k, :], banks(0, 1024)[:, k * P:(k + 1) * P],
                                                        ACT.Relu, bias=b1c[:, k:k + 1])
                        return last
                    project_act(act, pj2, h1T, relu_bias)
                    act.wait_ge(s_turned, 4)
                    nc.scalar.copy(rows2[:, :], banks(0, P)[:2 * NT, :]).then_inc(s_rows, 1)

                @block.vector
                def _(dve):
                    v = nc.vector
                    link = chain(dve)
                    v.memset(hB[:, :, DIM:], 1.0)
                    v.tensor_copy(iota_b[:, :], iota[:, :])
                    v.tensor_copy(src_parts[:, :, :, 0], pidx[:, 0:1].unsqueeze(2).to_broadcast([P, NT, NT]))
                    link(v.tensor_scalar(src_parts[:, :, :, 1], iota[:, 0:NT].unsqueeze(2).to_broadcast([P, NT, NT]),
                                         float(P), None, ALU.mult))

                    def relations(j):
                        return range(j * RQ, min(RELATIONS, (j + 1) * RQ))

                    def one_hots(j):
                        for q, r in enumerate(relations(j)):
                            v.tensor_tensor(hot_place[:, q, :, :], pair_place[:, :, r:r + 1].to_broadcast([P, NT, P]),
                                            iota_b[:, :].unsqueeze(1).to_broadcast([P, NT, P]), ALU.is_equal)
                            link(v.tensor_tensor(hot_tile[:, q, :, :], pair_tile[:, :, r:r + 1].to_broadcast([P, NT, NT]),
                                                 iota_b[:, 0:NT].unsqueeze(1).to_broadcast([P, NT, NT]), ALU.is_equal))
                            v.tensor_tensor(tile_src[:, q, :, :, :], hot_tile[:, q, :, :].unsqueeze(3).to_broadcast([P, NT, NT, 2]),
                                            src_parts[:, :, :, :], ALU.mult).then_inc(s_hp, 1)

                    one_hots(0)
                    for j in range(NT):
                        dve.wait_ge(pj2.multiplied, j + 1)
                        v.tensor_copy(hB[:, j, 0:DIM], banks(2 + 3 * (j % 2), DIM))
                        v.tensor_copy(uv2[:, :, j], banks(2 + 3 * (j % 2), DIM + 2)[:, DIM:]).then_inc(pj2.taken, 1)
                        if relations(j):
                            dve.wait_ge(s_srcd, relations(j)[-1] + 1)
                        for q, r in enumerate(relations(j)):
                            at = dve.value_load(rel_base[0:1, r:r + 1], min_val=0, max_val=REL_TILES - 1)
                            ins = v.tensor_reduce(rtab[:, ds(at, NT)], banks(4, RQ * 2 * NT)[:, q * 2 * NT:(q + 1) * 2 * NT].rearrange(
                                "p (a o) -> p a o", o=2), AX.X, ALU.add)
                            ins.then_inc(s_srct, 1)
                            dve.wait_ge(s_srct, r + 1)
                        one_hots(j + 1)

                @block.tensor
                def _(pe):
                    pe.wait_ge(s_w2, 16)
                    for g in range(2 * KH):
                        if g >= 2:
                            pe.wait_ge(s_w2e, g - 1)
                        for u in range(3):
                            o = 3 * (g % 2) + u
                            last = nc.tensor.transpose(banks(g % 2, 384)[:, u * P:(u + 1) * P],
                                                       w2[:, o, (g // 2) * P:(g // 2 + 1) * P], ident[:, :])
                        last.then_inc(s_w2t, 1)
                    pe.wait_ge(s_p2, 48)
                    for k in range(KH):
                        for o in range(KD):
                            last = nc.tensor.matmul(banks(2, 16)[:, 2 * k:2 * k + 2], w2[:, o, k * P:(k + 1) * P], att2[:, o, :],
                                                    start=(o == 0), stop=(o == KD - 1))
                    last.then_inc(s_wa2, 1)
                    pe.wait_ge(s_w2e, 2 * KH + 1)

                    def h1_ready(j):
                        return 16 * (j // 2 + 1)

                    def sources(j):
                        for r in range(j * RQ, min(RELATIONS, (j + 1) * RQ)):
                            pe.wait_ge(s_hp, r + 1)
                            if r % RQ == 0 and r:
                                pe.wait_ge(s_srct, r)
                            for k in range(NT):
                                last = nc.tensor.matmul(banks(4, 512)[:, (r % RQ) * 2 * NT:(r % RQ + 1) * 2 * NT], hot_place[:, r % RQ, k, :],
                                                        tile_src[:, r % RQ, k, :, :].rearrange("p a o -> p (a o)"),
                                                        start=(k == 0), stop=(k == NT - 1))
                            last.then_inc(s_srcd, 1)

                    project_pe(pe, pj2, lambda j: h1[:, j % 2, :], (s_h1, h1_ready), h1T, w2T, sources)
                    pe.wait_ge(pj2.taken, NT)
                    nc.tensor.transpose(banks(0, P)[:2 * NT, :], uv2[:, :, :].rearrange("p c j -> p (c j)"), ident[:, :]).then_inc(s_turned, 1)

        with ExitStack() as st:
            sb = holder(st)
            s_cto = sem("ct_out")
            row_a = sb("row_a", [P, NP])
            row_m = sb("row_m", [P, NP])
            pr = sb("pr", [P, NT, NP])
            M2 = sb("M2", [P, NT])
            Mz2 = sb("Mz2", [P, NT])
            u2p = sb("u2p", [P, NT])
            u2n = sb("u2n", [P, NT])
            m2_sb = sb("m2_sb", [NT, P])
            rden2 = sb("rden2", [P, NT])
            b2row = sb("b2row", [P, DIM])
            s_ra, s_rm, s_M2, s_x2 = (sem(n) for n in (
                "row2_in", "rowm2_in", "m2_ready", "x_again"))
            widx5 = sb("widx5", [P, 2, SB], i32)
            wst = sb("wst", [P, 2, SB])
            s_wst, s_wkeep, s_wld = sem("w_staged"), sem("w_kept"), [sem(f"w_gathered{u}") for u in range(2)]
            s_pre2, s_sub2, s_exp2, s_mul2, s_mm2, s_tk2 = (sem(n) for n in (
                "leaky2", "shifted2", "exped2", "probs2", "tile_done2", "tile_taken2"))

            with nc.Block() as block:
                @block.sync
                def _(sp):
                    sp.dma_start(row_a[:, :], row_of(uv2_rows, 0)).then_inc(s_ra, 16)
                    sp.dma_start(b2row[:, :], vector_row(b2, DIM)).then_inc(s_biases, 16)
                    sp.dma_start(ct_dram, CT[:, :, :].rearrange("p k d -> p (k d)")).then_inc(s_cto, 16)
                    sp.wait_ge(s_M2, 1)
                    sp.dma_start(row_a[:, :], row_of(uv2_rows, 1)).then_inc(s_ra, 16)
                    sp.wait_ge(s_rows, 5)
                    sp.dma_start(m2_rows, m2_sb[:, :]).then_inc(s_moved, 16)
                    all_moved(sp, 1)
                    sp.dma_start(row_m[:, :], row_of(m2_rows, 0)).then_inc(s_rm, 16)
                    sp.dma_start(x2[:, 0:NT - 1, :], x[0:(NT - 1) * P, :].rearrange("(j p) i -> p j i", p=P)).then_inc(s_x2, 16)
                    sp.wait_ge(s_pad, 2)
                    sp.dma_start(x2[:LAST, NT - 1, :], x[(NT - 1) * P:NODES, :]).then_inc(s_x2, 16)
                    sp.wait_ge(s_cto, 16)

                @block.gpsimd
                def _(pool):
                    def gather(c, half):
                        nc.gpsimd.tensor_copy(widx5[:, half, :], etab[:, ds(c * SB, SB), F_DREL]).then_inc(s_wst, 1)
                        pool.wait_ge(s_wst, c + 1)
                        pool.sem_inc(s_go, 1)
                        for u in range(SB):
                            pool.indirect_dma_start(wst[:, half, u:u + 1], None, inv_count,
                                                    bass.IndirectOffsetOnAxis(widx5[:, half, u:u + 1], 0)).then_inc(s_wld[half], 16)

                    def keep_weights(c, half):
                        nc.gpsimd.tensor_copy(weight[:, ds(c * SB, SB)], wst[:, half, :]).then_inc(s_wkeep, 1)
                        pool.wait_ge(s_wkeep, c + 3)
                        pool.sem_inc(s_go, 1)

                    groups = pool.value_load(n_groups[0:1, 0:1], min_val=1, max_val=GROUPS)
                    pool.sem_inc(s_wkeep, 2)
                    walk_columns(pool, groups, gather, keep_weights, s_wld)

                @block.scalar
                def _(act):
                    act.wait_ge(s_turned, 5)
                    nc.scalar.copy(m2_sb[:, :], banks(0, P)[:NT, :]).then_inc(s_rows, 1)
                    act.wait_ge(s_ra, 32)
                    for k in range(NT):
                        nc.scalar.activation(pr[:, k, :], row_a[:, :], ACT.Relu, bias=u2p[:, k:k + 1],
                                             scale=1.0 - NEG_SLOPE).then_inc(s_pre2, 1)
                    for k in range(NT):
                        act.wait_ge(s_sub2, k + 1)
                        nc.scalar.activation(pr[:, k, :], pr[:, k, :], ACT.Exp).then_inc(s_exp2, 1)

                @block.vector
                def _(dve):
                    v = nc.vector
                    link = chain(dve)
                    dve.wait_ge(s_ra, 16)
                    for j in range(NT):
                        link(v.tensor_tensor_reduce(out=pr[:, 0, :], in0=mask[:, j, :], in1=row_a[:, :], scale=1.0,
                                                    scalar=NEGATIVE, op0=ALU.add, op1=ALU.max, accum_out=M2[:, j:j + 1]))
                    v.memset(x2[:, NT - 1, :], 0.0).then_inc(s_pad, 1)
                    v.tensor_scalar(u2p[:, :], uv2[:, 0, :], 1.0 - NEG_SLOPE, None, ALU.mult)
                    v.tensor_scalar(u2n[:, :], uv2[:, 0, :], NEG_SLOPE, None, ALU.mult)
                    link(v.scalar_tensor_tensor(M2[:, :], M2[:, :], NEGATIVE / 2, M2[:, :], ALU.is_gt, ALU.mult))
                    link(v.tensor_tensor(M2[:, :], M2[:, :], uv2[:, 1, :], ALU.add))
                    link(v.tensor_scalar(Mz2[:, :], M2[:, :], NEG_SLOPE, None, ALU.mult))
                    v.tensor_tensor(Mz2[:, :], Mz2[:, :], M2[:, :], ALU.max).then_inc(s_M2, 1)
                    dve.wait_ge(s_rm, 16)
                    dve.wait_ge(s_ra, 32)
                    link(v.scalar_tensor_tensor(row_m[:, :], row_a[:, :], NEG_SLOPE, row_m[:, :], ALU.mult, ALU.subtract))

                    def shift(k):
                        dve.wait_ge(s_pre2, k + 1)
                        v.scalar_tensor_tensor(pr[:, k, :], pr[:, k, :], u2n[:, k:k + 1], row_m[:, :], ALU.add, ALU.add).then_inc(s_sub2, 1)
                    shift(0)
                    for k in range(NT):
                        if k + 1 < NT:
                            shift(k + 1)
                        dve.wait_ge(s_exp2, k + 1)
                        v.scalar_tensor_tensor(pr[:, k, :], pr[:, k, :], BIG, CT[:, k, :], ALU.min, ALU.mult).then_inc(s_mul2, 1)
                    dve.wait_ge(s_x2, 32)
                    dve.wait_ge(s_biases, 16)
                    for j in range(NT):
                        last = v.tensor_tensor(x2[:, j, :], x2[:, j, :], b2row[:, :], ALU.add)
                    link(last)
                    for j in range(NT):
                        o = banks(2 * (j % 4), DIM + 1)
                        dve.wait_ge(s_mm2, j + 1)
                        link(v.tensor_scalar(rden2[:, j:j + 1], o[:, DIM:], SOFTMAX_EPS, None, ALU.add))
                        link(v.reciprocal(rden2[:, j:j + 1], rden2[:, j:j + 1]))
                        v.scalar_tensor_tensor(x2[:, j, :], o[:, 0:DIM], rden2[:, j:j + 1], x2[:, j, :], ALU.mult, ALU.add).then_inc(s_tk2, 1)

                @block.tensor
                def _(pe):
                    pe.wait_ge(s_M2, 1)
                    nc.tensor.transpose(banks(0, P)[:NT, :], Mz2[:, :], ident[:, :]).then_inc(s_turned, 1)
                    pe.wait_ge(s_rows, 5)
                    for j in range(NT):
                        if j >= 4:
                            pe.wait_ge(s_tk2, j - 3)
                        for k in range(NT):
                            if j == 0:
                                pe.wait_ge(s_mul2, k + 1)
                            for a, w in ((0, 512), (512, DIM + 1 - 512)):
                                last = nc.tensor.matmul(banks(2 * (j % 4), 1024)[:, a:a + w], pr[:, k, j * P:(j + 1) * P],
                                                        hB[:, k, a:a + w], start=(k == 0), stop=(k == NT - 1))
                        last.then_inc(s_mm2, 1)

        counts_life.close()

        wrel_life = ExitStack()
        wraw = holder(wrel_life)("wraw", [P, KD, DIM])
        wv = Wrel.rearrange("r (k p) o -> p r k o", p=P)
        s_w = sem("wrel_in")

        with ExitStack() as st:
            sb = holder(st)
            hR = sb("hR", [P, NT, DIM])
            wr = sb("wr", [P, KD, DIM])
            wrhi = sb("wrhi", [P, KD, DIM], f32r)
            wrlo = sb("wrlo", [P, KD, DIM], f32r)
            hThi = sb("hThi", [P, 2, KD, P], f32r)
            hTlo = sb("hTlo", [P, 2, KD, P], f32r)
            s_wrh, s_wrl = sem("wroot_high"), sem("wroot_split")
            brow = sb("brow", [P, DIM])
            stats2 = sb("stats2", [P, NT, 2, 6])
            mv2 = sb("mv2", [P, NT, 2])
            rstd2 = sb("rstd2", [P, NT])
            nmr2 = sb("nmr2", [P, NT])
            s_wr, s_mvb, s_lnb, s_hb = (sem(n) for n in (
                "wroot_in", "ln2_stats", "ln2_scale", "h_ready"))
            pj3 = SplitProjection("wroot", KD, [512, 256])

            with nc.Block() as block:
                @block.sync
                def _(sp):
                    sp.dma_start(wr[:, :, :], Wroot.rearrange("(k p) o -> p k o", p=P)).then_inc(s_wr, 16)
                    sp.dma_start(brow[:, :], vector_row(brg, DIM)).then_inc(s_biases, 16)
                    sp.dma_start(wraw[:, :, :], wv[:, 0, :, :]).then_inc(s_w, 16)
                    for j in range(NT):
                        sp.wait_ge(s_hb, j + 1)
                        sp.dma_start(h_dram[j * P:(j + 1) * P, :], hR[:, j, :]).then_inc(s_moved, 16)
                    all_moved(sp, NT)

                @block.scalar
                def _(act):
                    act.wait_ge(s_wr, 16)
                    split_weights_high(act, wr, wrhi, s_wrh)
                    act.wait_ge(s_mvb, 1)
                    nc.scalar.activation(rstd2[:, :], mv2[:, :, 1], ACT.Sqrt, bias=eps_ln[:, :]).then_inc(s_sqrt, 1)
                    act.wait_ge(s_lnb, 1)
                    for j in range(NT):
                        nc.scalar.activation(hR[:, j, :], x2[:, j, :], ACT.Relu, bias=nmr2[:, j:j + 1],
                                             scale=rstd2[:, j:j + 1]).then_inc(s_hb, 1)
                    for j in range(NT):
                        move_high(act, pj3, hThi, j)

                @block.vector
                def _(dve):
                    v = nc.vector
                    link = chain(dve)
                    for j in range(NT):
                        for c in range(2):
                            last = v.bn_stats(stats2[:, j, c, :], x2[:, j, c * 384:(c + 1) * 384])
                    link(last)
                    for j in range(NT):
                        last = v.bn_aggr(mv2[:, j, :], stats2[:, j, :, :].rearrange("p a b -> p (a b)"))
                    last.then_inc(s_mvb, 1)
                    dve.wait_ge(s_sqrt, 3)
                    link(v.reciprocal(rstd2[:, :], rstd2[:, :]))
                    dve.wait_ge(s_mvb, 1)
                    v.scalar_tensor_tensor(nmr2[:, :], mv2[:, :, 0], -1.0, rstd2[:, :], ALU.mult, ALU.mult).then_inc(s_lnb, 1)
                    split_weights_low(dve, wr, wrhi, wrlo, s_wrh, s_wrl)
                    dve.wait_ge(s_biases, 32)
                    move_low(dve, pj3, hThi, hTlo, 0)
                    for j in range(NT):
                        if j + 1 < NT:
                            move_low(dve, pj3, hThi, hTlo, j + 1)
                        dve.wait_ge(pj3.multiplied, j + 1)
                        v.tensor_tensor(acc[:, j, :], banks(2 + 3 * (j % 2), DIM), brow[:, :], ALU.add).then_inc(pj3.taken, 1)

                @block.tensor
                def _(pe):
                    pe.wait_ge(s_wrl, 1)
                    split_project_pe(pe, pj3, lambda j: hR[:, j, :], (s_hb, lambda j: j + 1), hThi, hTlo, wrhi, wrlo)

        with ExitStack() as st:
            sb = holder(st)
            whi = sb("whi", [P, 2, KD, DIM], f32r)
            wlo = sb("wlo", [P, 2, KD, DIM], f32r)
            gx = sb("gx", [P, 2, DIM])
            ghi = sb("ghi", [P, 2, KD, P], f32r)
            glo = sb("glo", [P, 2, KD, P], f32r)
            mo = sb("mo", [P, 2, DIM])
            gidx = sb("gidx", [P, 2, 1], i32)
            s_idx, s_tn, s_tm, s_tl, s_mt, s_mo, s_whi, s_wlo = (sem(n) for n in (
                "src_staged", "edges_turned", "edges_hi", "edges_lo", "messages_done", "messages_moved",
                "wrel_hi", "wrel_lo"))
            s_gx = [sem(f"edges_in{u}") for u in range(2)]
            s_ms = [sem(f"messages_stored{u}") for u in range(2)]
            TL = REL_TILES
            CHUNK = max(c for c in range(1, 9) if TL // 2 % c == 0)

            with nc.Block() as block:
                def pairs(eng):
                    return eng.value_load(n_rel_tiles[0:1, 0:1], min_val=1, max_val=TL)

                @block.sync
                def _(sp):
                    with sp.Fori(1, RELATIONS) as r:
                        sp.wait_ge(s_wlo, r)
                        sp.sem_inc(s_go_sp, 1)
                        sp.dma_start(wraw[:, :, :], wv[:, ds(r, 1), :, :].rearrange("p o k n -> p (o k) n")).then_inc(s_w, 16)
                    sp.wait_ge(s_w, 16 * RELATIONS)

                @block.gpsimd
                def _(pool):
                    def gather(t, n, u):
                        pool.wait_ge(s_tn, n)
                        nc.gpsimd.tensor_copy(gidx[:, u, :], rtab[:, ds(t, 1)]).then_inc(s_idx, 1)
                        pool.wait_ge(s_idx, n)
                        pool.sem_inc(s_go, 1)
                        pool.indirect_dma_start(gx[:, u, :], None, h_dram,
                                                bass.IndirectOffsetOnAxis(gidx[:, u, :], 0)).then_inc(s_gx[u], 16)

                    tiles = pairs(pool)
                    gather(0, 1, 0)
                    with pool.Fori(0, TL // 2 // CHUNK) as c:
                        with pool.If(c * (2 * CHUNK) < tiles):
                            with pool.Fori(0, CHUNK) as in_chunk:
                                i = pool.snap(c * CHUNK + in_chunk)
                                with pool.If(i * 2 < tiles):
                                    gather(i * 2 + 1, i * 2 + 2, 1)
                                    gather(i * 2 + 2, i * 2 + 3, 0)

                @block.scalar
                def _(act):
                    mv_ = msg_dram.rearrange("(t p) o -> t p o", p=P)

                    def move(t, u):
                        act.wait_ge(s_tn, t + 3)
                        act.wait_ge(s_mt, t + 1)
                        nc.scalar.copy(ghi[:, u, :, :].rearrange("p k n -> p (k n)"), banks(6 * u, DIM)).then_inc(s_tm, 1)

                    def split(r, slot):
                        act.wait_ge(s_w, r * 16 + 16)
                        for k in range(0, KD, 2):
                            nc.scalar.copy(whi[:, slot, k:k + 2, :].rearrange("p o k n -> p (o k n)"),
                                           wraw[:, k:k + 2, :].rearrange("p k n -> p (k n)")).then_inc(s_whi, 1)

                    def store(t, u):
                        act.wait_ge(s_mo, t + 3)
                        act.dma_start(mv_[ds(t, 1), :, :].rearrange("o p n -> (o p) n"), mo[:, u, :]).then_inc(s_ms[u], 16)

                    tiles = pairs(act)
                    move(0, 0)
                    split(0, ds(0, 1))
                    with act.Fori(0, TL // 2 // CHUNK) as c:
                        with act.If(c * (2 * CHUNK) < tiles):
                            with act.Fori(0, CHUNK) as in_chunk:
                                i = act.snap(c * CHUNK + in_chunk)
                                with act.If(i * 2 < tiles):
                                    for u in range(2):
                                        move(i * 2 + (u + 1), (u + 1) % 2)
                                        nxt = act.value_load(next_rel[0:1, ds(i * 2 + u, 1)], min_val=0, max_val=RELATIONS - 1)
                                        with act.If(nxt > 0):
                                            act.wait_ge(s_mt, i * 2 + (u + 2))
                                            split(nxt, ds(act.snap(nxt % 2), 1))
                                        store(i * 2 + u, u)
                    stored = act.snap((tiles + 1) // 2)
                    for u in range(2):
                        act.wait_ge(s_ms[u], stored * 16)
                        act.sem_inc(s_go_sp, 1)

                @block.vector
                def _(dve):
                    v = nc.vector

                    def rest(t, u):
                        dve.wait_ge(s_tm, t + 1)
                        v.tensor_tensor(glo[:, u, :, :].rearrange("p k n -> p (k n)"), banks(6 * u, DIM),
                                        ghi[:, u, :, :].rearrange("p k n -> p (k n)").bitcast(f32), ALU.subtract).then_inc(s_tl, 1)

                    def split(r, slot):
                        for k in range(0, KD, 2):
                            dve.wait_ge(s_whi, r * (KD // 2) + (k // 2 + 1))
                            last = v.tensor_tensor(wlo[:, slot, k:k + 2, :].rearrange("p o k n -> p (o k n)"),
                                                   wraw[:, k:k + 2, :].rearrange("p k n -> p (k n)"),
                                                   whi[:, slot, k:k + 2, :].rearrange("p o k n -> p (o k n)").bitcast(f32), ALU.subtract)
                        last.then_inc(s_wlo, 1)

                    def take(t, u):
                        dve.wait_ge(s_mt, t + 3)
                        v.tensor_copy(mo[:, u, :], banks(2 + 2 * u, DIM)).then_inc(s_mo, 1)

                    tiles = pairs(dve)
                    rest(0, 0)
                    split(0, ds(0, 1))
                    with dve.Fori(0, TL // 2 // CHUNK) as c:
                        with dve.If(c * (2 * CHUNK) < tiles):
                            with dve.Fori(0, CHUNK) as in_chunk:
                                i = dve.snap(c * CHUNK + in_chunk)
                                with dve.If(i * 2 < tiles):
                                    for u in range(2):
                                        rest(i * 2 + (u + 1), (u + 1) % 2)
                                        nxt = dve.value_load(next_rel[0:1, ds(i * 2 + u, 1)], min_val=0, max_val=RELATIONS - 1)
                                        with dve.If(nxt > 0):
                                            split(nxt, ds(dve.snap(nxt % 2), 1))
                                        with dve.If(i > 0):
                                            dve.wait_ge(s_ms[u], i * 16)
                                            dve.sem_inc(s_go_sp, 1)
                                        take(i * 2 + u, u)

                @block.tensor
                def _(pe):
                    for s in (s_tn, s_tl, s_mt, s_mo):
                        pe.sem_inc(s, 2)

                    def turn(t, n, u):
                        pe.wait_ge(s_gx[u], n)
                        pe.wait_ge(s_tl, t + 1)
                        for k in range(KD):
                            last = nc.tensor.transpose(banks(6 * u, DIM)[:, k * P:(k + 1) * P], gx[:, u, k * P:(k + 1) * P], ident[:, :])
                        last.then_inc(s_tn, 1)

                    def multiply(t, u):
                        r = pe.value_load(tile_rel[0:1, ds(t, 1)], min_val=0, max_val=RELATIONS - 1)
                        pe.wait_ge(s_wlo, r + 1)
                        slot = pe.snap(r % 2)
                        pe.wait_ge(s_tl, t + 3)
                        pe.wait_ge(s_mo, t + 1)
                        for k in range(KD):
                            for n, (g, w_) in enumerate(((ghi, whi), (ghi, wlo), (glo, whi))):
                                for a, w in ((0, 512), (512, 256)):
                                    last = nc.tensor.matmul(banks(2 + 2 * u, DIM)[:, a:a + w], g[:, u, k, :],
                                                            w_[:, ds(slot, 1), k, a:a + w].rearrange("p o n -> p (o n)"),
                                                            start=(k == 0 and n == 0), stop=(k == KD - 1 and n == 2))
                        last.then_inc(s_mt, 1)

                    tiles = pairs(pe)
                    turn(0, 16, 0)
                    with pe.Fori(0, TL // 2 // CHUNK) as c:
                        with pe.If(c * (2 * CHUNK) < tiles):
                            with pe.Fori(0, CHUNK) as in_chunk:
                                i = pe.snap(c * CHUNK + in_chunk)
                                with pe.If(i * 2 < tiles):
                                    turn(i * 2 + 1, i * 16 + 16, 1)
                                    multiply(i * 2, 0)
                                    turn(i * 2 + 2, i * 16 + 32, 0)
                                    multiply(i * 2 + 1, 1)

        wrel_life.close()
        wgcn_life = ExitStack()
        wghi = holder(wgcn_life)("wghi", [P, KD, DIM], f32r)
        wglo = holder(wgcn_life)("wglo", [P, KD, DIM], f32r)
        s_wg, s_wgh, s_wgl = sem("wgcn_in"), sem("wgcn_high"), sem("wgcn_split")

        with ExitStack() as st:
            sb = holder(st)
            RING = 2 * GT
            wg = sb("wg", [P, KD, DIM])
            mg = sb("mg", [P, RING, DIM])
            mhi = sb("mhi", [P, GT, DIM], f32r)
            mlo = sb("mlo", [P, GT, DIM], f32r)
            hotd = sb("hotd", [P, GT, P], f32r)
            midx = sb("midx", [P, RING, 1], i32)
            s_mg = [sem(f"messages_in{u}") for u in range(RING)]
            far = sb("far", [P, 2, P])
            s_fard, s_ix, s_mh, s_ml, s_us, s_ad = (sem(n) for n in (
                "dst_distances", "slots_staged", "messages_hi", "messages_lo", "messages_used", "sum_added"))

            with nc.Block() as block:
                def pairs(eng):
                    return eng.value_load(n_groups[0:1, 0:1], min_val=0, max_val=GROUPS)

                @block.sync
                def _(sp):
                    sp.dma_start(wg[:, :, :], Wgcn.rearrange("(k p) o -> p k o", p=P)).then_inc(s_wg, 16)

                @block.gpsimd
                def _(pool):
                    groups = pairs(pool)
                    with pool.Fori(0, GROUPS // 2) as i:
                        with pool.If(i * 2 < groups):
                            for u in range(RING):
                                t = i * RING + u
                                pool.wait_ge(s_ml, t + 1)
                                nc.gpsimd.tensor_copy(midx[:, u, :], slot_of[:, ds(t, 1)]).then_inc(s_ix, 1)
                                pool.wait_ge(s_ix, t + 1)
                                pool.sem_inc(s_go, 1)
                                pool.indirect_dma_start(mg[:, u, :], None, msg_dram,
                                                        bass.IndirectOffsetOnAxis(midx[:, u, :], 0)).then_inc(s_mg[u], 16)

                @block.scalar
                def _(act):
                    groups = pairs(act)
                    with act.Fori(0, GROUPS // 2) as i:
                        with act.If(i * 2 < groups):
                            for u in range(RING):
                                t = i * RING + u
                                act.wait_ge(s_us, t + 1)
                                if u % 2:
                                    nc.scalar.activation(far[:, u // 2 % 2, :], iota[:, :], ACT.Abs,
                                                         bias=etab[:, ds(t, 1), F_DLOC], scale=-1.0).then_inc(s_fard, 1)
                                act.wait_ge(s_mg[u], i * 16 + 16)
                                last = nc.scalar.activation(mhi[:, u % GT, :], mg[:, u, :], ACT.Identity, scale=weight[:, ds(t, 1)])
                                if u % 2:
                                    act.wait_ge(s_fard, i * GT + (u + 1) // 2)
                                    last = nc.scalar.activation(hotd[:, u % GT, :], far[:, u // 2 % 2, :], ACT.Relu,
                                                                bias=ones[:, 0:1], scale=-1.0)
                                last.then_inc(s_mh, 1)
                    act.wait_ge(s_wg, 16)
                    split_weights_high(act, wg, wghi, s_wgh)

                @block.vector
                def _(dve):
                    v = nc.vector

                    def add(n1, used, added, g):
                        at = dve.value_load(group_tile[0:1, ds(n1, 1)], min_val=0, max_val=NT - 1)
                        dve.wait_ge(s_us, used)
                        dve.wait_ge(s_ad, added)
                        a = acc[:, ds(at, 1), :].rearrange("p o c -> p (o c)")
                        v.tensor_tensor(a, a, banks(2 * g, DIM), ALU.add).then_inc(s_ad, 1)

                    groups = pairs(dve)
                    with dve.Fori(0, GROUPS // 2) as i:
                        with dve.If(i * 2 < groups):
                            for u in range(RING):
                                t = i * RING + u
                                if u % 2 == 0:
                                    dve.wait_ge(s_us, t + 1)
                                    v.tensor_scalar(hotd[:, u % GT, :], iota16[:, 0:P], etab[:, ds(t, 1), F_DLOC], None, ALU.is_equal)
                                dve.wait_ge(s_mh, t + 1)
                                v.scalar_tensor_tensor(mlo[:, u % GT, :], mg[:, u, :], weight[:, ds(t, 1)],
                                                       mhi[:, u % GT, :].bitcast(f32), ALU.mult, ALU.subtract).then_inc(s_ml, 1)
                                if u == GT - 1:
                                    with dve.If(i > 0):
                                        add(i * 2, i * RING + GT, i * 2 + 1, 1)
                            add(i * 2 + 1, i * RING + 2 * GT, i * 2 + 2, 0)
                    both = dve.snap((groups + 1) // 2)
                    add(both * 2, both * RING + GT, both * 2 + 1, 1)
                    split_weights_low(dve, wg, wghi, wglo, s_wgh, s_wgl)

                @block.tensor
                def _(pe):
                    pe.sem_inc(s_us, GT)
                    pe.sem_inc(s_ml, RING)
                    pe.sem_inc(s_ad, 2)
                    groups = pairs(pe)
                    with pe.Fori(0, GROUPS // 2) as i:
                        with pe.If(i * 2 < groups):
                            for g in range(2):
                                pe.wait_ge(s_ad, i * 2 + (g + 1))
                                for q in range(GT):
                                    pe.wait_ge(s_ml, i * RING + (g * GT + q + 1) + RING)
                                    for part in (mhi, mlo):
                                        for a, w in ((0, 512), (512, 256)):
                                            last = nc.tensor.matmul(banks(2 * g, DIM)[:, a:a + w], hotd[:, q, :], part[:, q, a:a + w],
                                                                    start=(q == 0 and part is mhi), stop=(q == GT - 1 and part is mlo))
                                    last.then_inc(s_us, 1)

        with ExitStack() as st:
            sb = holder(st)
            Yhi = sb("Yhi", [P, NT, DIM], f32r)
            Ylo = sb("Ylo", [P, NT, DIM], f32r)
            craw = region_h[:, NT * DIM:NT * DIM + 2 * NP].rearrange("p (u k d) -> p u k d", u=2, k=NT)
            ctv = ct_dram.rearrange("p (k d) -> p k d", k=NT)
            s_yh, s_self, s_ch, s_cl, s_fm, s_fo = (sem(n) for n in (
                "scaled_high", "self_edges", "counts_high", "counts_split", "sums_done", "rows_ready"))
            s_cr = [sem("counts_in0"), sem("counts_in1")]
            pj4 = SplitProjection("wgcn", KD, [512, 256])

            def load_counts(sp, j):
                sp.dma_start(craw[:, j % 2, :, :], ctv[:, :, j * P:(j + 1) * P]).then_inc(s_cr[j % 2], 16)

            with ExitStack() as st2:
                sb2 = holder(st2)
                cThi = sb2("cThi", [P, 2, KD, P], f32r)
                cTlo = sb2("cTlo", [P, 2, KD, P], f32r)
                bgrow = sb2("bgrow", [P, DIM])
                with nc.Block() as block:
                    @block.sync
                    def _(sp):
                        sp.dma_start(bgrow[:, :], vector_row(bgcn, DIM)).then_inc(s_biases, 16)
                        for j in range(2):
                            load_counts(sp, j)

                    @block.scalar
                    def _(act):
                        move_high(act, pj4, cThi, 0)
                        for j in range(NT):
                            if j + 1 < NT:
                                move_high(act, pj4, cThi, j + 1)
                            act.wait_ge(pj4.multiplied, j + 1)
                            nc.scalar.activation(Yhi[:, j, :], banks(2 + 3 * (j % 2), DIM), ACT.Identity,
                                                 scale=dinv[:, j:j + 1]).then_inc(s_yh, 1)

                    @block.vector
                    def _(dve):
                        v = nc.vector
                        dve.wait_ge(s_biases, 48)
                        move_low(dve, pj4, cThi, cTlo, 0)
                        for j in range(NT):
                            if j + 1 < NT:
                                move_low(dve, pj4, cThi, cTlo, j + 1)
                            v.tensor_tensor(x2[:, j, :], x2[:, j, :], bgrow[:, :], ALU.add)
                            dve.wait_ge(s_yh, j + 1)
                            v.scalar_tensor_tensor(Ylo[:, j, :], banks(2 + 3 * (j % 2), DIM), dinv[:, j:j + 1],
                                                   Yhi[:, j, :].bitcast(f32), ALU.mult, ALU.subtract).then_inc(pj4.taken, 1)

                    @block.tensor
                    def _(pe):
                        split_project_pe(pe, pj4, lambda j: acc[:, j, :], (s_wgl, lambda j: 1), cThi, cTlo, wghi, wglo)

            with ExitStack() as st2:
                sb2 = holder(st2)
                chi = sb2("chi", [P, 2, NT, P], f32r)
                clo = sb2("clo", [P, 2, NT, P], f32r)

                def store(sp, j):
                    n = P if j < NT - 1 else LAST
                    sp.wait_ge(s_fo, j + 1)
                    sp.dma_start(out[j * P:j * P + n, :], x2[:n, j, :]).then_inc(s_moved, 16)

                with nc.Block() as block:
                    @block.sync
                    def _(sp):
                        for j in range(2, NT):
                            sp.wait_ge(s_cl, j - 1)
                            load_counts(sp, j)
                            store(sp, j - 2)
                        for j in range(NT - 2, NT):
                            store(sp, j)
                        all_moved(sp, NT)

                    @block.scalar
                    def _(act):
                        for j in range(NT):
                            act.wait_ge(s_self, j + 1)
                            if j >= 2:
                                act.wait_ge(s_fm, j - 1)
                            nc.scalar.copy(chi[:, j % 2, :, :].rearrange("p k d -> p (k d)"),
                                           craw[:, j % 2, :, :].rearrange("p k d -> p (k d)")).then_inc(s_ch, 1)

                    @block.vector
                    def _(dve):
                        v = nc.vector

                        def split(j):
                            dve.wait_ge(s_cr[j % 2], 16 * (j // 2 + 1))
                            v.tensor_tensor(craw[:, j % 2, j, :], craw[:, j % 2, j, :], ident[:, :], ALU.add).then_inc(s_self, 1)
                            dve.wait_ge(s_ch, j + 1)
                            v.tensor_tensor(clo[:, j % 2, :, :].rearrange("p k d -> p (k d)"),
                                            craw[:, j % 2, :, :].rearrange("p k d -> p (k d)"),
                                            chi[:, j % 2, :, :].rearrange("p k d -> p (k d)").bitcast(f32), ALU.subtract).then_inc(s_cl, 1)

                        split(0)
                        for j in range(NT):
                            if j + 1 < NT:
                                split(j + 1)
                            dve.wait_ge(s_fm, j + 1)
                            v.scalar_tensor_tensor(x2[:, j, :], banks(2 * (j % 4), DIM), dinv[:, j:j + 1], x2[:, j, :],
                                                   ALU.mult, ALU.add).then_inc(s_fo, 1)

                    @block.tensor
                    def _(pe):
                        for j in range(NT):
                            pe.wait_ge(s_cl, j + 1)
                            if j >= 4:
                                pe.wait_ge(s_fo, j - 3)
                            for k in range(NT):
                                for n, (c, y) in enumerate(((chi, Yhi), (chi, Ylo), (clo, Yhi))):
                                    for a, w in ((0, 512), (512, 256)):
                                        last = nc.tensor.matmul(banks(2 * (j % 4), DIM)[:, a:a + w], c[:, j % 2, k, :],
                                                                y[:, k, a:a + w], start=(k == 0 and n == 0),
                                                                stop=(k == NT - 1 and n == 2))
                            last.then_inc(s_fm, 1)
        wgcn_life.close()


_INS = ['x', 'src', 'dst', 'edge_type_34', 'L0_gnn_W1', 'L0_gnn_att_src1', 'L0_gnn_att_dst1', 'L0_gnn_b1',
        'L0_gnn_W2', 'L0_gnn_att_src2', 'L0_gnn_att_dst2', 'L0_gnn_b2', 'L1_gnn_W_rel', 'L1_gnn_W_root',
        'L1_gnn_b_rgcn', 'L1_gnn_W_gcn', 'L1_gnn_b_gcn']


def kernel(**inputs):
    import numpy as _np
    import concourse.bacc as _bacc
    from concourse import mybir as _mybir
    from concourse.bass_utils import run_bass_kernel_spmd as _run

    nc = _bacc.Bacc("TRN2", target_bir_lowering=False, num_devices=1)
    arrays, args = {}, []
    for name in _INS:
        a = _np.ascontiguousarray(inputs[name])
        arrays[f"in_{name}_dram"] = a
        args.append(nc.dram_tensor(f"in_{name}_dram", a.shape, _mybir.dt.from_np(a.dtype), kind="ExternalInput").ap())
    args.append(nc.dram_tensor("out_0_dram", (NODES, DIM), _mybir.dt.float32, kind="ExternalOutput").ap())
    gnn_kernel(nc, *args)
    r = _run(nc, [arrays], core_ids=[0])
    return r.results[0]["out_0_dram"]
```
